# Optimizing a Trainium2 kernel written in Bass

```python
import numpy as np
import jax
import jax.numpy as jnp

def _softmax(x, axis=-1):
    return jax.nn.softmax(x, axis=axis)

def _gelu(x):
    return jax.nn.gelu(x, approximate=True)

def _silu(x):
    return jax.nn.silu(x)

def _sigmoid(x):
    return jax.nn.sigmoid(x)

def _layernorm(x, axis=-1, eps=1e-05):
    m = jnp.mean(x, axis=axis, keepdims=True)
    v = jnp.var(x, axis=axis, keepdims=True)
    return (x - m) / jnp.sqrt(v + eps)

def _scatter_add(tgt, idx, src, axis=0):
    return tgt.at[idx].add(src)

def _segment_sum(src, seg, n):
    return jax.ops.segment_sum(src, seg, n)
kernel_name = 'mk_flamingo_gated_d4_seqx_r8_d9258e'

def setup_inputs(seed: int=0):
    np.random.seed(seed)
    _w = jnp.asarray

    def _rec_inputs():
        import jax
        import jax.numpy as jnp
        _rk = jax.random.key(seed)
        x = -0.0002928 + 1 * jax.random.normal(jax.random.fold_in(_rk, 1), (16, 128, 128), jnp.float32)
        _lenS = 128 - jax.random.randint(jax.random.fold_in(_rk, 7), (16,), 0, max(1, 128 // 4) + 1, jnp.int32)
        _lenS2 = 128 - jax.random.randint(jax.random.fold_in(_rk, 8), (16,), 0, max(1, 128 // 4) + 1, jnp.int32)
        _ctx_1024P = jax.random.normal(jax.random.fold_in(_rk, 11), (16, 16, 128), jnp.float32)
        _ctx_1024c = jax.random.dirichlet(jax.random.fold_in(_rk, 511), 0.3 * jnp.ones((16,), jnp.float32), (16, 128))
        _ctx_1024t = jnp.einsum('bsk,bkd->bsd', _ctx_1024c, _ctx_1024P)
        _ctx_1024t = _ctx_1024t * jax.lax.rsqrt(jnp.mean(jnp.square(_ctx_1024t)) + 1e-12) * 0.953939
        ctx_1024 = -1.39393e-06 + 0.999914 * (_ctx_1024t + 0.3 * jax.random.normal(jax.random.fold_in(_rk, 611), (16, 128, 128), jnp.float32))
        _g = jax.random.normal(jax.random.fold_in(_rk, 9001), (2, 4), jnp.float32)
        _g = jnp.sign(_g) * jnp.maximum(jnp.abs(_g), 1.0) + (_g == 0) * 1.0
        g_xattn = _g[0]
        g_ffn = _g[1]
        return (x, ctx_1024, g_xattn, g_ffn)
    x, ctx_1024, g_xattn, g_ffn = _rec_inputs()

    def _L0_xattn_setup():
        import jax, jax.numpy as jnp
        import numpy as np
        B, T, N_EMBD, N_HEAD = (2, 256, 128, 16)
        HEAD = N_EMBD // N_HEAD
        WINDOW = 64
        key = jax.random.key(seed)
        kq, kk, kv, kw = jax.random.split(key, 4)
        q = jax.random.normal(kq, (B, T, N_EMBD), dtype=jnp.float32)
        k = jax.random.normal(kk, (B, T, N_EMBD), dtype=jnp.float32)
        v = jax.random.normal(kv, (B, T, N_EMBD), dtype=jnp.float32)
        W_proj = jax.random.normal(kw, (N_EMBD, N_EMBD), dtype=jnp.float32) * (1.0 / np.sqrt(N_EMBD))
        b_proj = jnp.zeros((N_EMBD,), dtype=jnp.float32)
        return {'q': q, 'k': k, 'v': v, 'W_proj': W_proj, 'b_proj': b_proj}
    _L0_xattn_all = _L0_xattn_setup()
    _L0_xattn_in = {k: v for k, v in _L0_xattn_all.items() if k in ('W_proj', 'b_proj')}
    del _L0_xattn_all

    def _L0_ffn_setup():
        import jax, jax.numpy as jnp
        import numpy as np
        E = 8
        TOP_K = 2
        D = 128
        H = 2 * D
        key = jax.random.key(seed)
        k0, k1, k2, k3, k4 = jax.random.split(key, 5)
        scale = 0.02
        x = jax.random.normal(k0, (4, 256, D), dtype=jnp.float32)
        Wg = jax.random.normal(k1, (D, E), dtype=jnp.float32) * scale
        W1 = jax.random.normal(k2, (E, D, H), dtype=jnp.float32) * scale
        W2 = jax.random.normal(k3, (E, D, H), dtype=jnp.float32) * scale
        W3 = jax.random.normal(k4, (E, H, D), dtype=jnp.float32) * scale
        return {'x': x, 'Wg': Wg, 'W1': W1, 'W2': W2, 'W3': W3}
    _L0_ffn_all = _L0_ffn_setup()
    _L0_ffn_in = {k: v for k, v in _L0_ffn_all.items() if k in ('Wg', 'W1', 'W2', 'W3')}
    del _L0_ffn_all

    def _L1_xattn_setup():
        import jax, jax.numpy as jnp
        import numpy as np
        DIM = 128
        HEAD_DIM = 64
        NUM_HEADS = 8
        INNER = HEAD_DIM * NUM_HEADS
        ROT_DIM = HEAD_DIM
        ROPE_BASE = 10000.0
        EPS = 1e-05

        def layer_norm(x, g, b):
            mu = jnp.mean(x, axis=-1, keepdims=True)
            var = jnp.var(x, axis=-1, keepdims=True)
            return (x - mu) * jax.lax.rsqrt(var + EPS) * g + b

        def rope_rotate_k(k):
            n = k.shape[1]
            half = ROT_DIM // 2
            inv_freq = 1.0 / ROPE_BASE ** (jnp.arange(0, ROT_DIM, 2, dtype=jnp.float32) / ROT_DIM)
            theta = jnp.arange(n, dtype=jnp.float32)[:, None] * inv_freq[None, :]
            angles = jnp.concatenate([theta, theta], axis=-1)
            cos = jnp.cos(angles)[None, :, None, :].astype(k.dtype)
            sin = jnp.sin(angles)[None, :, None, :].astype(k.dtype)
            k_rope, k_pass = (k[..., :ROT_DIM], k[..., ROT_DIM:])
            neg_half = jnp.concatenate([-k_rope[..., half:], k_rope[..., :half]], axis=-1)
            k_rope = k_rope * cos + neg_half * sin
            return jnp.concatenate([k_rope, k_pass], axis=-1)
        key = jax.random.key(seed)
        ks = jax.random.split(key, 5)
        b, n, m = (8, 1024, 64)
        s = 1.0 / np.sqrt(DIM)
        return {'x': jax.random.normal(ks[0], (b, n, DIM), jnp.float32), 'latents': jax.random.normal(ks[1], (b, m, DIM), jnp.float32), 'gamma_x': jnp.ones((DIM,), jnp.float32), 'beta_x': jnp.zeros((DIM,), jnp.float32), 'gamma_l': jnp.ones((DIM,), jnp.float32), 'beta_l': jnp.zeros((DIM,), jnp.float32), 'Wq': jax.random.normal(ks[2], (DIM, INNER), jnp.float32) * s, 'Wkv': jax.random.normal(ks[3], (DIM, 2 * INNER), jnp.float32) * s, 'Wo': jax.random.normal(ks[4], (INNER, DIM), jnp.float32) * (1.0 / np.sqrt(INNER))}
    _L1_xattn_all = _L1_xattn_setup()
    _L1_xattn_in = {k: v for k, v in _L1_xattn_all.items() if k in ('gamma_x', 'beta_x', 'gamma_l', 'beta_l', 'Wq', 'Wkv', 'Wo')}
    del _L1_xattn_all

    def _L1_ffn_setup():
        import jax, jax.numpy as jnp
        import numpy as np
        DIM = 128
        EXPERT_DIM = 64
        N_EXPERTS = 16
        TOPK = 2
        SHARED_HIDDEN = EXPERT_DIM * TOPK
        B, T = (4, 128)

        def _moe_forward(x, router_w, router_bias, up_proj, gate_proj, down_proj, sh_gate, sh_up, sh_down):
            Bb, Tt, D = x.shape
            flat = x.reshape(Bb * Tt, D)
            N = flat.shape[0]
            logits = flat @ router_w.T
            topk_scores, topk_idx = jax.lax.top_k(logits + router_bias, TOPK)
            topk_scores = jax.nn.softmax(topk_scores, axis=-1)
            combine = jnp.zeros((N, N_EXPERTS), flat.dtype)
            combine = combine.at[jnp.arange(N)[:, None], topk_idx].add(topk_scores)
            up_all = jnp.einsum('nd,kde->nke', flat, up_proj)
            gate_all = jnp.einsum('nd,kde->nke', flat, gate_proj)
            hidden = jax.nn.silu(gate_all) * up_all
            down_all = jnp.einsum('nke,ked->nkd', hidden, down_proj)
            out = jnp.einsum('nk,nkd->nd', combine, down_all)
            sh_hidden = jax.nn.silu(flat @ sh_gate.T) * (flat @ sh_up.T)
            out = out + sh_hidden @ sh_down.T
            return out.reshape(Bb, Tt, D)
        key = jax.random.key(seed)
        ks = jax.random.split(key, 9)
        std = 0.02
        return {'x': jax.random.normal(ks[0], (B, T, DIM), jnp.float32), 'router_w': jax.random.normal(ks[1], (N_EXPERTS, DIM), jnp.float32) * std, 'router_bias': jnp.zeros((N_EXPERTS,), jnp.float32), 'up_proj': jax.random.normal(ks[2], (N_EXPERTS, DIM, EXPERT_DIM), jnp.float32) * std, 'gate_proj': jax.random.normal(ks[3], (N_EXPERTS, DIM, EXPERT_DIM), jnp.float32) * std, 'down_proj': jax.random.normal(ks[4], (N_EXPERTS, EXPERT_DIM, DIM), jnp.float32) * std, 'sh_gate': jax.random.normal(ks[5], (SHARED_HIDDEN, DIM), jnp.float32) * std, 'sh_up': jax.random.normal(ks[6], (SHARED_HIDDEN, DIM), jnp.float32) * std, 'sh_down': jax.random.normal(ks[7], (DIM, SHARED_HIDDEN), jnp.float32) * std}
    _L1_ffn_all = _L1_ffn_setup()
    _L1_ffn_in = {k: v for k, v in _L1_ffn_all.items() if k in ('router_w', 'router_bias', 'up_proj', 'gate_proj', 'down_proj', 'sh_gate', 'sh_up', 'sh_down')}
    del _L1_ffn_all

    def _L2_xattn_setup():
        import jax, jax.numpy as jnp
        import numpy as np
        import math
        B, S, D, H = (4, 256, 128, 16)
        DH = D // H

        def _split_heads(x):
            b, s, _ = x.shape
            return x.reshape(b, s, H, DH).transpose(0, 2, 1, 3)
        key = jax.random.key(seed)
        ks = jax.random.split(key, 12)
        sc = 1.0 / math.sqrt(D)
        return {'x_q': jax.random.normal(ks[0], (B, S, D), jnp.float32), 'x_kv': jax.random.normal(ks[1], (B, S, D), jnp.float32), 'W_q': jax.random.normal(ks[2], (D, D), jnp.float32) * sc, 'b_q': jnp.zeros((D,), jnp.float32), 'W_k': jax.random.normal(ks[3], (D, D), jnp.float32) * sc, 'b_k': jnp.zeros((D,), jnp.float32), 'W_v': jax.random.normal(ks[4], (D, D), jnp.float32) * sc, 'b_v': jnp.zeros((D,), jnp.float32), 'W_out': jax.random.normal(ks[5], (D, D), jnp.float32) * sc, 'b_out': jnp.zeros((D,), jnp.float32)}
    _L2_xattn_all = _L2_xattn_setup()
    _L2_xattn_in = {k: v for k, v in _L2_xattn_all.items() if k in ('W_q', 'b_q', 'W_k', 'b_k', 'W_v', 'b_v', 'W_out', 'b_out')}
    del _L2_xattn_all

    def _L2_ffn_setup():
        import jax, jax.numpy as jnp
        import numpy as np
        DIM = 128

        def _reference_tuple_inner(x, W_r, W_k, W_v, mu_r, mu_k):
            B, T, C = x.shape
            x_prev = jnp.concatenate([jnp.zeros((B, 1, C), x.dtype), x[:, :-1, :]], axis=1)
            xr = mu_r * x + (1.0 - mu_r) * x_prev
            xk = mu_k * x + (1.0 - mu_k) * x_prev
            r = jax.nn.sigmoid(jnp.einsum('btc,dc->btd', xr, W_r))
            k = jnp.einsum('btc,dc->btd', xk, W_k)
            k_act = jnp.square(jax.nn.relu(k))
            out = r * jnp.einsum('btc,dc->btd', k_act, W_v)
            new_state = x[:, -1, :]
            return (out, new_state)
        key = jax.random.key(seed)
        ks = jax.random.split(key, 6)
        B, T, C = (8, 256, DIM)
        x = jax.random.normal(ks[0], (B, T, C), dtype=jnp.float32)
        s = 1.0 / np.sqrt(C)
        W_r = jax.random.uniform(ks[1], (C, C), jnp.float32, -s, s)
        W_k = jax.random.uniform(ks[2], (C, C), jnp.float32, -s, s)
        W_v = jax.random.uniform(ks[3], (C, C), jnp.float32, -s, s)
        mu_r = jax.random.uniform(ks[4], (C,), jnp.float32)
        mu_k = jax.random.uniform(ks[5], (C,), jnp.float32)
        return {'x': x, 'W_r': W_r, 'W_k': W_k, 'W_v': W_v, 'mu_r': mu_r, 'mu_k': mu_k}
    _L2_ffn_all = _L2_ffn_setup()
    _L2_ffn_in = {k: v for k, v in _L2_ffn_all.items() if k in ('W_r', 'W_k', 'W_v', 'mu_r', 'mu_k')}
    del _L2_ffn_all

    def _L3_xattn_setup():
        import jax, jax.numpy as jnp
        import numpy as np
        import math
        B, L, D, H = (8, 256, 128, 16)
        E = D // H
        FACTOR = 1
        TOP_K = int(FACTOR * math.log(L))
        key = jax.random.key(seed)
        ks = jax.random.split(key, 11)
        s = 1.0 / math.sqrt(D)
        f32 = jnp.float32
        return {'queries': jax.random.normal(ks[0], (B, L, D), f32), 'keys': jax.random.normal(ks[1], (B, L, D), f32), 'values': jax.random.normal(ks[2], (B, L, D), f32), 'Wq': jax.random.normal(ks[3], (D, D), f32) * s, 'bq': jax.random.normal(ks[4], (D,), f32) * 0.01, 'Wk': jax.random.normal(ks[5], (D, D), f32) * s, 'bk': jax.random.normal(ks[6], (D,), f32) * 0.01, 'Wv': jax.random.normal(ks[7], (D, D), f32) * s, 'bv': jax.random.normal(ks[8], (D,), f32) * 0.01, 'Wo': jax.random.normal(ks[9], (D, D), f32) * s, 'bo': jax.random.normal(ks[10], (D,), f32) * 0.01}
    _L3_xattn_all = _L3_xattn_setup()
    _L3_xattn_in = {k: v for k, v in _L3_xattn_all.items() if k in ('Wq', 'bq', 'Wk', 'bk', 'Wv', 'bv', 'Wo', 'bo')}
    del _L3_xattn_all

    def _L3_ffn_setup():
        import jax, jax.numpy as jnp
        import numpy as np
        B, S, H, M, E, K = (4, 256, 128, 512, 8, 2)
        key = jax.random.key(seed)
        ks = jax.random.split(key, 6)
        x = jax.random.normal(ks[0], (B, S, H), dtype=jnp.float32)
        Wr = jax.random.normal(ks[1], (E, H), dtype=jnp.float32) * (1.0 / np.sqrt(H))
        W1 = jax.random.normal(ks[2], (E, M, H), dtype=jnp.float32) * np.sqrt(2.0 / (H + M))
        b1 = jax.random.normal(ks[3], (E, M), dtype=jnp.float32) * 1e-06
        W2 = jax.random.normal(ks[4], (E, H, M), dtype=jnp.float32) * np.sqrt(2.0 / (H + M))
        b2 = jax.random.normal(ks[5], (E, H), dtype=jnp.float32) * 1e-06
        return {'x': x, 'Wr': Wr, 'W1': W1, 'b1': b1, 'W2': W2, 'b2': b2}
    _L3_ffn_all = _L3_ffn_setup()
    _L3_ffn_in = {k: v for k, v in _L3_ffn_all.items() if k in ('Wr', 'W1', 'b1', 'W2', 'b2')}
    del _L3_ffn_all
    return {'x': x, 'ctx_1024': ctx_1024, 'g_xattn': g_xattn, 'g_ffn': g_ffn, 'L0_xattn_W_proj': _L0_xattn_in['W_proj'], 'L0_xattn_b_proj': _L0_xattn_in['b_proj'], 'L0_ffn_Wg': _L0_ffn_in['Wg'], 'L0_ffn_W1': _L0_ffn_in['W1'], 'L0_ffn_W2': _L0_ffn_in['W2'], 'L0_ffn_W3': _L0_ffn_in['W3'], 'L1_xattn_gamma_x': _L1_xattn_in['gamma_x'], 'L1_xattn_beta_x': _L1_xattn_in['beta_x'], 'L1_xattn_gamma_l': _L1_xattn_in['gamma_l'], 'L1_xattn_beta_l': _L1_xattn_in['beta_l'], 'L1_xattn_Wq': _L1_xattn_in['Wq'], 'L1_xattn_Wkv': _L1_xattn_in['Wkv'], 'L1_xattn_Wo': _L1_xattn_in['Wo'], 'L1_ffn_router_w': _L1_ffn_in['router_w'], 'L1_ffn_router_bias': _L1_ffn_in['router_bias'], 'L1_ffn_up_proj': _L1_ffn_in['up_proj'], 'L1_ffn_gate_proj': _L1_ffn_in['gate_proj'], 'L1_ffn_down_proj': _L1_ffn_in['down_proj'], 'L1_ffn_sh_gate': _L1_ffn_in['sh_gate'], 'L1_ffn_sh_up': _L1_ffn_in['sh_up'], 'L1_ffn_sh_down': _L1_ffn_in['sh_down'], 'L2_xattn_W_q': _L2_xattn_in['W_q'], 'L2_xattn_b_q': _L2_xattn_in['b_q'], 'L2_xattn_W_k': _L2_xattn_in['W_k'], 'L2_xattn_b_k': _L2_xattn_in['b_k'], 'L2_xattn_W_v': _L2_xattn_in['W_v'], 'L2_xattn_b_v': _L2_xattn_in['b_v'], 'L2_xattn_W_out': _L2_xattn_in['W_out'], 'L2_xattn_b_out': _L2_xattn_in['b_out'], 'L2_ffn_W_r': _L2_ffn_in['W_r'], 'L2_ffn_W_k': _L2_ffn_in['W_k'], 'L2_ffn_W_v': _L2_ffn_in['W_v'], 'L2_ffn_mu_r': _L2_ffn_in['mu_r'], 'L2_ffn_mu_k': _L2_ffn_in['mu_k'], 'L3_xattn_Wq': _L3_xattn_in['Wq'], 'L3_xattn_bq': _L3_xattn_in['bq'], 'L3_xattn_Wk': _L3_xattn_in['Wk'], 'L3_xattn_bk': _L3_xattn_in['bk'], 'L3_xattn_Wv': _L3_xattn_in['Wv'], 'L3_xattn_bv': _L3_xattn_in['bv'], 'L3_xattn_Wo': _L3_xattn_in['Wo'], 'L3_xattn_bo': _L3_xattn_in['bo'], 'L3_ffn_Wr': _L3_ffn_in['Wr'], 'L3_ffn_W1': _L3_ffn_in['W1'], 'L3_ffn_b1': _L3_ffn_in['b1'], 'L3_ffn_W2': _L3_ffn_in['W2'], 'L3_ffn_b2': _L3_ffn_in['b2']}

def reference(x, ctx_1024, g_xattn, g_ffn, L0_xattn_W_proj, L0_xattn_b_proj, L0_ffn_Wg, L0_ffn_W1, L0_ffn_W2, L0_ffn_W3, L1_xattn_gamma_x, L1_xattn_beta_x, L1_xattn_gamma_l, L1_xattn_beta_l, L1_xattn_Wq, L1_xattn_Wkv, L1_xattn_Wo, L1_ffn_router_w, L1_ffn_router_bias, L1_ffn_up_proj, L1_ffn_gate_proj, L1_ffn_down_proj, L1_ffn_sh_gate, L1_ffn_sh_up, L1_ffn_sh_down, L2_xattn_W_q, L2_xattn_b_q, L2_xattn_W_k, L2_xattn_b_k, L2_xattn_W_v, L2_xattn_b_v, L2_xattn_W_out, L2_xattn_b_out, L2_ffn_W_r, L2_ffn_W_k, L2_ffn_W_v, L2_ffn_mu_r, L2_ffn_mu_k, L3_xattn_Wq, L3_xattn_bq, L3_xattn_Wk, L3_xattn_bk, L3_xattn_Wv, L3_xattn_bv, L3_xattn_Wo, L3_xattn_bo, L3_ffn_Wr, L3_ffn_W1, L3_ffn_b1, L3_ffn_W2, L3_ffn_b2):
    import jax
    import jax.numpy as jnp

    def _L0_xattn_ref(q, k, v, W_proj, b_proj):
        import jax, jax.numpy as jnp
        import numpy as np
        B, T, N_EMBD, N_HEAD = (2, 256, 128, 16)
        HEAD = N_EMBD // N_HEAD
        WINDOW = 64
        Bsz, Tlen, _ = q.shape
        qh = q.reshape(Bsz, Tlen, N_HEAD, HEAD).transpose(0, 2, 1, 3)
        kh = k.reshape(Bsz, Tlen, N_HEAD, HEAD).transpose(0, 2, 1, 3)
        vh = v.reshape(Bsz, Tlen, N_HEAD, HEAD).transpose(0, 2, 1, 3)
        scale = 1.0 / np.sqrt(HEAD)
        scores = jnp.einsum('bhqd,bhkd->bhqk', qh, kh) * scale
        idx = jnp.arange(Tlen)
        dist = jnp.abs(idx[None, :] - idx[:, None])
        scores = jnp.where(dist[None, None] > WINDOW, -jnp.inf, scores)
        attn = jax.nn.softmax(scores, axis=-1)
        y = jnp.einsum('bhqk,bhkd->bhqd', attn, vh)
        y = y.transpose(0, 2, 1, 3).reshape(Bsz, Tlen, N_EMBD)
        return y @ W_proj.T + b_proj

    def _L0_ffn_ref(x, Wg, W1, W2, W3):
        import jax, jax.numpy as jnp
        import numpy as np
        E = 8
        TOP_K = 2
        D = 128
        H = 2 * D
        logits = jnp.einsum('bsd,de->bse', x, Wg)
        top_vals, top_idx = jax.lax.top_k(logits, TOP_K)
        probs = jax.nn.softmax(top_vals, axis=-1)
        onehot = jax.nn.one_hot(top_idx, E, dtype=x.dtype)
        weights = jnp.einsum('bsk,bske->bse', probs, onehot)
        out = jnp.zeros_like(x)
        for e in range(E):
            u = jnp.einsum('bsd,dh->bsh', x, W1[e])
            v = jnp.einsum('bsd,dh->bsh', x, W2[e])
            h = u * jax.nn.sigmoid(u) * v
            y = jnp.einsum('bsh,hd->bsd', h, W3[e])
            out = out + y * weights[..., e][..., None]
        return out

    def _L1_xattn_ref(x, latents, gamma_x, beta_x, gamma_l, beta_l, Wq, Wkv, Wo):
        import jax, jax.numpy as jnp
        import numpy as np
        DIM = 128
        HEAD_DIM = 64
        NUM_HEADS = 8
        INNER = HEAD_DIM * NUM_HEADS
        ROT_DIM = HEAD_DIM
        ROPE_BASE = 10000.0
        EPS = 1e-05

        def layer_norm(x, g, b):
            mu = jnp.mean(x, axis=-1, keepdims=True)
            var = jnp.var(x, axis=-1, keepdims=True)
            return (x - mu) * jax.lax.rsqrt(var + EPS) * g + b

        def rope_rotate_k(k):
            n = k.shape[1]
            half = ROT_DIM // 2
            inv_freq = 1.0 / ROPE_BASE ** (jnp.arange(0, ROT_DIM, 2, dtype=jnp.float32) / ROT_DIM)
            theta = jnp.arange(n, dtype=jnp.float32)[:, None] * inv_freq[None, :]
            angles = jnp.concatenate([theta, theta], axis=-1)
            cos = jnp.cos(angles)[None, :, None, :].astype(k.dtype)
            sin = jnp.sin(angles)[None, :, None, :].astype(k.dtype)
            k_rope, k_pass = (k[..., :ROT_DIM], k[..., ROT_DIM:])
            neg_half = jnp.concatenate([-k_rope[..., half:], k_rope[..., :half]], axis=-1)
            k_rope = k_rope * cos + neg_half * sin
            return jnp.concatenate([k_rope, k_pass], axis=-1)
        b, n, _ = x.shape
        m = latents.shape[1]
        h, d = (NUM_HEADS, HEAD_DIM)
        scale = d ** (-0.5)
        xn = layer_norm(x, gamma_x, beta_x)
        ln = layer_norm(latents, gamma_l, beta_l)
        q = (ln @ Wq).reshape(b, m, h, d)
        kv_x = xn @ Wkv
        k_x, v_x = (kv_x[..., :INNER], kv_x[..., INNER:])
        kv_l = ln @ Wkv
        k_l, v_l = (kv_l[..., :INNER], kv_l[..., INNER:])
        k_x = k_x.reshape(b, n, h, d)
        v_x = v_x.reshape(b, n, h, d)
        k_x = rope_rotate_k(k_x)
        q = jnp.transpose(q, (0, 2, 1, 3)) * scale
        k_x = jnp.transpose(k_x, (0, 2, 1, 3))
        v_x = jnp.transpose(v_x, (0, 2, 1, 3))
        k_l = jnp.transpose(k_l.reshape(b, m, h, d), (0, 2, 1, 3))
        v_l = jnp.transpose(v_l.reshape(b, m, h, d), (0, 2, 1, 3))
        k = jnp.concatenate([k_x, k_l], axis=2)
        v = jnp.concatenate([v_x, v_l], axis=2)
        sim = jnp.einsum('bhid,bhjd->bhij', q, k)
        attn = jax.nn.softmax(sim, axis=-1)
        out = jnp.einsum('bhij,bhjd->bhid', attn, v)
        out = jnp.transpose(out, (0, 2, 1, 3)).reshape(b, m, INNER)
        return out @ Wo

    def _L1_ffn_ref(x, router_w, router_bias, up_proj, gate_proj, down_proj, sh_gate, sh_up, sh_down):
        import jax, jax.numpy as jnp
        import numpy as np
        DIM = 128
        EXPERT_DIM = 64
        N_EXPERTS = 16
        TOPK = 2
        SHARED_HIDDEN = EXPERT_DIM * TOPK
        B, T = (4, 128)

        def _moe_forward(x, router_w, router_bias, up_proj, gate_proj, down_proj, sh_gate, sh_up, sh_down):
            Bb, Tt, D = x.shape
            flat = x.reshape(Bb * Tt, D)
            N = flat.shape[0]
            logits = flat @ router_w.T
            topk_scores, topk_idx = jax.lax.top_k(logits + router_bias, TOPK)
            topk_scores = jax.nn.softmax(topk_scores, axis=-1)
            combine = jnp.zeros((N, N_EXPERTS), flat.dtype)
            combine = combine.at[jnp.arange(N)[:, None], topk_idx].add(topk_scores)
            up_all = jnp.einsum('nd,kde->nke', flat, up_proj)
            gate_all = jnp.einsum('nd,kde->nke', flat, gate_proj)
            hidden = jax.nn.silu(gate_all) * up_all
            down_all = jnp.einsum('nke,ked->nkd', hidden, down_proj)
            out = jnp.einsum('nk,nkd->nd', combine, down_all)
            sh_hidden = jax.nn.silu(flat @ sh_gate.T) * (flat @ sh_up.T)
            out = out + sh_hidden @ sh_down.T
            return out.reshape(Bb, Tt, D)
        return _moe_forward(x, router_w, router_bias, up_proj, gate_proj, down_proj, sh_gate, sh_up, sh_down)

    def _L2_xattn_ref(x_q, x_kv, W_q, b_q, W_k, b_k, W_v, b_v, W_out, b_out):
        import jax, jax.numpy as jnp
        import numpy as np
        import math
        B, S, D, H = (4, 256, 128, 16)
        DH = D // H

        def _split_heads(x):
            b, s, _ = x.shape
            return x.reshape(b, s, H, DH).transpose(0, 2, 1, 3)
        q = x_q @ W_q.T + b_q
        k = x_kv @ W_k.T + b_k
        v = x_kv @ W_v.T + b_v
        qh, kh, vh = (_split_heads(q), _split_heads(k), _split_heads(v))
        scale = 1.0 / math.sqrt(DH)
        scores = jnp.einsum('bhqd,bhkd->bhqk', qh, kh) * scale
        attn = jax.nn.softmax(scores, axis=-1)
        ctx = jnp.einsum('bhqk,bhkd->bhqd', attn, vh)
        ctx = ctx.transpose(0, 2, 1, 3).reshape(x_q.shape[0], x_q.shape[1], D)
        return ctx @ W_out.T + b_out

    def _L2_ffn_ref(x, W_r, W_k, W_v, mu_r, mu_k):
        import jax, jax.numpy as jnp
        import numpy as np
        DIM = 128

        def _reference_tuple_inner(x, W_r, W_k, W_v, mu_r, mu_k):
            B, T, C = x.shape
            x_prev = jnp.concatenate([jnp.zeros((B, 1, C), x.dtype), x[:, :-1, :]], axis=1)
            xr = mu_r * x + (1.0 - mu_r) * x_prev
            xk = mu_k * x + (1.0 - mu_k) * x_prev
            r = jax.nn.sigmoid(jnp.einsum('btc,dc->btd', xr, W_r))
            k = jnp.einsum('btc,dc->btd', xk, W_k)
            k_act = jnp.square(jax.nn.relu(k))
            out = r * jnp.einsum('btc,dc->btd', k_act, W_v)
            new_state = x[:, -1, :]
            return (out, new_state)
        return _reference_tuple_inner(x, W_r, W_k, W_v, mu_r, mu_k)[0]

    def _L3_xattn_ref(queries, keys, values, Wq, bq, Wk, bk, Wv, bv, Wo, bo):
        import jax, jax.numpy as jnp
        import numpy as np
        import math
        B, L, D, H = (8, 256, 128, 16)
        E = D // H
        FACTOR = 1
        TOP_K = int(FACTOR * math.log(L))
        Bq, Lq, Dq = queries.shape
        q = (queries @ Wq + bq).reshape(Bq, Lq, H, E).transpose(0, 2, 3, 1)
        k = (keys @ Wk + bk).reshape(Bq, Lq, H, E).transpose(0, 2, 3, 1)
        v = (values @ Wv + bv).reshape(Bq, Lq, H, E).transpose(0, 2, 3, 1)
        q_fft = jnp.fft.rfft(q, axis=-1)
        k_fft = jnp.fft.rfft(k, axis=-1)
        corr = jnp.fft.irfft(q_fft * jnp.conj(k_fft), n=Lq, axis=-1)
        mean_value = corr.mean(axis=(1, 2))
        _, index = jax.lax.top_k(mean_value.mean(axis=0), TOP_K)
        weights = mean_value[:, index]
        tmp_corr = jax.nn.softmax(weights, axis=-1)
        idx = (jnp.arange(Lq)[None, :] + index[:, None]) % Lq
        gathered = v[..., idx]
        agg = jnp.einsum('bhekl,bk->bhel', gathered, tmp_corr)
        out = agg.transpose(0, 3, 1, 2).reshape(Bq, Lq, Dq)
        return out @ Wo + bo

    def _L3_ffn_ref(x, Wr, W1, b1, W2, b2):
        import jax, jax.numpy as jnp
        import numpy as np
        B, S, H, M, E, K = (4, 256, 128, 512, 8, 2)
        logits = jnp.einsum('bsh,eh->bse', x, Wr)
        probs = jax.nn.softmax(logits, axis=-1)
        top_v, top_i = jax.lax.top_k(probs, K)
        top_v = top_v / jnp.sum(top_v, axis=-1, keepdims=True)
        out = jnp.zeros_like(x)
        for e in range(E):
            w_e = jnp.sum(jnp.where(top_i == e, top_v, 0.0), axis=-1)
            h = jnp.einsum('bsh,mh->bsm', x, W1[e]) + b1[e]
            h = jax.nn.gelu(h, approximate=False)
            y = jnp.einsum('bsm,hm->bsh', h, W2[e]) + b2[e]
            out = out + y * w_e[..., None]
        return out
    x = x + jnp.tanh(g_xattn[0]) * _L0_xattn_ref(_layernorm(x, axis=-1), ctx_1024, ctx_1024, L0_xattn_W_proj, L0_xattn_b_proj)
    x = x + jnp.tanh(g_ffn[0]) * _L0_ffn_ref(_layernorm(x, axis=-1), L0_ffn_Wg, L0_ffn_W1, L0_ffn_W2, L0_ffn_W3)
    x = x + jnp.tanh(g_xattn[1]) * _L1_xattn_ref(ctx_1024, _layernorm(x, axis=-1), L1_xattn_gamma_x, L1_xattn_beta_x, L1_xattn_gamma_l, L1_xattn_beta_l, L1_xattn_Wq, L1_xattn_Wkv, L1_xattn_Wo)
    x = x + jnp.tanh(g_ffn[1]) * _L1_ffn_ref(_layernorm(x, axis=-1), L1_ffn_router_w, L1_ffn_router_bias, L1_ffn_up_proj, L1_ffn_gate_proj, L1_ffn_down_proj, L1_ffn_sh_gate, L1_ffn_sh_up, L1_ffn_sh_down)
    x = x + jnp.tanh(g_xattn[2]) * _L2_xattn_ref(_layernorm(x, axis=-1), ctx_1024, L2_xattn_W_q, L2_xattn_b_q, L2_xattn_W_k, L2_xattn_b_k, L2_xattn_W_v, L2_xattn_b_v, L2_xattn_W_out, L2_xattn_b_out)
    x = x + jnp.tanh(g_ffn[2]) * _L2_ffn_ref(_layernorm(x, axis=-1), L2_ffn_W_r, L2_ffn_W_k, L2_ffn_W_v, L2_ffn_mu_r, L2_ffn_mu_k)
    x = x + jnp.tanh(g_xattn[3]) * _L3_xattn_ref(_layernorm(x, axis=-1), ctx_1024, ctx_1024, L3_xattn_Wq, L3_xattn_bq, L3_xattn_Wk, L3_xattn_bk, L3_xattn_Wv, L3_xattn_bv, L3_xattn_Wo, L3_xattn_bo)
    x = x + jnp.tanh(g_ffn[3]) * _L3_ffn_ref(_layernorm(x, axis=-1), L3_ffn_Wr, L3_ffn_W1, L3_ffn_b1, L3_ffn_W2, L3_ffn_b2)
    return x

_drawn_inputs = setup_inputs


def setup_inputs(seed=0):
    import zlib

    import numpy as np

    out = dict(_drawn_inputs(seed))
    spreads = {'L0_xattn_b_proj': (0.0, 0.1),
     'L1_xattn_gamma_x': (1.0, 0.2),
     'L1_xattn_beta_x': (0.0, 0.1),
     'L1_xattn_gamma_l': (1.0, 0.2),
     'L1_xattn_beta_l': (0.0, 0.1),
     'L1_ffn_router_bias': (0.0, 0.8),
     'L2_xattn_b_q': (0.0, 0.432),
     'L2_xattn_b_k': (0.0, 2.0),
     'L2_xattn_b_v': (0.0, 0.1),
     'L2_xattn_b_out': (0.0, 0.1)}
    factors = {'g_ffn': 44.976,
     'L0_ffn_Wg': 5.181,
     'L0_ffn_W1': 6.08,
     'L0_ffn_W3': 5.554,
     'L1_ffn_router_w': 8.0,
     'L1_ffn_up_proj': 8.0,
     'L1_ffn_gate_proj': 7.402,
     'L1_ffn_sh_gate': 4.732,
     'L1_ffn_sh_up': 5.046,
     'L1_ffn_sh_down': 4.948,
     'L2_ffn_mu_r': 4.812,
     'L3_xattn_bq': 64.0,
     'L3_xattn_bk': 64.0,
     'L3_xattn_bv': 4.055,
     'L3_xattn_bo': 4.423,
     'L3_ffn_b1': 64.0,
     'L3_ffn_b2': 64.0}
    for name, (base, spread) in spreads.items():
        noise = np.random.default_rng([zlib.crc32(name.encode()), seed]).standard_normal(out[name].shape)
        drawn = base * np.exp(spread * noise) if base else spread * noise
        out[name] = jnp.asarray(drawn.astype(out[name].dtype))
    for name, factor in factors.items():
        out[name] = (out[name] * factor).astype(out[name].dtype)
    return out
```

```python
import concourse.bass as bass
from concourse import mybir
from contextlib import ExitStack
import numpy as np

FP32 = mybir.dt.float32
BF16 = mybir.dt.bfloat16
ALU = mybir.AluOpType
ACT = mybir.ActivationFunctionType
AX = mybir.AxisListType

B, T, D = 16, 128, 128
EPS = 1e-5
NH, DH = 16, 8
HG = 4
NG = NH // HG
L1H, L1D = 8, 64
L1P = L1H // 2
INNER = L1H * L1D
WINDOW = 64
MASKED = -1e30
E0, H0 = 8, 256
E1, H1 = 16, 64
E3, M3 = 8, 512
TOP_SHIFTS = 5
CH = 256
NC_ = B * T // CH
TPC = CH // T
DROP = -3e38

ROWS = [("gates", 8), ("router_bias", E1), ("b_proj", D), ("b_v", D), ("b_out", D), ("b3v", D), ("b3o", D)]
COLS = [("gamma_x", 1), ("beta_x", 1), ("gamma_l", 1), ("beta_l", 1), ("b_q", 1), ("b_k", 1), ("mu_r", 1),
        ("mu_k", 1), ("b3q", 1), ("b3k", 1), ("b1", E3 * M3 // 128)]
CONSTS = [("ident", 128), ("cos", T), ("sin", T), ("headmask", HG), ("earlier", T), ("mirror", T),
          ("column", 2 * B - 1), ("mean", B), ("window", T), ("countdown0", E0), ("countdown1", E1)]
WEIGHTS0 = [("w_proj", D), ("wg0", E0)]
WEIGHTS_F0 = [("w1", E0 * H0), ("w2", E0 * H0), ("w3", E0 * 2 * D)]
WEIGHTS_A1 = [("wq1", INNER), ("wk1", INNER), ("wkrot1", INNER), ("wv1", INNER), ("wo1", L1P * D), ("wg1", E1)]
WEIGHTS_F1 = [("up1", E1 * H1), ("gate1", E1 * H1), ("sh_gate", D), ("sh_up", D), ("sh_down", D)]
WEIGHTS_2 = [("wq2", D), ("wk2", D), ("wv2", D), ("wo2", D), ("wr", D), ("wk", D), ("wv", D),
             ("wq3", D), ("wk3", D), ("wv3", D), ("wo3", D), ("wg3", E3)]
WEIGHTS_F3 = [("w1_3", E3 * M3), ("w2_3", E3 * 4 * D)]


def width(parts):
    return sum(n for _, n in parts)


def views(tile, parts):
    at, out = 0, {}
    for name, n in parts:
        out[name] = tile[:, at:at + n]
        at += n
    return out


def split(ap, b):
    return ap.rearrange("p (a b) -> p a b", b=b)


def over(ap, n, axis):
    p, a = ap.shape
    return ap.unsqueeze(axis).broadcast_to([p, n, a] if axis == 1 else [p, a, n])


def at(tile, b):
    if isinstance(b, int):
        return tile[:, b, :]
    return tile[:, bass.ds(b, 1), :].rearrange("p o n -> p (o n)")


def wait(eng, sem, value):
    if not isinstance(value, int) or value > 0:
        eng.wait_ge(sem, value)


def wait_apart(eng, k, sem, value):
    wait(eng, sem, value)
    if not isinstance(value, int):
        eng.sem_inc(k.passed, 1)


def walk(eng, stages):
    lags = [lag for _, lag in stages]
    lo, hi = max(lags) + 2, min(lags) + B
    pairs = (hi - lo) // 2

    def tick(t, parity):
        for stage, lag in stages:
            b = t - lag
            if not isinstance(b, int) or 0 <= b < B:
                stage(b, (parity + lag) % 2)

    for t in range(min(lags), lo):
        tick(t, t % 2)
    with eng.Fori(0, pairs) as i:
        for k in range(2):
            tick(i * 2 + (lo + k), (lo + k) % 2)
    for t in range(lo + 2 * pairs, max(lags) + B):
        tick(t, t % 2)


class Semaphores:
    pass


def norm_names(sems, prefix):
    s = Semaphores()
    s.raw_stats, s.stats, s.var_eps, s.rstd = sems.new(prefix, "raw_stats stats var_eps rstd")
    return s


class Sublayer:

    def __init__(self, nc):
        self.nc, self.held = nc, []

    def new(self, prefix, text):
        made = [self.nc.alloc_semaphore(f"{prefix}_{name}") for name in text.split()]
        self.held += made
        return made

    def __enter__(self):
        return self

    def __exit__(self, *_):
        with self.nc.Block() as block:
            @block.sync
            def _(sp):
                for sem in self.held:
                    sp.sem_clear(sem)
        for sem in self.held:
            self.nc.release_semaphore(sem)


class Core:
    pass


def set_up(nc, ctx, k, a):
    def sb(name, shape, dt=FP32):
        return ctx.enter_context(nc.sbuf_tensor(name, shape, dt))

    k.x = sb("x_tok", [T, B, D])
    k.ctx = sb("ctx_tok", [T, B, D])
    k.ctxT = sb("ctx_feat", [D, B, T])
    k.xT = sb("xhat_feat", [D, B, T])
    k.rows_t = sb("rows", [128, width(ROWS)])
    k.rows = views(k.rows_t, ROWS)
    k.cols_t = sb("cols", [128, width(COLS)])
    k.cols = views(k.cols_t, COLS)
    k.consts_t = sb("consts", [128, width(CONSTS)])
    k.c = views(k.consts_t, CONSTS)
    k.maskb = sb("mask_bias", [128, 128 + 4 * T], BF16)
    k.w = {}
    for name, parts in a.weight_parts:
        tile = sb(name, [128, width(parts)])
        a.weight_tiles.append(tile)
        k.w.update(views(tile, parts))
    k.down1 = sb("down_pairs", [128, E1 // 2, 2 * D])
    k.b2_3 = sb("b2_rows", [E3, D])
    k.tg = sb("tanh_gates", [128, 8])
    k.tgb = sb("gated_bias", [128, 3, D])
    k.omu = sb("one_minus_mu", [128, 2])
    k.half = sb("half_and_eps", [128, 2])
    k.euler = sb("euler", [128, B])
    k.logits = sb("logits", [128, B, E1])
    k.gate_w = sb("expert_weights", [128, B, E1])
    k.e = sb("exps", [128, 2, 2048])
    k.pT = sb("probs_keymajor", [128, 2048])
    k.work = sb("work", [128, 8192])
    k.mid = sb("mid", [128, 1280])
    k.small = sb("small", [128, 1024])
    k.bank = ctx.enter_context(nc.psum_tensor("banks", [128, 8, 512], FP32))


def layer_norm_steps(nc, k, sem, st, mv, rstd):

    def statistics(dve, src, s, n, used):
        wait_apart(dve, k, used, n - 2)
        nc.vector.bn_stats(st[:, s, :], src).then_inc(sem.raw_stats, 1)
        wait_apart(dve, k, sem.raw_stats, n)
        nc.vector.bn_aggr(mv[:, s, :], st[:, s, :]).then_inc(sem.stats, 1)

    def deviation(pool, s, n):
        wait(pool, sem.stats, n)
        nc.gpsimd.tensor_tensor(rstd[:, s, 0:1], mv[:, s, 1:2], k.half[:, 1:2], ALU.add).then_inc(sem.var_eps, 1)
        wait(pool, sem.var_eps, n)
        nc.gpsimd.tensor_tensor(rstd[:, s, 1:2], rstd[:, s, 0:1], k.half[:, 0:1], ALU.pow).then_inc(sem.rstd, 1)

    def normalise(dve, dst, src, s, n):
        wait(dve, sem.rstd, n)
        return nc.vector.tensor_scalar(dst, src, mv[:, s, 0:1], rstd[:, s, 1:2], ALU.subtract, ALU.mult)

    return statistics, deviation, normalise


def norm_scratch(tile, at_):
    st = split(tile[:, at_:at_ + 12], 6)
    mv = split(tile[:, at_ + 12:at_ + 16], 2)
    rstd = split(tile[:, at_ + 16:at_ + 20], 2)
    return st, mv, rstd


def load_block(nc, sems, k, a, ld):
    s = Semaphores()
    (s.zeroed, s.tanh, s.transposed, s.ctxT, s.ready) = sems.new("load", """
        zeroed tanh transposed ctxT ready""")
    c, rows = k.c, k.rows

    with nc.Block() as block:
        @block.sync
        def _(sp):
            sp.dma_start(k.consts_t[:, :], a.consts).then_inc(ld.consts, 16)
            sp.dma_start(k.ctx[:, :, :], a.ctx.rearrange("b t d -> t b d")).then_inc(ld.ctx, 16)
            sp.dma_start(k.x[:, :, :], a.x.rearrange("b t d -> t b d")).then_inc(ld.x, 16)
            for n in (1, 4):
                sp.dma_start(a.weight_tiles[n][:, :], a.weights[n]).then_inc(ld.weights[n], 16)

        @block.scalar
        def _(act):
            act.dma_start(k.rows_t[:, :], a.rows.partition_broadcast(128)).then_inc(ld.rows, 16)
            act.dma_start(k.cols_t[:, :], a.cols).then_inc(ld.rows, 16)
            for n in (0, 2, 3, 5):
                act.dma_start(a.weight_tiles[n][:, :], a.weights[n]).then_inc(ld.weights[n], 16)
            act.dma_start(k.b2_3[:, :], a.b2_3).then_inc(ld.weights[5], 16)
            act.wait_ge(s.zeroed, 5)
            for half in range(2):
                act.dma_start(k.down1[64 * half:64 * half + 64, :, half * D:half * D + D],
                              a.down[half].rearrange("e h d -> h e d")).then_inc(ld.weights[3], 16)
            act.wait_ge(ld.rows, 32)
            nc.scalar.activation(k.tg[:, :], rows["gates"], ACT.Tanh).then_inc(s.tanh, 1)
            for g in range(4):
                act.wait_ge(s.transposed, g + 1)
                nc.scalar.activation(k.ctxT[:, 4 * g:4 * g + 4, :].rearrange("p a b -> p (a b)"),
                                     k.bank[:, g, :], ACT.Copy).then_inc(s.ctxT, 1)

        @block.tensor
        def _(pe):
            pe.wait_ge(ld.consts, 16)
            pe.wait_ge(ld.ctx, 16)
            pe.wait_ge(ld.rows, 32)
            for b in range(B):
                last = nc.tensor.transpose(k.bank[:, b // 4, (b % 4) * T:(b % 4 + 1) * T], k.ctx[:, b, :], c["ident"])
                if b % 4 == 3:
                    last.then_inc(s.transposed, 1)

        @block.gpsimd
        def _(pool):
            pool.wait_ge(ld.consts, 16)
            pool.wait_ge(ld.rows, 32)
            pool.wait_ge(ld.ctx, 16)
            pool.wait_ge(ld.x, 16)

        @block.vector
        def _(dve):
            nc.vector.memset(k.down1[:, :, :], 0.0).then_inc(s.zeroed, 1)
            nc.vector.memset(k.work[:, :], 0.0).then_inc(s.zeroed, 1)
            nc.vector.memset(k.half[:, 0:1], -0.5).then_inc(s.zeroed, 1)
            nc.vector.memset(k.half[:, 1:2], EPS).then_inc(s.zeroed, 1)
            nc.vector.memset(k.euler[:, :], float(np.float32(np.e))).then_inc(s.zeroed, 1)
            dve.wait_ge(s.tanh, 1)
            dve.wait_ge(ld.consts, 16)
            nc.vector.tensor_copy(k.maskb[:, 0:128], c["ident"]).then_inc(s.ready, 1)
            nc.vector.tensor_copy(split(k.maskb[:, 128:], T), over(c["window"], HG, 1)).then_inc(s.ready, 1)
            dve.wait_ge(ld.rows, 32)
            dve.wait_ge(ld.ctx, 16)
            dve.wait_ge(ld.x, 16)
            for n, (name, gate) in enumerate((("b_proj", 0), ("b_out", 2), ("b3o", 3))):
                nc.vector.tensor_scalar(k.tgb[:, n, :], rows[name], k.tg[:, gate:gate + 1], None,
                                        ALU.mult).then_inc(s.ready, 1)
            nc.vector.tensor_scalar(k.omu[:, :], k.cols_t[:, 6:8], -1.0, 1.0, ALU.mult, ALU.add).then_inc(s.ready, 1)


def small_head_attention(nc, sems, k, tag, src, masked, project, w_out, tg, tgb, w_gate, n_gate, ld):
    s = Semaphores()
    (s.q, s.keys, s.shifted, s.scores, s.ots, s.added, s.logits_out, s.xs2, s.otr, s.exp, s.pT, s.ptr,
     s.o, s.oTp, s.xh2, s.xT2, s.xh, s.kT, s.v, s.xTp, s.vpad, s.pv, s.oT, s.out, s.logits, s.xhT,
     s.ctxs, s.qkv, s.max, s.recip, s.biased, s.cleared, s.kept) = sems.new(tag, """
        q keys shifted scores ots added logits_out xs2 otr exp pT ptr o oTp xh2 xT2 xh kT v xTp vpad pv
        oT out logits xhT ctxs qkv max recip biased cleared kept""")
    c, cols = k.c, k.cols
    bank = k.bank
    MA, MB, PT = 6, 7, 4
    w = k.work
    qz = w[:, 0:1024].rearrange("p (s g t) -> p s g t", s=2, g=NG)
    kx = w[:, 1024:2048].rearrange("p (s j t) -> p s j t", s=2, j=HG)
    vpad = w[:, 2048:3072].rearrange("p (s h c) -> p s h c", s=2, h=NH)
    xh = split(w[:, 3072:3328], D)
    xhT = split(w[:, 3328:3584], T)
    kT = split(w[:, 3584:3840], T)
    ctxs = split(w[:, 3840:4096], T)
    ots = w[:, 4096:4608]
    o = w[:, 4608:4736]
    oT = w[:, 4736:4864]
    xh2 = split(w[:, 4864:5120], D)
    xs2 = split(w[:, 5120:5376], T)
    vtok = w[:, 5376:5376 + B * D].rearrange("p (b d) -> p b d", b=B) if project else k.ctx
    mx = split(k.small[:, 0:2 * NH], NH)
    rc = k.small[:, 32:48]
    first = norm_scratch(k.small, 64)
    second = norm_scratch(k.small, 96)
    s1, s2 = norm_names(sems, tag + "_in"), norm_names(sems, tag + "_out")
    stats1, dev1, norm1 = layer_norm_steps(nc, k, s1, *first)
    stats2, dev2, norm2 = layer_norm_steps(nc, k, s2, *second)

    with nc.Block() as block:
        @block.tensor
        def _(pe):
            def scores(first):
                def stage(b, sl):
                    wait(pe, s.q, b + 1)
                    wait(pe, s.keys, b + 1)
                    wait(pe, s.shifted, b * 2 + (first // 2 - 1))
                    for g in range(first, first + 2):
                        if masked:
                            nc.tensor.matmul(bank[:, g, :], k.maskb[:, 0:128], k.maskb[:, 128:], start=True, stop=False)
                        last = nc.tensor.matmul(bank[:, g, :], qz[:, sl, g, :],
                                                kx[:, sl, :, :].rearrange("p j t -> p (j t)"),
                                                start=not masked, stop=True)
                    last.then_inc(s.scores, 1)
                return stage

            def output_transpose(b, sl):
                wait(pe, s.ots, b + 1)
                wait(pe, s.added, b)
                if w_gate is not None:
                    wait(pe, s.logits_out, b - 1)
                wait(pe, s.xs2, b - 1)
                for g in range(NG):
                    last = nc.tensor.transpose(bank[:, MB, g * 128:(g + 1) * 128], ots[:, g * 128:(g + 1) * 128],
                                               c["ident"])
                last.then_inc(s.otr, 1)

            def probs(first):
                def stage(b, sl):
                    wait(pe, s.exp, b + 1)
                    for g in range(first, first + 2):
                        wait(pe, s.pT, b * NG + (g - 1))
                        if g == 0:
                            wait(pe, s.ots, b)
                        for j in range(HG):
                            h = g * HG + j
                            last = nc.tensor.transpose(bank[:, PT + g % 2, j * T:(j + 1) * T],
                                                       k.e[:, sl, h * T:(h + 1) * T], c["ident"])
                        last.then_inc(s.ptr, 1)
                return stage

            def out_T(b, sl):
                wait(pe, s.o, b + 1)
                nc.tensor.transpose(bank[:, MB, 0:T], o, c["ident"]).then_inc(s.oTp, 1)

            def next_T(b, sl):
                wait(pe, s.xh2, b + 1)
                wait(pe, s.added, min(b + 2, B) if isinstance(b, int) else b + 2)
                if w_gate is not None:
                    wait(pe, s.logits_out, b)
                wait(pe, s.xs2, b)
                nc.tensor.transpose(bank[:, MB, 256:256 + T], xh2[:, sl, :], c["ident"]).then_inc(s.xT2, 1)

            def in_T(b, sl):
                wait(pe, s.xh, b + 1)
                wait(pe, s.q, b)
                if project:
                    wait(pe, s.kT, b)
                    wait(pe, s.v, b)
                nc.tensor.transpose(bank[:, MA, 0:T], xh[:, sl, :], c["ident"]).then_inc(s.xTp, 1)

            def pv(b, sl):
                wait(pe, s.pT, b * NG + NG)
                wait(pe, s.vpad, b + 1)
                for g in range(NG):
                    for j in range(HG):
                        h = g * HG + j
                        last = nc.tensor.matmul(bank[32 * j:32 * j + 32, PT, g * T:(g + 1) * T], vpad[:, sl, h, :],
                                                k.pT[:, h * T:(h + 1) * T], start=True, stop=True)
                last.then_inc(s.pv, 1)

            def out(b, sl):
                wait(pe, s.oT, b + 1)
                nc.tensor.matmul(bank[:, MB, 128:256], oT, w_out, start=True, stop=True).then_inc(s.out, 1)

            def logits(b, sl):
                wait(pe, s.xs2, b + 1)
                nc.tensor.matmul(bank[:, MB, 384:384 + n_gate], xs2[:, sl, :], w_gate,
                                 start=True, stop=True).then_inc(s.logits, 1)

            def qkv(b, sl):
                wait(pe, s.xhT, b + 1)
                wait(pe, s.ctxs, b + 1)
                nc.tensor.matmul(bank[:, MA, 128:256], k.w["wq2"], xhT[:, sl, :], start=True, stop=True)
                nc.tensor.matmul(bank[:, MA, 256:384], k.w["wk2"], ctxs[:, sl, :], start=True, stop=True)
                nc.tensor.matmul(bank[:, MA, 384:512], ctxs[:, sl, :], k.w["wv2"], start=True, stop=True).then_inc(s.qkv, 1)

            pe.wait_ge(ld.weights[4 if project else 0], 16)
            walk(pe, [(qkv, 1), (out, 5), (probs(2), 4), (scores(0), 2), (pv, 4), (next_T, 6), (scores(2), 2),
                  (output_transpose, 4), (in_T, 0), (probs(0), 3), (out_T, 4)]
                 if project else
                 [(in_T, 0), (output_transpose, 4), (probs(2), 3), (out_T, 4), (scores(2), 1), (out, 4), (pv, 3),
                  (next_T, 5), (scores(0), 0), (logits, 5), (probs(0), 2)])

        @block.vector
        def _(dve):
            def maximum(half):
                def stage(b, sl):
                    wait(dve, s.scores, b * 2 + (half + 1))
                    nc.vector.tensor_reduce(mx[:, sl, 8 * half:8 * half + 8],
                                            bank[:, 2 * half:2 * half + 2, :].rearrange("p g (j t) -> p (g j) t", j=HG),
                                            AX.X, ALU.max).then_inc(s.max, 1)
                return stage

            def shift(half):
                def stage(b, sl):
                    wait(dve, s.max, b * 2 + (half + 1))
                    wait(dve, s.ptr, b * NG - NG)
                    nc.vector.tensor_tensor(split(k.e[:, sl, 1024 * half:1024 * half + 1024], T),
                                            bank[:, 2 * half:2 * half + 2, :].rearrange("p g (j t) -> p (g j) t", j=HG),
                                            over(mx[:, sl, 8 * half:8 * half + 8], T, 2), ALU.subtract).then_inc(s.shifted, 1)
                return stage

            def divide(b, sl):
                wait(dve, s.otr, b + 1)
                heads = split(bank[:, MB, :], 32)
                nc.vector.reciprocal(rc, heads[:, :, DH:DH + 1].rearrange("p h o -> p (h o)")).then_inc(s.recip, 1)
                wait(dve, s.recip, b + 1)
                wait(dve, s.oTp, b)
                nc.vector.tensor_tensor(split(o, DH), heads[:, :, 0:DH], over(rc, DH, 2), ALU.mult).then_inc(s.o, 1)

            def add(b, sl):
                wait(dve, s.out, b + 1)
                wait(dve, s.biased, b + 1)
                nc.vector.scalar_tensor_tensor(at(k.x, b), bank[:, MB, 128:256], tg, at(k.x, b), ALU.mult,
                                               ALU.add).then_inc(s.added, 1)

            def stats_in(b, sl):
                stats1(dve, at(k.x, b), sl, b + 1, s.xh)

            def norm_in(b, sl):
                wait(dve, s.xTp, b - 1)
                norm1(dve, xh[:, sl, :], at(k.x, b), sl, b + 1).then_inc(s.xh, 1)

            def stats_out(b, sl):
                wait(dve, s.added, b + 1)
                stats2(dve, at(k.x, b), sl, b + 1, s.xh2)

            def norm_out(b, sl):
                wait(dve, s.xT2, b - 1)
                norm2(dve, xh2[:, sl, :], at(k.x, b), sl, b + 1).then_inc(s.xh2, 1)

            def values(b, sl):
                wait(dve, s.qkv, b + 1)
                wait(dve, s.q, b + 1)
                nc.vector.tensor_tensor(at(vtok, b), bank[:, MA, 384:512], k.rows["b_v"], ALU.add).then_inc(s.v, 1)

            walk(dve, [(divide, 5), (maximum(1), 3), (stats_in, 0), (shift(1), 3), (add, 5), (stats_out, 5),
                  (maximum(0), 2), (norm_in, 0), (values, 1), (norm_out, 5), (shift(0), 2)]
                 if project else
                 [(stats_in, 0), (maximum(1), 3), (norm_in, 1), (stats_out, 6), (shift(1), 3), (norm_out, 6),
                  (divide, 5), (maximum(0), 2), (shift(0), 2), (add, 5)])

        @block.gpsimd
        def _(pool):
            nc.gpsimd.memset(qz, 0.0).then_inc(s.cleared, 1)
            nc.gpsimd.memset(vpad, 0.0).then_inc(s.cleared, 1)
            pool.wait_ge(s.cleared, 2)
            nc.gpsimd.memset(vpad[:, :, :, DH:DH + 1], 1.0).then_inc(s.cleared, 1)
            pool.wait_ge(s.cleared, 3)

            def dev_in(b, sl):
                dev1(pool, sl, b + 1)
                if project:
                    wait_apart(pool, k, s.qkv, b - 1)
                    nc.gpsimd.tensor_copy(ctxs[:, sl, :], at(k.ctxT, b)).then_inc(s.ctxs, 1)

            def bias(b, sl):
                wait_apart(pool, k, s.xh, b + 1)
                nc.gpsimd.tensor_tensor(at(k.x, b), at(k.x, b), tgb, ALU.add).then_inc(s.biased, 1)

            def dev_out(b, sl):
                dev2(pool, sl, b + 1)

            def spread_keys(b, sl):
                if project:
                    wait(pool, s.kT, b + 1)
                wait_apart(pool, k, s.scores, b * 2 - 2)
                keys = kT[:, sl, :] if project else at(k.ctxT, b)
                nc.gpsimd.tensor_tensor(kx[:, sl, :, :], over(keys, HG, 1), over(c["headmask"], T, 2),
                                        ALU.mult).then_inc(s.keys, 1)

            def spread_values(b, sl):
                if project:
                    wait(pool, s.v, b + 1)
                wait_apart(pool, k, s.pv, b - 1)
                nc.gpsimd.tensor_copy(vpad[:, sl, :, 0:DH], split(at(vtok, b), DH)).then_inc(s.vpad, 1)

            def keep(b, sl):
                wait_apart(pool, k, s.xs2, b + 1)
                nc.gpsimd.tensor_copy(at(k.xT, b), xs2[:, sl, :]).then_inc(s.kept, 1)

            walk(pool, [(bias, 3), (dev_in, 0), (spread_keys, 1), (keep, 6), (dev_out, 4), (spread_values, 2)]
                 if project else
                 [(dev_in, 0), (spread_keys, 1), (bias, 5), (dev_out, 5), (spread_values, 2), (keep, 6)])

        @block.scalar
        def _(act):
            act.wait_ge(s.cleared, 3)

            def exps(b, sl):
                wait(act, s.shifted, b * 2 + 2)
                nc.scalar.activation(k.e[:, sl, :], k.e[:, sl, :], ACT.Exp, scale=float(1 / np.sqrt(DH))).then_inc(s.exp, 1)

            def probs_out(b, sl):
                for g in range(NG):
                    wait(act, s.ptr, b * NG + (g + 1))
                    if g == 0:
                        wait(act, s.pv, b)
                    nc.scalar.activation(k.pT[:, g * 512:(g + 1) * 512], bank[:, PT + g % 2, :], ACT.Copy).then_inc(s.pT, 1)

            def out_T(b, sl):
                wait(act, s.oTp, b + 1)
                wait(act, s.out, b)
                nc.scalar.activation(oT, bank[:, MB, 0:T], ACT.Copy).then_inc(s.oT, 1)

            def next_T(b, sl):
                wait(act, s.xT2, b + 1)
                wait(act, s.kept, b - 1)
                if w_gate is not None:
                    wait(act, s.logits, b - 1)
                nc.scalar.activation(xs2[:, sl, :], bank[:, MB, 256:256 + T], ACT.Copy).then_inc(s.xs2, 1)

            def in_T(b, sl):
                wait(act, s.xTp, b + 1)
                wait(act, s.qkv, b - 1)
                nc.scalar.activation(xhT[:, sl, :], bank[:, MA, 0:T], ACT.Copy).then_inc(s.xhT, 1)

            def queries(b, sl):
                if project:
                    wait(act, s.qkv, b + 1)
                    wait(act, s.keys, b - 1)
                    nc.scalar.activation(kT[:, sl, :], bank[:, MA, 256:384], ACT.Identity,
                                         bias=cols["b_k"]).then_inc(s.kT, 1)
                else:
                    wait(act, s.xTp, b + 1)
                wait(act, s.scores, b * 2 - 2)
                for g in range(NG):
                    p = slice(32 * g, 32 * g + 32)
                    if project:
                        last = nc.scalar.activation(qz[p, sl, g, :], bank[p, MA, 128:256], ACT.Identity,
                                                    bias=cols["b_q"][p, :])
                    else:
                        last = nc.scalar.activation(qz[p, sl, g, :], bank[p, MA, 0:T], ACT.Copy)
                last.then_inc(s.q, 1)

            def outputs(b, sl):
                wait(act, s.pv, b + 1)
                wait(act, s.otr, b)
                nc.scalar.activation(ots, bank[:, PT, :], ACT.Copy).then_inc(s.ots, 1)

            def logits(b, sl):
                wait_apart(act, k, s.logits, b + 1)
                nc.scalar.activation(at(k.logits, b)[:, 0:n_gate], bank[:, MB, 384:384 + n_gate],
                                     ACT.Copy).then_inc(s.logits_out, 1)

            walk(act, [(probs_out, 4), (queries, 1), (exps, 3), (outputs, 4), (next_T, 6), (in_T, 0), (out_T, 4)]
                 if project else
                 [(probs_out, 3), (out_T, 4), (queries, 0), (exps, 2), (next_T, 5), (outputs, 3), (logits, 5)])



def latent_attention(nc, sems, k, ld):
    s = Semaphores()
    (s.ch, s.lh, s.v, s.inT, s.q, s.k_ctx, s.k_lat, s.exp, s.scores, s.k1, s.kvT, s.k2, s.t1, s.k3, s.t2,
     s.q1, s.v1, s.norm, s.pT, s.oT, s.ptr, s.pv, s.added, s.logits_out, s.out, s.xh2, s.xs2, s.xT2,
     s.logits, s.inv, s.max, s.nmax, s.xh, s.cleared, s.kept) = sems.new("a1", """
        ch lh v inT q k_ctx k_lat exp scores k1 kvT k2 t1 k3 t2 q1 v1 norm pT oT ptr pv added logits_out
        out xh2 xs2 xT2 logits inv max nmax xh cleared kept""")
    c, cols, bank, w = k.c, k.cols, k.bank, k.work
    MA, MB, PT = 6, 7, 4
    qm = w[:, 0:2048].rearrange("p (s h t) -> p s h t", s=2, h=L1H)
    kT = w[:, 2048:4096].rearrange("p (s h t) -> p s h t", s=2, h=L1P)
    v = w[:, 4096:6144].rearrange("p (s i n) -> p s i n", s=2, i=2)
    kvT = w[:, 6144:6656].rearrange("p (s t) -> p s t", s=2)
    t1, t2 = w[:, 6656:7168], w[:, 7168:7680]
    oT = w[:, 7680:8192]
    m = k.mid
    ch, xh, lh, xh2, xs2 = (split(m[:, n * 256:(n + 1) * 256], 128) for n in range(5))
    mx = split(k.small[:, 0:16], L1H)
    nmx = split(k.small[:, 16:32], L1H)
    sums = split(k.small[:, 32:48], L1H)
    inv = split(k.small[:, 48:64], L1H)
    sc, sx, sl2, so = (norm_names(sems, "a1_" + n) for n in ("ctx", "x", "lat", "out"))
    stats_c, dev_c, norm_c = layer_norm_steps(nc, k, sc, *norm_scratch(k.small, 64))
    stats_x, dev_x, norm_x = layer_norm_steps(nc, k, sx, *norm_scratch(k.small, 96))
    stats_l, dev_l, norm_l = layer_norm_steps(nc, k, sl2, *norm_scratch(k.small, 128))
    stats_o, dev_o, norm_o = layer_norm_steps(nc, k, so, *norm_scratch(k.small, 160))
    tg = k.tg[:, 1:2]
    SCALE = L1D ** -0.5

    with nc.Block() as block:
        @block.tensor
        def _(pe):
            def in_T(b, sl):
                wait(pe, s.ch, b + 1)
                wait(pe, s.lh, b + 1)
                wait(pe, s.v, 2 * b)
                nc.tensor.transpose(bank[:, MA, 0:T], ch[:, sl, :], c["ident"])
                nc.tensor.transpose(bank[:, MA, T:2 * T], lh[:, sl, :], c["ident"]).then_inc(s.inT, 1)

            def scores(half):
                def stage(b, sl):
                    wait(pe, s.q, b + 1)
                    wait(pe, s.k_ctx, b + 1)
                    wait(pe, s.k_lat, b + 1)
                    wait(pe, s.exp, L1H * b - (L1H // 2 if half == 0 else 0))
                    for h in range(4 * half, 4 * half + 4):
                        last = nc.tensor.matmul(bank[:, h // 2, (h % 2) * 256:(h % 2) * 256 + 256], qm[:, sl, h, :],
                                                kT[:, sl, h // 2, :], start=True, stop=True)
                    last.then_inc(s.scores, 1)
                return stage

            def project(weight, part, done, gate):
                def stage(b, sl):
                    gate(b)
                    for p in range(L1P):
                        last = nc.tensor.matmul(bank[:, MA, p * T:(p + 1) * T], k.w[weight][:, p * 128:(p + 1) * 128],
                                                kvT[:, sl, part * T:(part + 1) * T], start=True, stop=True)
                    last.then_inc(done, 1)
                return stage

            k_ctx = project("wk1", 0, s.k1, lambda b: wait(pe, s.kvT, b + 1))
            k_rot = project("wkrot1", 0, s.k2, lambda b: wait(pe, s.t1, b + 1))
            k_lat = project("wk1", 1, s.k3, lambda b: wait(pe, s.t2, b + 1))
            query = project("wq1", 1, s.q1, lambda b: wait(pe, s.k_lat, b + 1))

            def values(i):
                def stage(b, sl):
                    wait(pe, s.q, b + 1) if i == 0 else wait(pe, s.v, 2 * b + 1)
                    nc.tensor.matmul(bank[:, MA, :], kvT[:, sl, i * T:(i + 1) * T], k.w["wv1"], start=True,
                                     stop=True).then_inc(s.v1, 1)
                return stage

            def probs(g0):
                def stage(b, sl):
                    for g in range(g0, g0 + 2):
                        wait(pe, s.norm, b * L1H + 2 * g + 2)
                        wait(pe, s.pT, b * 4 + (g - 1))
                        if g == 0:
                            wait(pe, s.oT, b)
                        for j in range(4):
                            n = g * 4 + j
                            last = nc.tensor.transpose(bank[:, PT + g % 2, j * T:(j + 1) * T],
                                                       k.e[:, sl, n * T:(n + 1) * T], c["ident"])
                        last.then_inc(s.ptr, 1)
                return stage

            def pv(b, sl):
                wait(pe, s.pT, b * 4 + 4)
                wait(pe, s.v, 2 * b + 2)
                for p in range(L1P):
                    for i in range(2):
                        for par in range(2):
                            h = 2 * p + par
                            last = nc.tensor.matmul(bank[64 * par:64 * par + 64, PT, p * T:(p + 1) * T],
                                                    v[:, sl, i, h * L1D:(h + 1) * L1D],
                                                    k.pT[:, (2 * h + i) * T:(2 * h + i + 1) * T], start=i == 0, stop=i == 1)
                last.then_inc(s.pv, 1)

            def out(b, sl):
                wait(pe, s.oT, b + 1)
                wait(pe, s.added, b)
                wait(pe, s.logits_out, b - 1)
                for p in range(L1P):
                    last = nc.tensor.matmul(bank[:, MB, 0:D], oT[:, p * 128:(p + 1) * 128],
                                            k.w["wo1"][:, p * D:(p + 1) * D], start=p == 0, stop=p == L1P - 1)
                last.then_inc(s.out, 1)

            def next_T(b, sl):
                wait(pe, s.xh2, b + 1)
                wait(pe, s.added, min(b + 2, B) if isinstance(b, int) else b + 2)
                wait(pe, s.logits_out, b)
                wait(pe, s.xs2, b)
                nc.tensor.transpose(bank[:, MB, 128:256], xh2[:, sl, :], c["ident"]).then_inc(s.xT2, 1)

            def logits(b, sl):
                wait(pe, s.xs2, b + 1)
                wait(pe, s.logits_out, b)
                nc.tensor.matmul(bank[:, MB, 256:256 + E1], xs2[:, sl, :], k.w["wg1"], start=True,
                                 stop=True).then_inc(s.logits, 1)

            pe.wait_ge(ld.weights[2], 16)
            walk(pe, [(k_ctx, 1), (probs(0), 3), (k_rot, 1), (logits, 5), (scores(1), 2), (k_lat, 1),
                      (probs(2), 3), (query, 1), (pv, 3), (values(0), 1), (out, 3), (values(1), 1), (scores(0), 1),
                      (in_T, 0), (next_T, 4)])

        @block.vector
        def _(dve):
            def normalise(b, sl):
                wait(dve, s.exp, L1H * b + L1H)
                nc.vector.reciprocal(inv[:, sl, :], sums[:, sl, :]).then_inc(s.inv, 1)
                wait(dve, s.inv, b + 1)
                for h in range(L1H):
                    part = k.e[:, sl, h * 256:(h + 1) * 256]
                    nc.vector.tensor_scalar(part, part, inv[:, sl, h:h + 1], None, ALU.mult).then_inc(s.norm, 1)

            def rope_cos(b, sl):
                wait(dve, s.k1, b + 1)
                wait(dve, s.k_ctx, b)
                nc.vector.tensor_tensor(split(t1, T), split(bank[:, MA, :], T), over(c["cos"], L1P, 1),
                                        ALU.mult).then_inc(s.t1, 1)

            def rope_sin(b, sl):
                wait(dve, s.k2, b + 1)
                nc.vector.tensor_tensor(split(t2, T), split(bank[:, MA, :], T), over(c["sin"], L1P, 1),
                                        ALU.mult).then_inc(s.t2, 1)

            def maximum(b, sl):
                wait(dve, s.scores, 2 * b + 2)
                wait(dve, s.exp, L1H * (b - 1))
                nc.vector.tensor_reduce(mx[:, sl, :], bank[:, 0:4, :].rearrange("p g (j t) -> p (g j) t", j=2), AX.X,
                                        ALU.max).then_inc(s.max, 1)
                wait(dve, s.max, b + 1)
                nc.vector.tensor_scalar(nmx[:, sl, :], mx[:, sl, :], -SCALE, None, ALU.mult).then_inc(s.nmax, 1)

            def outputs(b, sl):
                wait(dve, s.pv, b + 1)
                wait(dve, s.out, b)
                nc.vector.tensor_copy(oT, bank[:, PT, :]).then_inc(s.oT, 1)

            def values(i):
                def stage(b, sl):
                    wait(dve, s.v1, 2 * b + i + 1)
                    wait(dve, s.pv, b - 1)
                    nc.vector.tensor_copy(v[:, sl, i, :], bank[:, MA, :]).then_inc(s.v, 1)
                return stage

            def add(b, sl):
                wait(dve, s.out, b + 1)
                wait(dve, s.xh, b + 1)
                nc.vector.scalar_tensor_tensor(at(k.x, b), bank[:, MB, 0:D], tg, at(k.x, b), ALU.mult,
                                               ALU.add).then_inc(s.added, 1)

            def stats_in(b, sl):
                stats_x(dve, at(k.x, b), sl, b + 1, s.xh)
                stats_c(dve, at(k.ctx, b), sl, b + 1, s.ch)

            def norm_in(b, sl):
                wait(dve, s.lh, b - 1)
                norm_x(dve, xh[:, sl, :], at(k.x, b), sl, b + 1).then_inc(s.xh, 1)
                wait(dve, s.inT, b - 1)
                norm_c(dve, ch[:, sl, :], at(k.ctx, b), sl, b + 1).then_inc(s.ch, 1)
                wait(dve, s.xh, b + 1)
                stats_l(dve, xh[:, sl, :], sl, b + 1, s.lh)

            def norm_latent(b, sl):
                wait(dve, s.inT, b - 1)
                norm_l(dve, lh[:, sl, :], xh[:, sl, :], sl, b + 1).then_inc(s.lh, 1)

            def stats_out(b, sl):
                wait(dve, s.added, b + 1)
                stats_o(dve, at(k.x, b), sl, b + 1, s.xh2)

            def norm_out(b, sl):
                wait(dve, s.xT2, b - 1)
                norm_o(dve, xh2[:, sl, :], at(k.x, b), sl, b + 1).then_inc(s.xh2, 1)

            def logits(b, sl):
                wait(dve, s.logits, b + 1)
                nc.vector.tensor_tensor(at(k.logits, b)[:, 0:E1], bank[:, MB, 256:256 + E1], k.rows["router_bias"],
                                        ALU.add).then_inc(s.logits_out, 1)

            walk(dve, [(outputs, 4), (norm_latent, 1), (values(0), 2), (norm_out, 5), (add, 4), (values(1), 2),
                       (normalise, 3), (rope_cos, 1), (stats_in, 0), (rope_sin, 1), (stats_out, 4), (logits, 5),
                       (maximum, 2), (norm_in, 0)])

        @block.gpsimd
        def _(pool):
            nc.gpsimd.memset(qm, 0.0).then_inc(s.cleared, 1)

            def dev_in(b, sl):
                dev_x(pool, sl, b + 1)
                dev_c(pool, sl, b + 1)

            def dev_latent(b, sl):
                dev_l(pool, sl, b + 1)

            def dev_out(b, sl):
                dev_o(pool, sl, b + 1)

            def rope_add(b, sl):
                wait(pool, s.t1, b + 1)
                wait(pool, s.t2, b + 1)
                wait(pool, s.scores, 2 * (b - 1))
                nc.gpsimd.tensor_tensor(kT[:, sl, :, 0:T], split(t1, T), split(t2, T), ALU.add).then_inc(s.k_ctx, 1)

            def keep(b, sl):
                wait_apart(pool, k, s.xs2, b + 1)
                nc.gpsimd.tensor_copy(at(k.xT, b), xs2[:, sl, :]).then_inc(s.kept, 1)

            walk(pool, [(rope_add, 2), (dev_out, 5), (dev_latent, 1), (keep, 6), (dev_in, 0)])

        @block.scalar
        def _(act):
            act.wait_ge(s.cleared, 1)

            def in_T(b, sl):
                wait(act, s.inT, b + 1)
                wait(act, s.v1, 2 * (b - 1))
                for i, (gamma, beta) in enumerate((("gamma_x", "beta_x"), ("gamma_l", "beta_l"))):
                    last = nc.scalar.activation(kvT[:, sl, i * T:(i + 1) * T], bank[:, MA, i * T:(i + 1) * T], ACT.Identity,
                                                scale=cols[gamma], bias=cols[beta])
                last.then_inc(s.kvT, 1)

            def probs(g0):
                def stage(b, sl):
                    for g in range(g0, g0 + 2):
                        wait(act, s.ptr, b * 4 + (g + 1))
                        if g == 0:
                            wait(act, s.pv, b)
                        nc.scalar.activation(k.pT[:, g * 512:(g + 1) * 512], bank[:, PT + g % 2, :],
                                             ACT.Copy).then_inc(s.pT, 1)
                return stage

            def k_lat(b, sl):
                wait(act, s.k3, b + 1)
                wait(act, s.scores, 2 * (b - 1))
                nc.scalar.activation(kT[:, sl, :, T:2 * T], split(bank[:, MA, :], T), ACT.Copy).then_inc(s.k_lat, 1)

            def query(b, sl):
                wait(act, s.q1, b + 1)
                wait(act, s.scores, 2 * (b - 1))
                for par in range(2):
                    p = slice(64 * par, 64 * par + 64)
                    last = nc.scalar.activation(qm[p, sl, par::2, :], split(bank[p, MA, :], T), ACT.Copy)
                last.then_inc(s.q, 1)

            def exps(b, sl):
                wait(act, s.nmax, b + 1)
                wait(act, s.ptr, 4 * (b - 1))
                wait(act, s.inv, b - 1)
                for h in range(L1H):
                    nc.scalar.activation(k.e[:, sl, h * 256:(h + 1) * 256],
                                         bank[:, h // 2, (h % 2) * 256:(h % 2) * 256 + 256], ACT.Exp,
                                         bias=nmx[:, sl, h:h + 1], scale=SCALE,
                                         accum_out=sums[:, sl, h:h + 1]).then_inc(s.exp, 1)

            def next_T(b, sl):
                wait(act, s.xT2, b + 1)
                wait(act, s.kept, b - 1)
                wait(act, s.logits, b - 1)
                nc.scalar.activation(xs2[:, sl, :], bank[:, MB, 128:256], ACT.Copy).then_inc(s.xs2, 1)

            walk(act, [(next_T, 5), (probs(0), 3), (k_lat, 1), (probs(2), 3), (query, 1), (exps, 2), (in_T, 0)])


def choose_experts(nc, s, k, n, gate, dve, pool):
    lg = k.logits[:, :, 0:n]
    wt = k.gate_w[:, :, 0:n]
    sc = k.small
    eq1, eq2, lg2 = (sc[:, i * B * n:(i + 1) * B * n].rearrange("p (b e) -> p b e", e=n) for i in range(3))
    col = lambda i: sc[:, 768 + B * i:768 + B * i + B]
    m1, m2, r1, r2, d, ex, den, w1, w2 = (col(i) for i in range(9))
    count = k.c["countdown0" if n == E0 else "countdown1"].unsqueeze(1).broadcast_to([128, B, n])
    if pool is not None:
        pool.wait_ge(s.gate_step, 13)
        nc.gpsimd.tensor_tensor(ex, k.euler[:, :], d, ALU.pow).then_inc(s.gate_exp, 1)
        return
    done = [0]

    def step(instruction):
        done[0] += 1
        instruction.then_inc(s.gate_step, 1)
        dve.wait_ge(s.gate_step, done[0])

    v = nc.vector
    step(v.tensor_reduce(m1, lg, AX.X, ALU.max))
    step(v.tensor_tensor(eq1, lg, over(m1, n, 2), ALU.is_equal))
    step(v.tensor_tensor(eq1, eq1, count, ALU.mult))
    step(v.tensor_reduce(r1, eq1, AX.X, ALU.max))
    step(v.tensor_tensor(eq1, eq1, over(r1, n, 2), ALU.is_equal))
    step(v.scalar_tensor_tensor(lg2, eq1, DROP, lg, ALU.mult, ALU.add))
    step(v.tensor_reduce(m2, lg2, AX.X, ALU.max))
    step(v.tensor_tensor(eq2, lg2, over(m2, n, 2), ALU.is_equal))
    step(v.tensor_tensor(eq2, eq2, count, ALU.mult))
    step(v.tensor_reduce(r2, eq2, AX.X, ALU.max))
    step(v.tensor_tensor(eq2, eq2, over(r2, n, 2), ALU.is_equal))
    step(v.tensor_tensor(d, m2, m1, ALU.subtract))
    step(v.tensor_scalar(d, d, -100.0, None, ALU.max))
    dve.wait_ge(s.gate_exp, 1)
    step(v.tensor_scalar(den, ex, 1.0, None, ALU.add))
    step(v.reciprocal(den, den))
    step(v.tensor_scalar(w1, den, gate, None, ALU.mult))
    step(v.tensor_tensor(w2, ex, w1, ALU.mult))
    step(v.tensor_tensor(wt, eq1, over(w1, n, 2), ALU.mult))
    step(v.tensor_tensor(eq2, eq2, over(w2, n, 2), ALU.mult))
    step(v.tensor_tensor(wt, wt, eq2, ALU.add))


def two_deep(eng, ahead, behind, n):
    def chunk(cc, last):
        for e in range(n):
            if not (last and e == n - 1):
                ahead(cc + (e + 1) // n, (e + 1) % n)
            behind(cc, e)
    ahead(0, 0)
    chunk(0, False)
    with eng.Fori(1, NC_ - 1) as cc:
        chunk(cc, False)
    chunk(NC_ - 1, True)


class Step:

    def __init__(self, gates, ups, biases, downs, shares):
        self.gates, self.ups, self.biases = gates, ups, biases
        self.downs = downs
        self.shares = shares


def expert_layer(nc, sems, k, tag, steps, slots, func, n_gate, gate, loaded, b2=None):
    s = Semaphores()
    (s.gate_step, s.wT, s.wT_out, s.b2, s.b2_added, s.h, s.up, s.added, s.y, s.act, s.gate_exp) = sems.new(tag, """
        gate_step wT wT_out b2 b2_added h up added y act gate_exp""")
    bank, n = k.bank, len(steps)
    blocks = len(steps[0].gates)
    per = max(1, blocks * (2 if steps[0].ups else 1) * CH // 512)
    ybase = per * slots
    gate_sb = k.e[:, :, :].rearrange("p a b -> p (a b)")
    gs = [gate_sb[:, i * 512:i * 512 + blocks * CH] for i in range(slots)]
    hs = [k.work[:, i * 1024:i * 1024 + blocks * CH] for i in range(slots)]
    parts = [len(st.shares) * TPC for st in steps]
    before = [sum(parts[:e]) for e in range(n)]
    hidden = lambda slot: bank[:, per * slot:per * (slot + 1), :].rearrange("p a b -> p (a b)")

    with nc.Block() as block:
        @block.tensor
        def _(pe):
            pe.wait_ge(loaded[0], loaded[1])
            if b2 is not None:
                pe.wait_ge(s.gate_step, 20)
                for b in range(B):
                    last = nc.tensor.transpose(bank[0:n_gate, b // 4, (b % 4) * T:(b % 4 + 1) * T],
                                               k.gate_w[:, b, 0:n_gate], k.c["ident"])
                last.then_inc(s.wT, 1)
                pe.wait_ge(s.wT_out, 1)
                for b in range(B):
                    last = nc.tensor.matmul(bank[:, 4 + b // 4, (b % 4) * T:(b % 4 + 1) * T],
                                            k.e[0:n_gate, b // 8, (b % 8) * T:(b % 8 + 1) * T], b2,
                                            start=True, stop=True)
                last.then_inc(s.b2, 1)
                pe.wait_ge(s.b2_added, 1)

            def up(cc, e):
                m = cc * n + e
                wait(pe, s.h, m + 1 - slots)
                rhs = (k.xT[:, TPC * cc:TPC * cc + TPC, :] if isinstance(cc, int)
                       else k.xT[:, bass.ds(cc * TPC, TPC), :]).rearrange("p b t -> p (b t)")
                out = hidden(e % slots)
                for i, lhsT in enumerate(steps[e].gates + steps[e].ups):
                    last = nc.tensor.matmul(out[:, i * CH:(i + 1) * CH], lhsT, rhs, start=True, stop=True)
                last.then_inc(s.up, 1)

            def down(cc, e):
                m = cc * n + e
                wait(pe, s.h, m + 1)
                if slots <= e:
                    wait(pe, s.added, cc * sum(parts) + before[e - slots + 1])
                elif not isinstance(cc, int) or cc > 0:
                    wait(pe, s.added, (cc - 1) * sum(parts) + (before + [sum(parts)])[e - slots + 1 + n])
                wide = len(steps[e].shares) * D
                for i in range(TPC):
                    for j, rhs in enumerate(steps[e].downs):
                        last = nc.tensor.matmul(bank[:, ybase + e % slots, i * wide:(i + 1) * wide],
                                                hs[e % slots][:, j * CH + i * T:j * CH + (i + 1) * T], rhs,
                                                start=j == 0, stop=j == len(steps[e].downs) - 1)
                last.then_inc(s.y, 1)

            two_deep(pe, up, down, n)

        @block.scalar
        def _(act):
            if b2 is not None:
                act.wait_ge(s.wT, 1)
                nc.scalar.activation(k.e[0:n_gate, :, 0:1024], bank[0:n_gate, 0:4, :].rearrange("p (a b) t -> p a (b t)", a=2),
                                     ACT.Copy).then_inc(s.wT_out, 1)
                act.wait_ge(s.b2, 1)

            def nonlinear(cc, e):
                m = cc * n + e
                wait(act, s.up, m + 1)
                src = hidden(e % slots)
                if steps[e].ups:
                    wait(act, s.h, m + 1 - slots)
                    nc.scalar.activation(gs[e % slots], src[:, 0:blocks * CH], func).then_inc(s.act, 1)
                else:
                    wait(act, s.y, m + 1 - slots)
                    for i, bias in enumerate(steps[e].biases):
                        last = nc.scalar.activation(hs[e % slots][:, i * CH:(i + 1) * CH], src[:, i * CH:(i + 1) * CH],
                                                    func, bias=bias)
                    last.then_inc(s.h, 1)

            def nothing(cc, e):
                pass
            two_deep(act, nothing, nonlinear, n)

        @block.vector
        def _(dve):
            choose_experts(nc, s, k, n_gate, gate, dve, None)
            if b2 is not None:
                dve.wait_ge(s.b2, 1)
                nc.vector.scalar_tensor_tensor(k.x[:, :, :].rearrange("p b d -> p (b d)"),
                                               bank[:, 4:8, :].rearrange("p a b -> p (a b)"), 1.0,
                                               k.x[:, :, :].rearrange("p b d -> p (b d)"), ALU.mult,
                                               ALU.add).then_inc(s.b2_added, 1)
                dve.wait_ge(s.b2_added, 1)

            def product(cc, e):
                if not steps[e].ups:
                    return
                m = cc * n + e
                wait(dve, s.act, m + 1)
                wait(dve, s.y, m + 1 - slots)
                nc.vector.tensor_tensor(hs[e % slots], gs[e % slots], hidden(e % slots)[:, blocks * CH:2 * blocks * CH],
                                        ALU.mult).then_inc(s.h, 1)

            def add(cc, e):
                m = cc * n + e
                wait(dve, s.y, m + 1)
                q = 0
                for j, share in enumerate(steps[e].shares):
                    for i in range(TPC):
                        b = cc * TPC + i
                        wide = len(steps[e].shares) * D
                        wait(dve, s.added, cc * sum(parts) + (before[e] + q + 1 - TPC))
                        nc.vector.scalar_tensor_tensor(at(k.x, b), bank[:, ybase + e % slots, i * wide + j * D:i * wide + j * D + D],
                                                       share(b), at(k.x, b), ALU.mult, ALU.add).then_inc(s.added, 1)
                        q += 1

            two_deep(dve, product, add, n)

        @block.gpsimd
        def _(pool):
            choose_experts(nc, s, k, n_gate, gate, None, pool)


def receptance_layer(nc, sems, k):
    s = Semaphores()
    (s.xh, s.xs, s.xT, s.xr, s.xk, s.kr, s.rk, s.ka, s.tt, s.kv, s.cleared, s.pk, s.sg, s.pr, s.added) = sems.new("f2", """
        xh xs xT xr xk kr rk ka tt kv cleared pk sg pr added""")
    c, cols, bank, w = k.c, k.cols, k.bank, k.work
    xh = split(w[:, 0:256], D)
    xs = w[:, 256:256 + 2 * 130].rearrange("p (s t) -> p s t", s=2)
    pr, pk, xr, xk, sg, kr, ka, tt = (split(w[:, 1024 + 256 * n:1280 + 256 * n], T) for n in range(8))
    sn = norm_names(sems, "f2_in")
    stats, dev, norm = layer_norm_steps(nc, k, sn, *norm_scratch(k.small, 0))
    tg = k.tg[:, 6:7]

    with nc.Block() as block:
        @block.tensor
        def _(pe):
            def in_T(b, sl):
                wait(pe, s.xh, b + 1)
                wait(pe, s.xs, b - 1)
                nc.tensor.transpose(bank[:, sl, 0:T], xh[:, sl, :], c["ident"]).then_inc(s.xT, 1)

            def project(b, sl):
                wait(pe, s.xr, b + 1)
                wait(pe, s.xk, b + 1)
                wait(pe, s.kr, b - 1)
                nc.tensor.matmul(bank[:, 2 + sl, 0:D], xr[:, sl, :], k.w["wr"], start=True, stop=True)
                nc.tensor.matmul(bank[:, 2 + sl, D:2 * D], k.w["wk"], xk[:, sl, :], start=True, stop=True).then_inc(s.rk, 1)

            def value(b, sl):
                wait(pe, s.ka, b + 1)
                wait(pe, s.tt, b - 1)
                nc.tensor.matmul(bank[:, 4 + sl, 0:D], ka[:, sl, :], k.w["wv"], start=True, stop=True).then_inc(s.kv, 1)

            walk(pe, [(project, 3), (value, 4), (in_T, 0)])

        @block.scalar
        def _(act):
            act.wait_ge(s.cleared, 1)

            def in_T(b, sl):
                wait(act, s.xT, b + 1)
                wait(act, s.xr, b - 1)
                wait(act, s.xk, b - 1)
                wait(act, s.pk, b - 1)
                nc.scalar.activation(xs[:, sl, 1:T + 1], bank[:, sl, 0:T], ACT.Copy).then_inc(s.xs, 1)

            def gates(b, sl):
                wait(act, s.rk, b + 1)
                wait(act, s.tt, b - 1)
                wait(act, s.ka, b - 1)
                nc.scalar.activation(sg[:, sl, :], bank[:, 2 + sl, 0:D], ACT.Sigmoid).then_inc(s.sg, 1)
                nc.scalar.activation(kr[:, sl, :], bank[:, 2 + sl, D:2 * D], ACT.Relu).then_inc(s.kr, 1)

            walk(act, [(in_T, 0), (gates, 2)])

        @block.gpsimd
        def _(pool):
            nc.gpsimd.memset(xs, 0.0).then_inc(s.cleared, 1)
            pool.wait_ge(s.cleared, 1)

            def dev_in(b, sl):
                dev(pool, sl, b + 1)

            def square(b, sl):
                wait(pool, s.kr, b + 1)
                wait(pool, s.kv, b - 1)
                nc.gpsimd.tensor_tensor(ka[:, sl, :], kr[:, sl, :], kr[:, sl, :], ALU.mult).then_inc(s.ka, 1)

            walk(pool, [(dev_in, 0), (square, 4)])

        @block.vector
        def _(dve):
            def stats_in(b, sl):
                stats(dve, at(k.x, b), sl, b + 1, s.xh)

            def norm_in(b, sl):
                wait(dve, s.xT, b - 1)
                norm(dve, xh[:, sl, :], at(k.x, b), sl, b + 1).then_inc(s.xh, 1)

            def previous(b, sl):
                wait(dve, s.xs, b + 1)
                wait(dve, s.xk, b - 1)
                nc.vector.tensor_scalar(pr[:, sl, :], xs[:, sl, 0:T], k.omu[:, 0:1], None, ALU.mult).then_inc(s.pr, 1)
                nc.vector.tensor_scalar(pk[:, sl, :], xs[:, sl, 0:T], k.omu[:, 1:2], None, ALU.mult).then_inc(s.pk, 1)

            def mix(b, sl):
                wait(dve, s.rk, b - 1)
                wait(dve, s.pr, b + 1)
                nc.vector.scalar_tensor_tensor(xr[:, sl, :], xs[:, sl, 1:T + 1], cols["mu_r"], pr[:, sl, :], ALU.mult,
                                               ALU.add).then_inc(s.xr, 1)
                wait(dve, s.pk, b + 1)
                nc.vector.scalar_tensor_tensor(xk[:, sl, :], xs[:, sl, 1:T + 1], cols["mu_k"], pk[:, sl, :], ALU.mult,
                                               ALU.add).then_inc(s.xk, 1)

            def gated(b, sl):
                wait(dve, s.kv, b + 1)
                wait(dve, s.sg, b + 1)
                wait(dve, s.added, b - 1)
                nc.vector.tensor_tensor(tt[:, sl, :], bank[:, 4 + sl, 0:D], sg[:, sl, :], ALU.mult).then_inc(s.tt, 1)

            def add(b, sl):
                wait(dve, s.tt, b + 1)
                wait(dve, s.xh, b + 1)
                nc.vector.scalar_tensor_tensor(at(k.x, b), tt[:, sl, :], tg, at(k.x, b), ALU.mult,
                                               ALU.add).then_inc(s.added, 1)

            walk(dve, [(stats_in, 0), (norm_in, 1), (previous, 2), (mix, 2), (gated, 5), (add, 6)])


def correlation_block(nc, sems, k, scratch_g, scratch_c):
    s = Semaphores()
    (s.xh, s.xhT, s.xT, s.ctxs, s.qk_out, s.v, s.qkv, s.g2, s.g, s.skew, s.mean, s.m, s.all_mean, s.eq,
     s.eqT, s.eqT_out, s.rank, s.cw, s.cwT, s.cwT_out, s.cr, s.pen, s.ex, s.biased, s.sent0, s.sent1,
     s.cr2, s.sent_c, s.circ, s.step) = sems.new("c3", """
        xh xhT xT ctxs qk_out v qkv g2 g skew mean m all_mean eq eqT eqT_out rank cw cwT cwT_out cr pen
        ex biased sent0 sent1 cr2 sent_c circ step""")
    c, cols, bank, w = k.c, k.cols, k.bank, k.work
    xh, xhT, qT, kT, ctxs = (split(w[:, 256 * n:256 * (n + 1)], 128) for n in range(5))
    g2 = w[:, 1280:1792].rearrange("p (s r t) -> p s r t", s=2, r=2)
    vtok = w[:, 2048:4096].rearrange("p (b d) -> p b d", b=B)
    skew = k.e[:, 0, :].rearrange("p (b t) -> p b t", b=B)
    circ = k.pT[:, :].rearrange("p (b t) -> p b t", b=B)
    r = w[0:B, 4096:8192]
    m, gm, gt, eq, sel, pen, ex, cw, tmp = (r[:, 128 * n:128 * (n + 1)] for n in range(9))
    cr2 = split(r[:, 1280:1536], T)
    top8, ngt, mxv, rs, ri = (r[:, 1536 + 8 * n:1544 + 8 * n] for n in range(5))
    eqT, cwT = w[:, 6144:6144 + B], w[:, 6160:6160 + B]
    sn = norm_names(sems, "c3_in")
    stats, dev, norm = layer_norm_steps(nc, k, sn, *norm_scratch(k.small, 0))

    with nc.Block() as block:
        @block.tensor
        def _(pe):
            def in_T(b, sl):
                wait(pe, s.xh, b + 1)
                wait(pe, s.xhT, b - 1)
                nc.tensor.transpose(bank[:, sl, 0:T], xh[:, sl, :], c["ident"]).then_inc(s.xT, 1)

            def project(b, sl):
                wait(pe, s.xhT, b + 1)
                wait(pe, s.ctxs, b + 1)
                wait(pe, s.qk_out, b - 1)
                wait(pe, s.v, b - 1)
                nc.tensor.matmul(bank[:, 2 + sl, 0:T], k.w["wq3"], xhT[:, sl, :], start=True, stop=True)
                nc.tensor.matmul(bank[:, 2 + sl, T:2 * T], k.w["wk3"], ctxs[:, sl, :], start=True, stop=True)
                nc.tensor.matmul(bank[:, 2 + sl, 256:384], ctxs[:, sl, :], k.w["wv3"], start=True, stop=True).then_inc(s.qkv, 1)

            def products(b, sl):
                wait(pe, s.qk_out, b + 1)
                wait(pe, s.g2, b - 1)
                nc.tensor.matmul(bank[:, 4 + sl, 0:T], kT[:, sl, :], qT[:, sl, :], start=True, stop=True).then_inc(s.g, 1)

            walk(pe, [(in_T, 0), (products, 2), (project, 0)])
            pe.wait_ge(s.skew, 16)
            for b in range(B):
                last = nc.tensor.matmul(bank[0:B, 6, 0:T], c["column"][:, B - 1 - b:2 * B - 1 - b], skew[:, b, :],
                                        start=b == 0, stop=b == B - 1)
            last.then_inc(s.mean, 1)
            pe.wait_ge(s.m, 1)
            nc.tensor.matmul(bank[0:B, 7, 0:T], c["mean"][0:B, :], m, start=True, stop=True).then_inc(s.all_mean, 1)
            pe.wait_ge(s.eq, 1)
            nc.tensor.transpose(bank[:, 7, 128:128 + B], eq, c["ident"][0:B, 0:B]).then_inc(s.eqT, 1)
            pe.wait_ge(s.eqT_out, 1)
            nc.tensor.matmul(bank[0:B, 7, 256:256 + T], eqT, c["earlier"], start=True, stop=True).then_inc(s.rank, 1)
            pe.wait_ge(s.cw, 1)
            nc.tensor.transpose(bank[:, 6, 128:128 + B], cw, c["ident"][0:B, 0:B]).then_inc(s.cwT, 1)
            pe.wait_ge(s.cwT_out, 1)
            nc.tensor.matmul(bank[0:B, 6, 256:256 + T], cwT, c["mirror"], start=True, stop=True).then_inc(s.cr, 1)

        @block.scalar
        def _(act):
            def in_T(b, sl):
                wait(act, s.xT, b + 1)
                wait(act, s.qkv, b - 1)
                nc.scalar.activation(xhT[:, sl, :], bank[:, sl, 0:T], ACT.Copy).then_inc(s.xhT, 1)

            def qk(b, sl):
                wait(act, s.qkv, b + 1)
                wait(act, s.g, b - 1)
                nc.scalar.activation(qT[:, sl, :], bank[:, 2 + sl, 0:T], ACT.Identity, bias=cols["b3q"])
                nc.scalar.activation(kT[:, sl, :], bank[:, 2 + sl, T:2 * T], ACT.Identity, bias=cols["b3k"]).then_inc(s.qk_out, 1)

            walk(act, [(qk, 2), (in_T, 0)])
            act.wait_ge(s.pen, 2)
            nc.scalar.activation(ex, tmp, ACT.Exp, accum_out=rs[:, 0:1]).then_inc(s.ex, 1)

        @block.gpsimd
        def _(pool):
            def dev_in(b, sl):
                dev(pool, sl, b + 1)
                wait_apart(pool, k, s.qkv, b - 1)
                nc.gpsimd.tensor_copy(ctxs[:, sl, :], at(k.ctxT, b)).then_inc(s.ctxs, 1)

            def bias(b, sl):
                wait_apart(pool, k, s.xh, b + 1)
                nc.gpsimd.tensor_tensor(at(k.x, b), at(k.x, b), k.tgb[:, 2, :], ALU.add).then_inc(s.biased, 1)

            walk(pool, [(dev_in, 0), (bias, 6)])

        @block.sync
        def _(sp):
            def send(b, sl):
                wait(sp, s.g2, b + 1)
                dst = scratch_g[b] if isinstance(b, int) else scratch_g[bass.ds(b, 1)].rearrange("o t n -> (o t) n")
                sp.dma_start(dst, g2[:, sl, :, :].rearrange("p r t -> p (r t)")).then_inc((s.sent0, s.sent1)[sl], 16)

            walk(sp, [(send, 0)])
            sp.wait_ge((s.sent0, s.sent1)[0], 16 * B // 2)
            sp.wait_ge((s.sent0, s.sent1)[1], 16 * B // 2)
            row = 2 * T
            sp.dma_start(skew, bass.AP(scratch_g.tensor, 0, [[row + 1, T], [T * row, B], [1, T]])).then_inc(s.skew, 16)
            sp.wait_ge(s.cr2, 1)
            sp.dma_start(scratch_c, cr2.rearrange("p r t -> p (r t)")).then_inc(s.sent_c, 16)
            sp.wait_ge(s.sent_c, 16)
            sp.dma_start(circ, bass.AP(scratch_c.tensor, 0, [[1, T], [row, B], [1, T]])).then_inc(s.circ, 16)
            sp.wait_ge(s.circ, 16)

        @block.vector
        def _(dve):
            def stats_in(b, sl):
                stats(dve, at(k.x, b), sl, b + 1, s.xh)

            def norm_in(b, sl):
                wait(dve, s.xT, b - 1)
                norm(dve, xh[:, sl, :], at(k.x, b), sl, b + 1).then_inc(s.xh, 1)

            def values(b, sl):
                wait(dve, s.qkv, b + 1)
                wait(dve, s.qk_out, b + 1)
                nc.vector.tensor_tensor(at(vtok, b), bank[:, 2 + sl, 256:384], k.rows["b3v"], ALU.add).then_inc(s.v, 1)

            def twice(b, sl):
                wait(dve, s.g, b + 1)
                wait(dve, (s.sent0, s.sent1)[sl], 8 * (b - sl))
                nc.vector.tensor_copy(g2[:, sl, :, :], over(bank[:, 4 + sl, 0:T], 2, 1)).then_inc(s.g2, 1)

            walk(dve, [(stats_in, 0), (norm_in, 1), (twice, 4), (values, 3)])
            v = nc.vector
            done = [0]

            def step(instruction):
                done[0] += 1
                instruction.then_inc(s.step, 1)
                dve.wait_ge(s.step, done[0])

            dve.wait_ge(s.mean, 1)
            v.tensor_copy(m, bank[0:B, 6, 0:T]).then_inc(s.m, 1)
            dve.wait_ge(s.all_mean, 1)
            step(v.tensor_copy(gm, bank[0:B, 7, 0:T]))
            step(v.max(top8, gm))
            fifth = top8[:, TOP_SHIFTS - 1:TOP_SHIFTS]
            v.tensor_scalar(eq, gm, fifth, None, ALU.is_equal).then_inc(s.eq, 1)
            step(v.tensor_scalar(gt, gm, fifth, None, ALU.is_gt))
            step(v.tensor_reduce(ngt[:, 0:1], gt, AX.X, ALU.add))
            dve.wait_ge(s.eqT, 1)
            v.tensor_copy(eqT, bank[:, 7, 128:128 + B]).then_inc(s.eqT_out, 1)
            dve.wait_ge(s.rank, 1)
            step(v.tensor_scalar(sel, bank[0:B, 7, 256:256 + T], ngt[:, 0:1], float(TOP_SHIFTS), ALU.add, ALU.is_lt))
            step(v.tensor_tensor(sel, sel, eq, ALU.mult))
            step(v.tensor_tensor(sel, sel, gt, ALU.add))
            step(v.tensor_scalar(pen, sel, -MASKED, MASKED, ALU.mult, ALU.add))
            dve.wait_ge(s.m, 1)
            step(v.tensor_tensor(tmp, m, pen, ALU.add))
            v.tensor_reduce(mxv[:, 0:1], tmp, AX.X, ALU.max).then_inc(s.pen, 1)
            dve.wait_ge(s.pen, 1)
            v.tensor_scalar(tmp, tmp, mxv[:, 0:1], None, ALU.subtract).then_inc(s.pen, 1)
            dve.wait_ge(s.ex, 1)
            step(v.reciprocal(ri[:, 0:1], rs[:, 0:1]))
            v.tensor_scalar(cw, ex, ri[:, 0:1], None, ALU.mult).then_inc(s.cw, 1)
            dve.wait_ge(s.cwT, 1)
            v.tensor_copy(cwT, bank[:, 6, 128:128 + B]).then_inc(s.cwT_out, 1)
            dve.wait_ge(s.cr, 1)
            v.tensor_copy(cr2, over(bank[0:B, 6, 256:256 + T], 2, 1)).then_inc(s.cr2, 1)


def roll_block(nc, sems, k):
    s = Semaphores()
    (s.xs2, s.kept, s.vs, s.vm, s.agg_out, s.agg, s.added, s.out, s.xh2, s.xT2, s.logits_out, s.logits) = sems.new("r3", """
        xs2 kept vs vm agg_out agg added out xh2 xT2 logits_out logits""")
    c, bank, w = k.c, k.bank, k.work
    vtok = w[:, 2048:4096].rearrange("p (b d) -> p b d", b=B)
    circ = k.pT[:, :].rearrange("p (b t) -> p b t", b=B)
    vs, agg, xh2, xs2 = (split(w[:, 256 * n:256 * (n + 1)], 128) for n in range(4))
    so = norm_names(sems, "r3_out")
    stats, dev, norm = layer_norm_steps(nc, k, so, *norm_scratch(k.small, 0))
    tg = k.tg[:, 3:4]

    with nc.Block() as block:
        @block.gpsimd
        def _(pool):
            def dev_out(b, sl):
                dev(pool, sl, b + 1)

            def keep(b, sl):
                wait_apart(pool, k, s.xs2, b + 1)
                nc.gpsimd.tensor_copy(at(k.xT, b), xs2[:, sl, :]).then_inc(s.kept, 1)

            walk(pool, [(keep, 3), (dev_out, 0)])

        @block.tensor
        def _(pe):
            def mirror(b, sl):
                wait(pe, s.vs, b)
                nc.tensor.matmul(bank[:, 7, 0:D], c["mirror"], at(vtok, b), start=True, stop=True).then_inc(s.vm, 1)

            def aggregate(b, sl):
                wait(pe, s.vs, b + 1)
                wait(pe, s.agg_out, b - 1)
                nc.tensor.matmul(bank[:, sl, 0:T], vs[:, sl, :], at(circ, b), start=True, stop=True).then_inc(s.agg, 1)

            def out(b, sl):
                wait(pe, s.agg_out, b + 1)
                wait(pe, s.added, b - 1)
                nc.tensor.matmul(bank[:, 2 + sl, 0:D], agg[:, sl, :], k.w["wo3"], start=True, stop=True).then_inc(s.out, 1)

            def next_T(b, sl):
                wait(pe, s.xh2, b + 1)
                wait(pe, s.xs2, b - 1)
                nc.tensor.transpose(bank[:, 4 + sl, 0:T], xh2[:, sl, :], c["ident"]).then_inc(s.xT2, 1)

            def logits(b, sl):
                wait(pe, s.xs2, b + 1)
                wait(pe, s.logits_out, b)
                nc.tensor.matmul(bank[:, 6, 0:E3], xs2[:, sl, :], k.w["wg3"], start=True, stop=True).then_inc(s.logits, 1)

            walk(pe, [(out, 2), (aggregate, 1), (mirror, 0), (logits, 6), (next_T, 5)])

        @block.scalar
        def _(act):
            def mirrored(b, sl):
                wait(act, s.vm, b + 1)
                wait(act, s.agg, b - 1)
                nc.scalar.activation(vs[:, sl, :], bank[:, 7, 0:D], ACT.Copy).then_inc(s.vs, 1)

            def aggregated(b, sl):
                wait(act, s.agg, b + 1)
                wait(act, s.out, b - 1)
                nc.scalar.activation(agg[:, sl, :], bank[:, sl, 0:T], ACT.Copy).then_inc(s.agg_out, 1)

            def next_T(b, sl):
                wait(act, s.xT2, b + 1)
                wait(act, s.kept, b - 1)
                wait(act, s.logits, b - 1)
                nc.scalar.activation(xs2[:, sl, :], bank[:, 4 + sl, 0:T], ACT.Copy).then_inc(s.xs2, 1)

            def logits(b, sl):
                wait_apart(act, k, s.logits, b + 1)
                nc.scalar.activation(at(k.logits, b)[:, 0:E3], bank[:, 6, 0:E3], ACT.Copy).then_inc(s.logits_out, 1)

            walk(act, [(mirrored, 0), (next_T, 5), (logits, 6), (aggregated, 0)])

        @block.vector
        def _(dve):
            def add(b, sl):
                wait(dve, s.out, b + 1)
                nc.vector.scalar_tensor_tensor(at(k.x, b), bank[:, 2 + sl, 0:D], tg, at(k.x, b), ALU.mult,
                                               ALU.add).then_inc(s.added, 1)

            def stats_out(b, sl):
                wait(dve, s.added, b + 1)
                stats(dve, at(k.x, b), sl, b + 1, s.xh2)

            def norm_out(b, sl):
                wait(dve, s.xT2, b - 1)
                norm(dve, xh2[:, sl, :], at(k.x, b), sl, b + 1).then_inc(s.xh2, 1)

            walk(dve, [(stats_out, 2), (norm_out, 3), (add, 0)])


def flamingo_layers(nc, a, out, until=8):
    ctx = ExitStack()
    with ctx:
        k = Core()
        set_up(nc, ctx, k, a)
        scratch_g = nc.dram_tensor("shifted_rows", [B, T, 2 * T], FP32, kind="Internal").ap()
        scratch_c = nc.dram_tensor("circulant_rows", [B, 2 * T], FP32, kind="Internal").ap()
        ld = Semaphores()
        ld.consts, ld.ctx, ld.x, ld.rows, ld.out = (ctx.enter_context(nc.semaphore(f"dma_{name}"))
                                                    for name in ("consts", "ctx", "x", "rows", "out"))
        k.passed = ctx.enter_context(nc.semaphore("passed"))
        ld.weights = [ctx.enter_context(nc.semaphore(f"dma_{name}")) for name, _ in a.weight_parts]
        with Sublayer(nc) as sems:
            load_block(nc, sems, k, a, ld)
        with Sublayer(nc) as sems:
            small_head_attention(nc, sems, k, "a0", None, True, False, k.w["w_proj"], k.tg[:, 0:1], k.tgb[:, 0, :],
                                 k.w["wg0"], E0, ld)
        weight = lambda e: lambda b: k.gate_w[:, b, e:e + 1] if isinstance(b, int) else \
            k.gate_w[:, bass.ds(b, 1), e:e + 1].rearrange("p o n -> p (o n)")
        w = k.w
        col = lambda name, n, m=128: w[name][:, n * m:(n + 1) * m]
        if until >= 2:
            steps = [Step([col("w1", 2 * e), col("w1", 2 * e + 1)], [col("w2", 2 * e), col("w2", 2 * e + 1)], None,
                          [col("w3", 2 * e), col("w3", 2 * e + 1)], [weight(e)]) for e in range(E0)]
            with Sublayer(nc) as sems:
                expert_layer(nc, sems, k, "f0", steps, 2, ACT.Silu, E0, k.tg[:, 4:5], (ld.weights[1], 16))
        if until >= 3:
            with Sublayer(nc) as sems:
                latent_attention(nc, sems, k, ld)
        if until >= 4:
            steps = [Step([col("gate1", p)], [col("up1", p)], None, [k.down1[:, p, :]], [weight(2 * p), weight(2 * p + 1)])
                     for p in range(E1 // 2)]
            steps.append(Step([w["sh_gate"]], [w["sh_up"]], None, [w["sh_down"]], [lambda b: k.tg[:, 5:6]]))
            with Sublayer(nc) as sems:
                expert_layer(nc, sems, k, "f1", steps, 3, ACT.Silu, E1, k.tg[:, 5:6], (ld.weights[3], 48))
        if until >= 5:
            with Sublayer(nc) as sems:
                small_head_attention(nc, sems, k, "a2", None, False, True, w["wo2"], k.tg[:, 2:3], k.tgb[:, 1, :],
                                     None, 0, ld)
        if until >= 6:
            with Sublayer(nc) as sems:
                receptance_layer(nc, sems, k)
        if until >= 7:
            with Sublayer(nc) as sems:
                correlation_block(nc, sems, k, scratch_g, scratch_c)
            with Sublayer(nc) as sems:
                roll_block(nc, sems, k)
        if until >= 8:
            steps = [Step([col("w1_3", 4 * e + i) for i in range(4)], [],
                          [k.cols["b1"][:, 4 * e + i:4 * e + i + 1] for i in range(4)],
                          [col("w2_3", 4 * e + i) for i in range(4)], [weight(e)]) for e in range(E3)]
            with Sublayer(nc) as sems:
                expert_layer(nc, sems, k, "f3", steps, 2, ACT.Gelu, E3, k.tg[:, 7:8], (ld.weights[5], 32), k.b2_3[:, :])
        with nc.Block() as block:
            @block.sync
            def _(sp):
                sp.dma_start(out.rearrange("b t d -> t b d"), k.x[:, :, :]).then_inc(ld.out, 16)
                sp.wait_ge(ld.out, 16)
                for n, count in ((0, 16), (1, 16), (2, 16), (3, 48), (4, 16), (5, 32)):
                    sp.wait_ge(ld.weights[n], count)


WEIGHT_PARTS = [("weights_a0", WEIGHTS0), ("weights_f0", WEIGHTS_F0), ("weights_a1", WEIGHTS_A1), ("weights_f1", WEIGHTS_F1),
                ("weights_2", WEIGHTS_2), ("weights_f3", WEIGHTS_F3)]


def cat(parts, arrays):
    assert [a.shape[1] for a in arrays] == [n for _, n in parts], ([a.shape for a in arrays], parts)
    return np.ascontiguousarray(np.concatenate(arrays, axis=1))


def shape_constants():
    d = np.arange(L1D)
    theta = np.arange(T, dtype=np.float32)[:, None] * (
        1.0 / np.float32(10000.0) ** (np.arange(0, L1D, 2, dtype=np.float32) / L1D))[None, :]
    angles = np.concatenate([theta, theta], axis=1).astype(np.float32).T
    cos = np.tile(np.cos(angles), (2, 1))
    sin = np.tile(np.sin(angles) * np.where(d < L1D // 2, -1.0, 1.0)[:, None], (2, 1))
    p, t = np.arange(128)[:, None], np.arange(128)[None, :]
    column = np.zeros((128, 2 * B - 1))
    column[:, B - 1] = 1.0 / 128
    consts = [np.eye(128), cos, sin, (p % 32) // DH == np.arange(HG)[None, :], p < t, (p + t) % 128 == 0, column,
              np.full((128, B), 1.0 / B), np.where(np.abs(p - t) > WINDOW, MASKED, 0.0), np.tile(np.arange(E0, 0, -1.0), (128, 1)), np.tile(np.arange(E1, 0, -1.0), (128, 1))]
    consts = cat(CONSTS, [np.asarray(x, np.float32) for x in consts])
    return consts


def kernel(**inputs):
    import concourse.bacc as _bacc
    from concourse.bass_utils import run_bass_kernel_spmd as _run

    i = {name: np.asarray(v) for name, v in inputs.items()}
    stack = lambda m: m.transpose(1, 0, 2).reshape(m.shape[1], -1)
    tall = lambda m: stack(m.reshape(-1, 128, m.shape[-1]))
    wkv = i["L1_xattn_Wkv"]
    wk, wv = wkv[:, :INNER], wkv[:, INNER:]
    rotated = (np.arange(INNER) // L1D) * L1D + (np.arange(INNER) + L1D // 2) % L1D
    w2_3 = i["L3_ffn_W2"].transpose(2, 0, 1).reshape(4, 128, E3, D).transpose(1, 2, 0, 3).reshape(128, -1)
    w3 = i["L0_ffn_W3"].reshape(E0, 2, 128, D).transpose(2, 0, 1, 3).reshape(128, -1)
    weights = [
        [i["L0_xattn_W_proj"].T, i["L0_ffn_Wg"]],
        [stack(i["L0_ffn_W1"]), stack(i["L0_ffn_W2"]), w3],
        [i["L1_xattn_Wq"], wk, wk[:, rotated], wv, tall(i["L1_xattn_Wo"]), i["L1_ffn_router_w"].T],
        [stack(i["L1_ffn_up_proj"]), stack(i["L1_ffn_gate_proj"]), i["L1_ffn_sh_gate"].T, i["L1_ffn_sh_up"].T,
         i["L1_ffn_sh_down"].T],
        [i["L2_xattn_W_q"].T, i["L2_xattn_W_k"].T, i["L2_xattn_W_v"].T, i["L2_xattn_W_out"].T, i["L2_ffn_W_r"].T,
         i["L2_ffn_W_k"].T, i["L2_ffn_W_v"].T, i["L3_xattn_Wq"], i["L3_xattn_Wk"], i["L3_xattn_Wv"], i["L3_xattn_Wo"],
         i["L3_ffn_Wr"].T],
        [i["L3_ffn_W1"].transpose(2, 0, 1).reshape(128, -1), w2_3],
    ]
    cols = [i[n].reshape(128, 1) for n in ("L1_xattn_gamma_x", "L1_xattn_beta_x", "L1_xattn_gamma_l", "L1_xattn_beta_l",
                                           "L2_xattn_b_q", "L2_xattn_b_k", "L2_ffn_mu_r", "L2_ffn_mu_k", "L3_xattn_bq",
                                           "L3_xattn_bk")]
    cols.append(i["L3_ffn_b1"].reshape(E3 * M3 // 128, 128).T)
    rows = [i["g_xattn"], i["g_ffn"], i["L1_ffn_router_bias"], i["L0_xattn_b_proj"], i["L2_xattn_b_v"], i["L2_xattn_b_out"],
            i["L3_xattn_bv"], i["L3_xattn_bo"]]
    consts = shape_constants()
    arrays = {"x": i["x"], "ctx": i["ctx_1024"], "rows": np.concatenate(rows), "cols": cat(COLS, cols), "consts": consts,
              "down": i["L1_ffn_down_proj"].reshape(E1 // 2, 2, H1, D).transpose(1, 0, 2, 3),
              "b2_3": i["L3_ffn_b2"]}
    for (name, parts), ws in zip(WEIGHT_PARTS, weights):
        arrays[name] = cat(parts, ws)
    arrays = {f"in_{n}": np.ascontiguousarray(v) for n, v in arrays.items()}

    nc = _bacc.Bacc("TRN2", target_bir_lowering=False, num_devices=1)
    dram = {name[3:]: nc.dram_tensor(name, v.shape, mybir.dt.from_np(v.dtype), kind="ExternalInput").ap()
            for name, v in arrays.items()}
    a = Core()
    a.x, a.ctx, a.rows, a.cols, a.consts, a.down, a.b2_3 = (
        dram[name] for name in ("x", "ctx", "rows", "cols", "consts", "down", "b2_3"))
    a.weight_parts, a.weight_tiles, a.weights = WEIGHT_PARTS, [], [dram[name] for name, _ in WEIGHT_PARTS]
    out = nc.dram_tensor("out_0", (B, T, D), FP32, kind="ExternalOutput").ap()
    flamingo_layers(nc, a, out)
    r = _run(nc, [arrays], core_ids=[0])
    return r.results[0]["out_0"]
```

```python
import concourse.bass as bass
from concourse import mybir
from contextlib import ExitStack
import numpy as np

FP32 = mybir.dt.float32
BF16 = mybir.dt.bfloat16
FP32R = mybir.dt.float32r
ALU = mybir.AluOpType
ACT = mybir.ActivationFunctionType
AX = mybir.AxisListType

B, T, D = 16, 128, 128
EPS = 1e-5
NH, DH = 16, 8
HG = 4
NG = NH // HG
L1H, L1D = 8, 64
L1P = L1H // 2
INNER = L1H * L1D
WINDOW = 64
MASKED = -1e30
E0, H0 = 8, 256
E1, H1 = 16, 64
E3, M3 = 8, 512
TOP_SHIFTS = 5
CH = 256
NC_ = B * T // CH
TPC = CH // T
DROP = -3e38
GATE_STEPS = 20

ROWS = [("gates", 8), ("router_bias", E1), ("b_proj", D), ("b_v", D), ("b_out", D), ("b3v", D), ("b3o", D)]
COLS = [("gamma_x", 1), ("beta_x", 1), ("gamma_l", 1), ("beta_l", 1), ("b_q", 1), ("b_k", 1), ("mu_r", 1),
        ("mu_k", 1), ("b3q", 1), ("b3k", 1), ("b1", E3 * M3 // 128)]
CONSTS = [("ident", 128), ("cos", T), ("sin", T), ("headmask", HG), ("earlier", T), ("mirror", T),
          ("column", 2 * B - 1), ("mean", B), ("window", T), ("countdown0", E0), ("countdown1", E1), ("owner", B)]
WEIGHTS0 = [("w_proj", D), ("wg0", E0)]
WEIGHTS_F0 = [("w1", E0 * H0), ("w2", E0 * H0), ("w3", E0 * 2 * D)]
WEIGHTS_A1 = [("wq1", INNER), ("wk1", INNER), ("wkrot1", INNER), ("wv1", INNER), ("wo1", L1P * D), ("wg1", E1)]
WEIGHTS_F1 = [("up1", E1 * H1), ("gate1", E1 * H1), ("sh_gate", D), ("sh_up", D), ("sh_down", D)]
WEIGHTS_2 = [("wq2", D), ("wk2", D), ("wv2", D), ("wo2", D), ("wr", D), ("wk", D), ("wv", D),
             ("wq3", D), ("wk3", D), ("wv3", D), ("wo3", D), ("wg3", E3)]
WEIGHTS_F3 = [("w1_3", E3 * M3), ("w2_3", E3 * 4 * D)]


def width(parts):
    return sum(n for _, n in parts)


def views(tile, parts):
    at, out = 0, {}
    for name, n in parts:
        out[name] = tile[:, at:at + n]
        at += n
    return out


def split(ap, b):
    return ap.rearrange("p (a b) -> p a b", b=b)


def over(ap, n, axis):
    p, a = ap.shape
    return ap.unsqueeze(axis).broadcast_to([p, n, a] if axis == 1 else [p, a, n])


def at(tile, b):
    if isinstance(b, int):
        return tile[:, b, :]
    return tile[:, bass.ds(b, 1), :].rearrange("p o n -> p (o n)")


def wait(eng, sem, value):
    if not isinstance(value, int) or value > 0:
        eng.wait_ge(sem, value)


def wait_apart(eng, k, sem, value):
    wait(eng, sem, value)
    if not isinstance(value, int):
        eng.sem_inc(k.passed, 1)


def walk(eng, stages):
    lags = [lag for _, lag in stages]
    lo, hi = max(lags) + 2, min(lags) + B
    pairs = (hi - lo) // 2

    def tick(t, parity):
        for stage, lag in stages:
            b = t - lag
            if not isinstance(b, int) or 0 <= b < B:
                stage(b, (parity + lag) % 2)

    for t in range(min(lags), lo):
        tick(t, t % 2)
    with eng.Fori(0, pairs) as i:
        for k in range(2):
            tick(i * 2 + (lo + k), (lo + k) % 2)
    for t in range(lo + 2 * pairs, max(lags) + B):
        tick(t, t % 2)


class Semaphores:
    pass


def norm_names(sems, prefix):
    s = Semaphores()
    s.raw_stats, s.stats, s.var_eps, s.rstd = sems.new(prefix, "raw_stats stats var_eps rstd")
    return s


class Sublayer:

    def __init__(self, nc, core):
        self.nc, self.core, self.held = nc, core, []

    def new(self, prefix, text):
        made = [self.nc.alloc_semaphore(f"{prefix}_{name}") for name in text.split()]
        self.held += made
        return made

    def __enter__(self):
        return self

    def __exit__(self, *_):
        for sem in self.core.used:
            self.nc.release_semaphore(sem)
        self.core.used = self.held

    def clear_last(self, sp):
        for sem in self.core.used:
            sp.sem_clear(sem)


class Core:
    pass


def set_up(nc, ctx, k, a):
    def sb(name, shape, dt=FP32):
        return ctx.enter_context(nc.sbuf_tensor(name, shape, dt))

    k.x = sb("x_tok", [T, B, D])
    k.ctx = sb("ctx_tok", [T, B, D])
    k.ctxT = sb("ctx_feat", [D, B, T])
    k.xT = sb("xhat_feat", [D, B, T])
    k.rows_t = sb("rows", [128, width(ROWS)])
    k.rows = views(k.rows_t, ROWS)
    k.cols_t = sb("cols", [128, width(COLS)])
    k.cols = views(k.cols_t, COLS)
    k.consts_t = sb("consts", [128, width(CONSTS)])
    k.c = views(k.consts_t, CONSTS)
    k.maskb = sb("mask_bias", [128, 128 + 4 * T], BF16)
    k.w = {}
    for name, parts in a.weight_parts:
        tile = sb(name, [128, width(parts)])
        a.weight_tiles.append(tile)
        k.w.update(views(tile, parts))
    k.down1 = sb("down_pairs", [128, E1 // 2, 2 * D])
    k.b2_3 = sb("b2_rows", [B * E3, D])
    k.tg = sb("tanh_gates", [128, 8])
    k.tgb = sb("gated_bias", [128, 3, D])
    k.omu = sb("one_minus_mu", [128, 2])
    k.half = sb("half_and_eps", [128, 2])
    k.logits = sb("logits", [128, B, E1])
    k.gate_t = sb("expert_weights", [128, B * E1])
    k.gate_w = lambda n: split(k.gate_t[:, 0:B * n], n)
    k.small = sb("small", [128, 1024])
    k.bank = ctx.enter_context(nc.psum_tensor("banks", [128, 8, 512], FP32))


def attention_scratch(nc, k, tag):
    scratch = ExitStack()
    k.e, k.pT, k.work, k.mid = (scratch.enter_context(nc.sbuf_tensor(f"{name}_{tag}", shape, FP32)) for name, shape in (
        ("exps", [128, 2, 2048]), ("probs_keymajor", [128, 2048]), ("work", [128, 8192]), ("mid", [128, 1280])))
    return scratch


def expert_scratch(nc, k, tag, gates, hidden, weights, b2):
    scratch = ExitStack()
    k.gates, k.hidden, k.wT, k.b2x, k.w_hi, k.w_lo, k.x_hi, k.x_lo = (
        scratch.enter_context(nc.sbuf_tensor(f"{name}_{tag}", [128, n], dt)) for name, n, dt in (
            ("gates", gates, FP32), ("hidden", hidden, FP32), ("expert_weights_t", T if b2 else 1, FP32),
            ("b2_columns", B * D if b2 else 1, FP32), ("up_high", weights, FP32R), ("up_low", weights, FP32R),
            ("stream_high", B * T, FP32R), ("stream_low", B * T, FP32R)))
    return scratch


def layer_norm_steps(nc, k, sem, st, mv, rstd):

    def statistics(dve, src, s, n, used):
        wait_apart(dve, k, used, n - 2)
        nc.vector.bn_stats(st[:, s, :], src).then_inc(sem.raw_stats, 1)
        wait_apart(dve, k, sem.raw_stats, n)
        nc.vector.bn_aggr(mv[:, s, :], st[:, s, :]).then_inc(sem.stats, 1)

    def deviation(pool, s, n):
        wait(pool, sem.stats, n)
        nc.gpsimd.tensor_tensor(rstd[:, s, 0:1], mv[:, s, 1:2], k.half[:, 1:2], ALU.add).then_inc(sem.var_eps, 1)
        wait(pool, sem.var_eps, n)
        nc.gpsimd.tensor_tensor(rstd[:, s, 1:2], rstd[:, s, 0:1], k.half[:, 0:1], ALU.pow).then_inc(sem.rstd, 1)

    def normalise(dve, dst, src, s, n):
        wait(dve, sem.rstd, n)
        return nc.vector.tensor_scalar(dst, src, mv[:, s, 0:1], rstd[:, s, 1:2], ALU.subtract, ALU.mult)

    return statistics, deviation, normalise


def norm_scratch(tile, at_):
    st = split(tile[:, at_:at_ + 12], 6)
    mv = split(tile[:, at_ + 12:at_ + 16], 2)
    rstd = split(tile[:, at_ + 16:at_ + 20], 2)
    return st, mv, rstd


def load_block(nc, sems, k, a, ld):
    s = Semaphores()
    (s.zeroed, s.tanh, s.transposed, s.ctxT, s.ready) = sems.new("load", """
        zeroed tanh transposed ctxT ready""")
    c, rows = k.c, k.rows

    with nc.Block() as block:
        @block.sync
        def _(sp):
            sp.dma_start(k.consts_t[:, :], a.consts).then_inc(ld.consts, 16)
            sp.dma_start(k.ctx[:, :, :], a.ctx.rearrange("b t d -> t b d")).then_inc(ld.ctx, 16)
            sp.dma_start(k.x[:, :, :], a.x.rearrange("b t d -> t b d")).then_inc(ld.x, 16)
            for n in (1, 4):
                sp.dma_start(a.weight_tiles[n][:, :], a.weights[n]).then_inc(ld.weights[n], 16)

        @block.scalar
        def _(act):
            act.dma_start(k.rows_t[:, :], a.rows.partition_broadcast(128)).then_inc(ld.rows, 16)
            act.dma_start(k.cols_t[:, :], a.cols).then_inc(ld.rows, 16)
            for n in (0, 2, 3, 5):
                act.dma_start(a.weight_tiles[n][:, :], a.weights[n]).then_inc(ld.weights[n], 16)
            act.dma_start(k.b2_3[:, :], a.b2_3).then_inc(ld.weights[5], 16)
            act.wait_ge(s.zeroed, 1)
            for half in range(2):
                act.dma_start(k.down1[64 * half:64 * half + 64, :, half * D:half * D + D],
                              a.down[half].rearrange("e h d -> h e d")).then_inc(ld.weights[3], 16)
            act.wait_ge(ld.rows, 32)
            nc.scalar.activation(k.tg[:, :], rows["gates"], ACT.Tanh).then_inc(s.tanh, 1)
            for g in range(4):
                act.wait_ge(s.transposed, g + 1)
                nc.scalar.activation(k.ctxT[:, 4 * g:4 * g + 4, :].rearrange("p a b -> p (a b)"),
                                     k.bank[:, g, :], ACT.Copy).then_inc(s.ctxT, 1)

        @block.tensor
        def _(pe):
            pe.wait_ge(ld.consts, 16)
            pe.wait_ge(ld.ctx, 16)
            pe.wait_ge(ld.rows, 32)
            for b in range(B):
                last = nc.tensor.transpose(k.bank[:, b // 4, (b % 4) * T:(b % 4 + 1) * T], k.ctx[:, b, :], c["ident"])
                if b % 4 == 3:
                    last.then_inc(s.transposed, 1)

        @block.gpsimd
        def _(pool):
            pool.wait_ge(ld.consts, 16)
            pool.wait_ge(ld.rows, 32)
            pool.wait_ge(ld.ctx, 16)
            pool.wait_ge(ld.x, 16)

        @block.vector
        def _(dve):
            nc.vector.memset(k.down1[:, :, :], 0.0).then_inc(s.zeroed, 1)
            nc.vector.memset(k.half[:, 0:1], -0.5).then_inc(s.zeroed, 1)
            nc.vector.memset(k.half[:, 1:2], EPS).then_inc(s.zeroed, 1)
            dve.wait_ge(s.tanh, 1)
            dve.wait_ge(ld.consts, 16)
            nc.vector.tensor_copy(k.maskb[:, 0:128], c["ident"]).then_inc(s.ready, 1)
            nc.vector.tensor_copy(split(k.maskb[:, 128:], T), over(c["window"], HG, 1)).then_inc(s.ready, 1)
            dve.wait_ge(ld.rows, 32)
            dve.wait_ge(ld.ctx, 16)
            dve.wait_ge(ld.x, 16)
            for n, (name, gate) in enumerate((("b_proj", 0), ("b_out", 2), ("b3o", 3))):
                nc.vector.tensor_scalar(k.tgb[:, n, :], rows[name], k.tg[:, gate:gate + 1], None,
                                        ALU.mult).then_inc(s.ready, 1)
            nc.vector.tensor_scalar(k.omu[:, :], k.cols_t[:, 6:8], -1.0, 1.0, ALU.mult, ALU.add).then_inc(s.ready, 1)


def small_head_attention(nc, sems, k, tag, src, masked, project, w_out, tg, tgb, w_gate, n_gate, ld):
    s = Semaphores()
    (s.q, s.keys, s.shifted, s.scores, s.ots, s.added, s.logits_out, s.xs2, s.otr, s.exp, s.pT, s.ptr,
     s.o, s.oTp, s.xh2, s.xT2, s.xh, s.kT, s.v, s.xTp, s.vpad, s.pv, s.oT, s.out, s.logits, s.xhT,
     s.ctxs, s.qkv, s.max, s.recip, s.biased, s.cleared, s.padded, s.kept) = sems.new(tag, """
        q keys shifted scores ots added logits_out xs2 otr exp pT ptr o oTp xh2 xT2 xh kT v xTp vpad pv
        oT out logits xhT ctxs qkv max recip biased cleared padded
        kept""")
    c, cols = k.c, k.cols
    bank = k.bank
    MA, MB, PT = 6, 7, 4
    w = k.work
    qz = w[:, 0:1024].rearrange("p (s g t) -> p s g t", s=2, g=NG)
    kx = w[:, 1024:2048].rearrange("p (s j t) -> p s j t", s=2, j=HG)
    vpad = w[:, 2048:3072].rearrange("p (s h c) -> p s h c", s=2, h=NH)
    xh = split(w[:, 3072:3328], D)
    xhT = split(w[:, 3328:3584], T)
    kT = split(w[:, 3584:3840], T)
    ctxs = split(w[:, 3840:4096], T)
    ots = w[:, 4096:4608]
    o = w[:, 4608:4736]
    oT = w[:, 4736:4864]
    xh2 = split(w[:, 4864:5120], D)
    xs2 = split(w[:, 5120:5376], T)
    vtok = w[:, 5376:5376 + B * D].rearrange("p (b d) -> p b d", b=B) if project else k.ctx
    mx = split(k.small[:, 0:2 * NH], NH)
    rc = k.small[:, 32:48]
    first = norm_scratch(k.small, 64)
    second = norm_scratch(k.small, 96)
    s1, s2 = norm_names(sems, tag + "_in"), norm_names(sems, tag + "_out")
    stats1, dev1, norm1 = layer_norm_steps(nc, k, s1, *first)
    stats2, dev2, norm2 = layer_norm_steps(nc, k, s2, *second)

    with nc.Block() as block:
        @block.sync
        def _(sp):
            sems.clear_last(sp)

        @block.tensor
        def _(pe):
            def scores(first):
                def stage(b, sl):
                    wait(pe, s.q, b + 1)
                    wait(pe, s.keys, b + 1)
                    wait(pe, s.shifted, b * 2 + (first // 2 - 1))
                    for g in range(first, first + 2):
                        if masked:
                            nc.tensor.matmul(bank[:, g, :], k.maskb[:, 0:128], k.maskb[:, 128:], start=True, stop=False)
                        last = nc.tensor.matmul(bank[:, g, :], qz[:, sl, g, :],
                                                kx[:, sl, :, :].rearrange("p j t -> p (j t)"),
                                                start=not masked, stop=True)
                    last.then_inc(s.scores, 1)
                return stage

            def output_transpose(b, sl):
                wait(pe, s.ots, b + 1)
                wait(pe, s.added, b)
                if w_gate is not None:
                    wait(pe, s.logits_out, b - 1)
                wait(pe, s.xs2, b - 1)
                for g in range(NG):
                    last = nc.tensor.transpose(bank[:, MB, g * 128:(g + 1) * 128], ots[:, g * 128:(g + 1) * 128],
                                               c["ident"])
                last.then_inc(s.otr, 1)

            def probs(first):
                def stage(b, sl):
                    wait(pe, s.exp, b + 1)
                    for g in range(first, first + 2):
                        wait(pe, s.pT, b * NG + (g - 1))
                        if g == 0:
                            wait(pe, s.ots, b)
                        for j in range(HG):
                            h = g * HG + j
                            last = nc.tensor.transpose(bank[:, PT + g % 2, j * T:(j + 1) * T],
                                                       k.e[:, sl, h * T:(h + 1) * T], c["ident"])
                        last.then_inc(s.ptr, 1)
                return stage

            def out_T(b, sl):
                wait(pe, s.o, b + 1)
                nc.tensor.transpose(bank[:, MB, 0:T], o, c["ident"]).then_inc(s.oTp, 1)

            def next_T(b, sl):
                wait(pe, s.xh2, b + 1)
                wait(pe, s.added, min(b + 2, B) if isinstance(b, int) else b + 2)
                if w_gate is not None:
                    wait(pe, s.logits_out, b)
                wait(pe, s.xs2, b)
                nc.tensor.transpose(bank[:, MB, 256:256 + T], xh2[:, sl, :], c["ident"]).then_inc(s.xT2, 1)

            def in_T(b, sl):
                wait(pe, s.xh, b + 1)
                wait(pe, s.q, b)
                if project:
                    wait(pe, s.kT, b)
                    wait(pe, s.v, b)
                nc.tensor.transpose(bank[:, MA, 0:T], xh[:, sl, :], c["ident"]).then_inc(s.xTp, 1)

            def pv(b, sl):
                wait(pe, s.pT, b * NG + NG)
                wait(pe, s.vpad, b + 1)
                for g in range(NG):
                    for j in range(HG):
                        h = g * HG + j
                        last = nc.tensor.matmul(bank[32 * j:32 * j + 32, PT, g * T:(g + 1) * T], vpad[:, sl, h, :],
                                                k.pT[:, h * T:(h + 1) * T], start=True, stop=True)
                last.then_inc(s.pv, 1)

            def out(b, sl):
                wait(pe, s.oT, b + 1)
                nc.tensor.matmul(bank[:, MB, 128:256], oT, w_out, start=True, stop=True).then_inc(s.out, 1)

            def logits(b, sl):
                wait(pe, s.xs2, b + 1)
                nc.tensor.matmul(bank[:, MB, 384:384 + n_gate], xs2[:, sl, :], w_gate,
                                 start=True, stop=True).then_inc(s.logits, 1)

            def qkv(b, sl):
                wait(pe, s.xhT, b + 1)
                wait(pe, s.ctxs, b + 1)
                nc.tensor.matmul(bank[:, MA, 128:256], k.w["wq2"], xhT[:, sl, :], start=True, stop=True)
                nc.tensor.matmul(bank[:, MA, 256:384], k.w["wk2"], ctxs[:, sl, :], start=True, stop=True)
                nc.tensor.matmul(bank[:, MA, 384:512], ctxs[:, sl, :], k.w["wv2"], start=True, stop=True).then_inc(s.qkv, 1)

            pe.wait_ge(ld.weights[4 if project else 0], 16)
            walk(pe, [(out_T, 5), (scores(0), 2), (qkv, 1), (out, 5), (pv, 4), (scores(2), 2), (next_T, 6),
                  (probs(0), 3), (output_transpose, 4), (probs(2), 3), (in_T, 0)]
                 if project else
                 [(scores(0), 1), (logits, 6), (probs(0), 3), (output_transpose, 4), (in_T, 0), (probs(2), 3),
                  (out_T, 4), (scores(2), 1), (out, 4), (pv, 3), (next_T, 5)])

        @block.vector
        def _(dve):
            nc.vector.memset(vpad, 0.0).then_inc(s.padded, 1)
            dve.wait_ge(s.padded, 1)
            nc.vector.memset(vpad[:, :, :, DH:DH + 1], 1.0).then_inc(s.padded, 1)

            def maximum(half):
                def stage(b, sl):
                    wait(dve, s.scores, b * 2 + (half + 1))
                    nc.vector.tensor_reduce(mx[:, sl, 8 * half:8 * half + 8],
                                            bank[:, 2 * half:2 * half + 2, :].rearrange("p g (j t) -> p (g j) t", j=HG),
                                            AX.X, ALU.max).then_inc(s.max, 1)
                return stage

            def shift(half):
                def stage(b, sl):
                    wait(dve, s.max, b * 2 + (half + 1))
                    wait(dve, s.ptr, b * NG - NG)
                    nc.vector.tensor_tensor(split(k.e[:, sl, 1024 * half:1024 * half + 1024], T),
                                            bank[:, 2 * half:2 * half + 2, :].rearrange("p g (j t) -> p (g j) t", j=HG),
                                            over(mx[:, sl, 8 * half:8 * half + 8], T, 2), ALU.subtract).then_inc(s.shifted, 1)
                return stage

            def divide(b, sl):
                wait(dve, s.otr, b + 1)
                heads = split(bank[:, MB, :], 32)
                nc.vector.reciprocal(rc, heads[:, :, DH:DH + 1].rearrange("p h o -> p (h o)")).then_inc(s.recip, 1)
                wait(dve, s.recip, b + 1)
                wait(dve, s.oTp, b)
                nc.vector.tensor_tensor(split(o, DH), heads[:, :, 0:DH], over(rc, DH, 2), ALU.mult).then_inc(s.o, 1)

            def add(b, sl):
                wait(dve, s.out, b + 1)
                wait(dve, s.biased, b + 1)
                nc.vector.scalar_tensor_tensor(at(k.x, b), bank[:, MB, 128:256], tg, at(k.x, b), ALU.mult,
                                               ALU.add).then_inc(s.added, 1)

            def stats_in(b, sl):
                stats1(dve, at(k.x, b), sl, b + 1, s.xh)

            def norm_in(b, sl):
                wait(dve, s.xTp, b - 1)
                norm1(dve, xh[:, sl, :], at(k.x, b), sl, b + 1).then_inc(s.xh, 1)

            def stats_out(b, sl):
                wait(dve, s.added, b + 1)
                stats2(dve, at(k.x, b), sl, b + 1, s.xh2)

            def norm_out(b, sl):
                wait(dve, s.xT2, b - 1)
                norm2(dve, xh2[:, sl, :], at(k.x, b), sl, b + 1).then_inc(s.xh2, 1)

            def values(b, sl):
                wait(dve, s.qkv, b + 1)
                wait(dve, s.q, b + 1)
                nc.vector.tensor_tensor(at(vtok, b), bank[:, MA, 384:512], k.rows["b_v"], ALU.add).then_inc(s.v, 1)

            walk(dve, [(shift(1), 4), (norm_in, 1), (stats_in, 0), (maximum(0), 3), (add, 6), (shift(0), 3),
                  (values, 2), (stats_out, 6), (maximum(1), 3), (norm_out, 6), (divide, 5)]
                 if project else
                 [(shift(0), 3), (add, 6), (stats_out, 6), (maximum(1), 3), (stats_in, 0), (shift(1), 3),
                  (divide, 5), (norm_out, 6), (maximum(0), 2), (norm_in, 0)])

        @block.gpsimd
        def _(pool):
            nc.gpsimd.memset(qz, 0.0).then_inc(s.cleared, 1)
            pool.wait_ge(s.padded, 2)

            def dev_in(b, sl):
                dev1(pool, sl, b + 1)
                if project:
                    wait_apart(pool, k, s.qkv, b - 1)
                    nc.gpsimd.tensor_copy(ctxs[:, sl, :], at(k.ctxT, b)).then_inc(s.ctxs, 1)

            def bias(b, sl):
                wait_apart(pool, k, s.xh, b + 1)
                nc.gpsimd.tensor_tensor(at(k.x, b), at(k.x, b), tgb, ALU.add).then_inc(s.biased, 1)

            def dev_out(b, sl):
                dev2(pool, sl, b + 1)

            def spread_keys(b, sl):
                if project:
                    wait(pool, s.kT, b + 1)
                wait_apart(pool, k, s.scores, b * 2 - 2)
                keys = kT[:, sl, :] if project else at(k.ctxT, b)
                nc.gpsimd.tensor_tensor(kx[:, sl, :, :], over(keys, HG, 1), over(c["headmask"], T, 2),
                                        ALU.mult).then_inc(s.keys, 1)

            def spread_values(b, sl):
                if project:
                    wait(pool, s.v, b + 1)
                wait_apart(pool, k, s.pv, b - 1)
                nc.gpsimd.tensor_copy(vpad[:, sl, :, 0:DH], split(at(vtok, b), DH)).then_inc(s.vpad, 1)

            def keep(b, sl):
                wait_apart(pool, k, s.xs2, b + 1)
                nc.gpsimd.tensor_copy(at(k.xT, b), xs2[:, sl, :]).then_inc(s.kept, 1)

            walk(pool, [(dev_in, 0), (spread_values, 3), (dev_out, 5), (spread_keys, 1), (bias, 4), (keep, 6)]
                 if project else
                 [(dev_in, 0), (spread_keys, 0), (dev_out, 5), (keep, 6), (bias, 0), (spread_values, 3)])

        @block.scalar
        def _(act):
            act.wait_ge(s.cleared, 1)

            def exps(b, sl):
                wait(act, s.shifted, b * 2 + 2)
                nc.scalar.activation(k.e[:, sl, :], k.e[:, sl, :], ACT.Exp, scale=float(1 / np.sqrt(DH))).then_inc(s.exp, 1)

            def probs_out(b, sl):
                for g in range(NG):
                    wait(act, s.ptr, b * NG + (g + 1))
                    if g == 0:
                        wait(act, s.pv, b)
                    nc.scalar.activation(k.pT[:, g * 512:(g + 1) * 512], bank[:, PT + g % 2, :], ACT.Copy).then_inc(s.pT, 1)

            def out_T(b, sl):
                wait(act, s.oTp, b + 1)
                wait(act, s.out, b)
                nc.scalar.activation(oT, bank[:, MB, 0:T], ACT.Copy).then_inc(s.oT, 1)

            def next_T(b, sl):
                wait(act, s.xT2, b + 1)
                wait(act, s.kept, b - 1)
                if w_gate is not None:
                    wait(act, s.logits, b - 1)
                nc.scalar.activation(xs2[:, sl, :], bank[:, MB, 256:256 + T], ACT.Copy).then_inc(s.xs2, 1)

            def in_T(b, sl):
                wait(act, s.xTp, b + 1)
                wait(act, s.qkv, b - 1)
                nc.scalar.activation(xhT[:, sl, :], bank[:, MA, 0:T], ACT.Copy).then_inc(s.xhT, 1)

            def queries(b, sl):
                if project:
                    wait(act, s.qkv, b + 1)
                    wait(act, s.keys, b - 1)
                    nc.scalar.activation(kT[:, sl, :], bank[:, MA, 256:384], ACT.Identity,
                                         bias=cols["b_k"]).then_inc(s.kT, 1)
                else:
                    wait(act, s.xTp, b + 1)
                wait(act, s.scores, b * 2 - 2)
                for g in range(NG):
                    p = slice(32 * g, 32 * g + 32)
                    if project:
                        last = nc.scalar.activation(qz[p, sl, g, :], bank[p, MA, 128:256], ACT.Identity,
                                                    bias=cols["b_q"][p, :])
                    else:
                        last = nc.scalar.activation(qz[p, sl, g, :], bank[p, MA, 0:T], ACT.Copy)
                last.then_inc(s.q, 1)

            def outputs(b, sl):
                wait(act, s.pv, b + 1)
                wait(act, s.otr, b)
                nc.scalar.activation(ots, bank[:, PT, :], ACT.Copy).then_inc(s.ots, 1)

            def logits(b, sl):
                wait_apart(act, k, s.logits, b + 1)
                nc.scalar.activation(at(k.logits, b)[:, 0:n_gate], bank[:, MB, 384:384 + n_gate],
                                     ACT.Copy).then_inc(s.logits_out, 1)

            walk(act, [(queries, 1), (outputs, 4), (next_T, 6), (probs_out, 3), (in_T, 0), (out_T, 4), (exps, 2)]
                 if project else
                 [(outputs, 4), (logits, 6), (probs_out, 3), (queries, 0), (out_T, 4), (exps, 2), (next_T, 5)])



def latent_attention(nc, sems, k, ld):
    s = Semaphores()
    (s.ch, s.lh, s.v, s.inT, s.q, s.k_ctx, s.k_lat, s.exp, s.scores, s.k1, s.kvT, s.k2, s.t1, s.k3, s.t2,
     s.q1, s.v1, s.norm, s.pT, s.oT, s.ptr, s.pv, s.added, s.logits_out, s.out, s.xh2, s.xs2, s.xT2,
     s.logits, s.inv, s.max, s.nmax, s.xh, s.cleared, s.kept) = sems.new("a1", """
        ch lh v inT q k_ctx k_lat exp scores k1 kvT k2 t1 k3 t2 q1 v1 norm pT oT ptr pv added logits_out
        out xh2 xs2 xT2 logits inv max nmax xh cleared kept""")
    c, cols, bank, w = k.c, k.cols, k.bank, k.work
    MA, MB, PT = 6, 7, 4
    qm = w[:, 0:2048].rearrange("p (s h t) -> p s h t", s=2, h=L1H)
    kT = w[:, 2048:4096].rearrange("p (s h t) -> p s h t", s=2, h=L1P)
    v = w[:, 4096:6144].rearrange("p (s i n) -> p s i n", s=2, i=2)
    kvT = w[:, 6144:6656].rearrange("p (s t) -> p s t", s=2)
    t1, t2 = w[:, 6656:7168], w[:, 7168:7680]
    oT = w[:, 7680:8192]
    m = k.mid
    ch, xh, lh, xh2, xs2 = (split(m[:, n * 256:(n + 1) * 256], 128) for n in range(5))
    mx = split(k.small[:, 0:16], L1H)
    nmx = split(k.small[:, 16:32], L1H)
    sums = split(k.small[:, 32:48], L1H)
    inv = split(k.small[:, 48:64], L1H)
    sc, sx, sl2, so = (norm_names(sems, "a1_" + n) for n in ("ctx", "x", "lat", "out"))
    stats_c, dev_c, norm_c = layer_norm_steps(nc, k, sc, *norm_scratch(k.small, 64))
    stats_x, dev_x, norm_x = layer_norm_steps(nc, k, sx, *norm_scratch(k.small, 96))
    stats_l, dev_l, norm_l = layer_norm_steps(nc, k, sl2, *norm_scratch(k.small, 128))
    stats_o, dev_o, norm_o = layer_norm_steps(nc, k, so, *norm_scratch(k.small, 160))
    tg = k.tg[:, 1:2]
    SCALE = L1D ** -0.5

    with nc.Block() as block:
        @block.sync
        def _(sp):
            sems.clear_last(sp)

        @block.tensor
        def _(pe):
            def in_T(b, sl):
                wait(pe, s.ch, b + 1)
                wait(pe, s.lh, b + 1)
                wait(pe, s.v, 2 * b)
                nc.tensor.transpose(bank[:, MA, 0:T], ch[:, sl, :], c["ident"])
                nc.tensor.transpose(bank[:, MA, T:2 * T], lh[:, sl, :], c["ident"]).then_inc(s.inT, 1)

            def scores(half):
                def stage(b, sl):
                    wait(pe, s.q, b + 1)
                    wait(pe, s.k_ctx, b + 1)
                    wait(pe, s.k_lat, b + 1)
                    wait(pe, s.exp, L1H * b - (L1H // 2 if half == 0 else 0))
                    for h in range(4 * half, 4 * half + 4):
                        last = nc.tensor.matmul(bank[:, h // 2, (h % 2) * 256:(h % 2) * 256 + 256], qm[:, sl, h, :],
                                                kT[:, sl, h // 2, :], start=True, stop=True)
                    last.then_inc(s.scores, 1)
                return stage

            def project(weight, part, done, gate):
                def stage(b, sl):
                    gate(b)
                    for p in range(L1P):
                        last = nc.tensor.matmul(bank[:, MA, p * T:(p + 1) * T], k.w[weight][:, p * 128:(p + 1) * 128],
                                                kvT[:, sl, part * T:(part + 1) * T], start=True, stop=True)
                    last.then_inc(done, 1)
                return stage

            k_ctx = project("wk1", 0, s.k1, lambda b: wait(pe, s.kvT, b + 1))
            k_rot = project("wkrot1", 0, s.k2, lambda b: wait(pe, s.t1, b + 1))
            k_lat = project("wk1", 1, s.k3, lambda b: wait(pe, s.t2, b + 1))
            query = project("wq1", 1, s.q1, lambda b: wait(pe, s.k_lat, b + 1))

            def values(i):
                def stage(b, sl):
                    wait(pe, s.q, b + 1) if i == 0 else wait(pe, s.v, 2 * b + 1)
                    nc.tensor.matmul(bank[:, MA, :], kvT[:, sl, i * T:(i + 1) * T], k.w["wv1"], start=True,
                                     stop=True).then_inc(s.v1, 1)
                return stage

            def probs(g0):
                def stage(b, sl):
                    for g in range(g0, g0 + 2):
                        wait(pe, s.norm, b * L1H + 2 * g + 2)
                        wait(pe, s.pT, b * 4 + (g - 1))
                        if g == 0:
                            wait(pe, s.oT, b)
                        for j in range(4):
                            n = g * 4 + j
                            last = nc.tensor.transpose(bank[:, PT + g % 2, j * T:(j + 1) * T],
                                                       k.e[:, sl, n * T:(n + 1) * T], c["ident"])
                        last.then_inc(s.ptr, 1)
                return stage

            def pv(b, sl):
                wait(pe, s.pT, b * 4 + 4)
                wait(pe, s.v, 2 * b + 2)
                for p in range(L1P):
                    for i in range(2):
                        for par in range(2):
                            h = 2 * p + par
                            last = nc.tensor.matmul(bank[64 * par:64 * par + 64, PT, p * T:(p + 1) * T],
                                                    v[:, sl, i, h * L1D:(h + 1) * L1D],
                                                    k.pT[:, (2 * h + i) * T:(2 * h + i + 1) * T], start=i == 0, stop=i == 1)
                last.then_inc(s.pv, 1)

            def out(b, sl):
                wait(pe, s.oT, b + 1)
                wait(pe, s.added, b)
                wait(pe, s.logits_out, b - 1)
                for p in range(L1P):
                    last = nc.tensor.matmul(bank[:, MB, 0:D], oT[:, p * 128:(p + 1) * 128],
                                            k.w["wo1"][:, p * D:(p + 1) * D], start=p == 0, stop=p == L1P - 1)
                last.then_inc(s.out, 1)

            def next_T(b, sl):
                wait(pe, s.xh2, b + 1)
                wait(pe, s.added, min(b + 2, B) if isinstance(b, int) else b + 2)
                wait(pe, s.logits_out, b)
                wait(pe, s.xs2, b)
                nc.tensor.transpose(bank[:, MB, 128:256], xh2[:, sl, :], c["ident"]).then_inc(s.xT2, 1)

            def logits(b, sl):
                wait(pe, s.xs2, b + 1)
                wait(pe, s.logits_out, b)
                nc.tensor.matmul(bank[:, MB, 256:256 + E1], xs2[:, sl, :], k.w["wg1"], start=True,
                                 stop=True).then_inc(s.logits, 1)

            pe.wait_ge(ld.weights[2], 16)
            walk(pe, [(k_rot, 1), (probs(2), 3), (k_lat, 1), (next_T, 5), (query, 1), (pv, 3), (values(0), 1),
                      (logits, 5), (scores(0), 1), (values(1), 1), (scores(1), 1), (in_T, 0), (out, 3), (k_ctx, 0),
                      (probs(0), 2)])

        @block.vector
        def _(dve):
            def normalise(b, sl):
                wait(dve, s.exp, L1H * b + L1H)
                nc.vector.reciprocal(inv[:, sl, :], sums[:, sl, :]).then_inc(s.inv, 1)
                wait(dve, s.inv, b + 1)
                for h in range(L1H):
                    part = k.e[:, sl, h * 256:(h + 1) * 256]
                    nc.vector.tensor_scalar(part, part, inv[:, sl, h:h + 1], None, ALU.mult).then_inc(s.norm, 1)

            def rope_cos(b, sl):
                wait(dve, s.k1, b + 1)
                wait(dve, s.k_ctx, b)
                nc.vector.tensor_tensor(split(t1, T), split(bank[:, MA, :], T), over(c["cos"], L1P, 1),
                                        ALU.mult).then_inc(s.t1, 1)

            def rope_sin(b, sl):
                wait(dve, s.k2, b + 1)
                nc.vector.tensor_tensor(split(t2, T), split(bank[:, MA, :], T), over(c["sin"], L1P, 1),
                                        ALU.mult).then_inc(s.t2, 1)

            def maximum(b, sl):
                wait(dve, s.scores, 2 * b + 2)
                wait(dve, s.exp, L1H * (b - 1))
                nc.vector.tensor_reduce(mx[:, sl, :], bank[:, 0:4, :].rearrange("p g (j t) -> p (g j) t", j=2), AX.X,
                                        ALU.max).then_inc(s.max, 1)
                wait(dve, s.max, b + 1)
                nc.vector.tensor_scalar(nmx[:, sl, :], mx[:, sl, :], -SCALE, None, ALU.mult).then_inc(s.nmax, 1)

            def values(b, sl):
                wait(dve, s.v1, 2 * b + 1)
                wait(dve, s.pv, b - 1)
                nc.vector.tensor_copy(v[:, sl, 0, :], bank[:, MA, :]).then_inc(s.v, 1)

            def add(b, sl):
                wait(dve, s.out, b + 1)
                wait(dve, s.xh, b + 1)
                nc.vector.scalar_tensor_tensor(at(k.x, b), bank[:, MB, 0:D], tg, at(k.x, b), ALU.mult,
                                               ALU.add).then_inc(s.added, 1)

            def stats_in(b, sl):
                stats_x(dve, at(k.x, b), sl, b + 1, s.xh)
                stats_c(dve, at(k.ctx, b), sl, b + 1, s.ch)

            def norm_in(b, sl):
                wait(dve, s.lh, b - 1)
                norm_x(dve, xh[:, sl, :], at(k.x, b), sl, b + 1).then_inc(s.xh, 1)
                wait(dve, s.inT, b - 1)
                norm_c(dve, ch[:, sl, :], at(k.ctx, b), sl, b + 1).then_inc(s.ch, 1)
                wait(dve, s.xh, b + 1)
                stats_l(dve, xh[:, sl, :], sl, b + 1, s.lh)

            def norm_latent(b, sl):
                wait(dve, s.inT, b - 1)
                norm_l(dve, lh[:, sl, :], xh[:, sl, :], sl, b + 1).then_inc(s.lh, 1)

            def stats_out(b, sl):
                wait(dve, s.added, b + 1)
                stats_o(dve, at(k.x, b), sl, b + 1, s.xh2)

            def norm_out(b, sl):
                wait(dve, s.xT2, b - 1)
                norm_o(dve, xh2[:, sl, :], at(k.x, b), sl, b + 1).then_inc(s.xh2, 1)

            def logits(b, sl):
                wait(dve, s.logits, b + 1)
                nc.vector.tensor_tensor(at(k.logits, b)[:, 0:E1], bank[:, MB, 256:256 + E1], k.rows["router_bias"],
                                        ALU.add).then_inc(s.logits_out, 1)

            walk(dve, [(norm_out, 6), (rope_sin, 2), (add, 5), (maximum, 3), (norm_in, 1), (stats_out, 5),
                       (values, 2), (logits, 6), (norm_latent, 1), (normalise, 3), (stats_in, 0), (rope_cos, 1)])

        @block.gpsimd
        def _(pool):
            nc.gpsimd.memset(qm, 0.0).then_inc(s.cleared, 1)

            def dev_in(b, sl):
                dev_x(pool, sl, b + 1)
                dev_c(pool, sl, b + 1)

            def dev_latent(b, sl):
                dev_l(pool, sl, b + 1)

            def dev_out(b, sl):
                dev_o(pool, sl, b + 1)

            def rope_add(b, sl):
                wait(pool, s.t1, b + 1)
                wait(pool, s.t2, b + 1)
                wait(pool, s.scores, 2 * (b - 1))
                nc.gpsimd.tensor_tensor(kT[:, sl, :, 0:T], split(t1, T), split(t2, T), ALU.add).then_inc(s.k_ctx, 1)

            def keep(b, sl):
                wait_apart(pool, k, s.xs2, b + 1)
                nc.gpsimd.tensor_copy(at(k.xT, b), xs2[:, sl, :]).then_inc(s.kept, 1)

            walk(pool, [(rope_add, 1), (keep, 6), (dev_in, 0), (dev_out, 4), (dev_latent, 0)])

        @block.scalar
        def _(act):
            act.wait_ge(s.cleared, 1)

            def in_T(b, sl):
                wait(act, s.inT, b + 1)
                wait(act, s.v1, 2 * (b - 1))
                for i, (gamma, beta) in enumerate((("gamma_x", "beta_x"), ("gamma_l", "beta_l"))):
                    last = nc.scalar.activation(kvT[:, sl, i * T:(i + 1) * T], bank[:, MA, i * T:(i + 1) * T], ACT.Identity,
                                                scale=cols[gamma], bias=cols[beta])
                last.then_inc(s.kvT, 1)

            def probs(g0):
                def stage(b, sl):
                    for g in range(g0, g0 + 2):
                        wait(act, s.ptr, b * 4 + (g + 1))
                        if g == 0:
                            wait(act, s.pv, b)
                        nc.scalar.activation(k.pT[:, g * 512:(g + 1) * 512], bank[:, PT + g % 2, :],
                                             ACT.Copy).then_inc(s.pT, 1)
                return stage

            def k_lat(b, sl):
                wait(act, s.k3, b + 1)
                wait(act, s.scores, 2 * (b - 1))
                nc.scalar.activation(kT[:, sl, :, T:2 * T], split(bank[:, MA, :], T), ACT.Copy).then_inc(s.k_lat, 1)

            def query(b, sl):
                wait(act, s.q1, b + 1)
                wait(act, s.scores, 2 * (b - 1))
                for par in range(2):
                    p = slice(64 * par, 64 * par + 64)
                    last = nc.scalar.activation(qm[p, sl, par::2, :], split(bank[p, MA, :], T), ACT.Copy)
                last.then_inc(s.q, 1)

            def exps(b, sl):
                wait(act, s.nmax, b + 1)
                wait(act, s.ptr, 4 * (b - 1))
                wait(act, s.inv, b - 1)
                for h in range(L1H):
                    nc.scalar.activation(k.e[:, sl, h * 256:(h + 1) * 256],
                                         bank[:, h // 2, (h % 2) * 256:(h % 2) * 256 + 256], ACT.Exp,
                                         bias=nmx[:, sl, h:h + 1], scale=SCALE,
                                         accum_out=sums[:, sl, h:h + 1]).then_inc(s.exp, 1)

            def next_T(b, sl):
                wait(act, s.xT2, b + 1)
                wait(act, s.kept, b - 1)
                wait(act, s.logits, b - 1)
                nc.scalar.activation(xs2[:, sl, :], bank[:, MB, 128:256], ACT.Copy).then_inc(s.xs2, 1)

            def outputs(b, sl):
                wait(act, s.pv, b + 1)
                wait(act, s.out, b)
                nc.scalar.activation(oT, bank[:, PT, :], ACT.Copy).then_inc(s.oT, 1)

            def values(b, sl):
                wait(act, s.v1, 2 * b + 2)
                wait(act, s.pv, b - 1)
                nc.scalar.activation(v[:, sl, 1, :], bank[:, MA, :], ACT.Copy).then_inc(s.v, 1)

            walk(act, [(exps, 2), (outputs, 3), (values, 1), (in_T, 0), (probs(0), 2), (probs(2), 2), (k_lat, 0),
                       (next_T, 4), (query, 0)])


def choose_experts(nc, s, k, n, gate, dve, act):
    lg = k.logits[:, :, 0:n]
    wt = k.gate_w(n)
    sc = k.small
    eq1, eq2, lg2 = (sc[:, i * B * n:(i + 1) * B * n].rearrange("p (b e) -> p b e", e=n) for i in range(3))
    col = lambda i: sc[:, 768 + B * i:768 + B * i + B]
    m1, m2, r1, r2, d, ex, den, w1, w2 = (col(i) for i in range(9))
    count = k.c["countdown0" if n == E0 else "countdown1"].unsqueeze(1).broadcast_to([128, B, n])
    if act is not None:
        act.wait_ge(s.gate_step, 13)
        nc.scalar.activation(ex, d, ACT.Exp).then_inc(s.gate_exp, 1)
        return
    done = [0]

    def step(instruction):
        done[0] += 1
        instruction.then_inc(s.gate_step, 1)
        dve.wait_ge(s.gate_step, done[0])

    v = nc.vector
    step(v.tensor_reduce(m1, lg, AX.X, ALU.max))
    step(v.tensor_tensor(eq1, lg, over(m1, n, 2), ALU.is_equal))
    step(v.tensor_tensor(eq1, eq1, count, ALU.mult))
    step(v.tensor_reduce(r1, eq1, AX.X, ALU.max))
    step(v.tensor_tensor(eq1, eq1, over(r1, n, 2), ALU.is_equal))
    step(v.scalar_tensor_tensor(lg2, eq1, DROP, lg, ALU.mult, ALU.add))
    step(v.tensor_reduce(m2, lg2, AX.X, ALU.max))
    step(v.tensor_tensor(eq2, lg2, over(m2, n, 2), ALU.is_equal))
    step(v.tensor_tensor(eq2, eq2, count, ALU.mult))
    step(v.tensor_reduce(r2, eq2, AX.X, ALU.max))
    step(v.tensor_tensor(eq2, eq2, over(r2, n, 2), ALU.is_equal))
    step(v.tensor_tensor(d, m2, m1, ALU.subtract))
    step(v.tensor_scalar(d, d, -100.0, None, ALU.max))
    dve.wait_ge(s.gate_exp, 1)
    step(v.tensor_scalar(den, ex, 1.0, None, ALU.add))
    step(v.reciprocal(den, den))
    step(v.tensor_scalar(w1, den, gate, None, ALU.mult))
    step(v.tensor_tensor(w2, ex, w1, ALU.mult))
    step(v.tensor_tensor(wt, eq1, over(w1, n, 2), ALU.mult))
    step(v.tensor_tensor(eq2, eq2, over(w2, n, 2), ALU.mult))
    step(v.tensor_tensor(wt, wt, eq2, ALU.add))


def two_deep(eng, ahead, behind, n):
    def chunk(cc, last):
        for e in range(n):
            if not (last and e == n - 1):
                ahead(cc + (e + 1) // n, (e + 1) % n)
            behind(cc, e)
    ahead(0, 0)
    chunk(0, False)
    with eng.Fori(1, NC_ - 1) as cc:
        chunk(cc, False)
    chunk(NC_ - 1, True)


class Step:

    def __init__(self, sources, gated, biases, downs, shares):
        self.sources = sources
        self.lhsTs = sum(ap.shape[1] for ap in sources) // 128
        self.gated, self.biases = gated, biases
        self.downs = downs
        self.shares = shares


def expert_layer(nc, sems, k, tag, steps, slots, func, n_gate, gate, loaded, b2=None):
    s = Semaphores()
    (s.gate_step, s.wT, s.wT_out, s.b2, s.b2_rows, s.b2_added, s.h, s.up, s.added, s.y, s.act, s.gate_exp, s.x_hi,
     s.x_lo, s.w_hi, s.w_lo) = sems.new(tag, """
        gate_step wT wT_out b2 b2_rows b2_added h up added y act gate_exp x_hi x_lo w_hi w_lo""")
    wT, b2x = k.wT[:, :], k.b2x[:, :]
    xT = k.xT[:, :, :].rearrange("p b t -> p (b t)")
    first, rest = slice(0, CH), slice(CH, B * T)
    bank, n = k.bank, len(steps)
    blocks = steps[0].lhsTs // (2 if steps[0].gated else 1)
    per = max(1, steps[0].lhsTs * CH // 512)
    ybase = per * slots
    gs = [k.gates[:, i * blocks * CH:(i + 1) * blocks * CH] for i in range(slots)] if steps[0].gated else []
    hs = [k.hidden[:, i * blocks * CH:(i + 1) * blocks * CH] for i in range(slots)]
    starts = [sum(st.lhsTs for st in steps[:e]) for e in range(n)]
    parts = [len(st.shares) * TPC for st in steps]
    before = [sum(parts[:e]) for e in range(n)]
    hidden = lambda slot: bank[:, per * slot:per * (slot + 1), :].rearrange("p a b -> p (a b)")

    with nc.Block() as block:
        @block.sync
        def _(sp):
            sems.clear_last(sp)

        @block.tensor
        def _(pe):
            pe.wait_ge(loaded[0], loaded[1])

            def up(cc, e):
                m = cc * n + e
                wait(pe, s.h, m + 1 - slots)
                first_chunk = isinstance(cc, int) and cc == 0
                wait(pe, s.x_lo, 1 if first_chunk else 2)
                if first_chunk:
                    wait(pe, s.w_lo, e + 1)
                hi, lo = (x[:, cc * CH:cc * CH + CH] if isinstance(cc, int) else x[:, bass.ds(cc * CH, CH)]
                          for x in (k.x_hi, k.x_lo))
                out = hidden(e % slots)
                for i in range(steps[e].lhsTs):
                    at_ = (starts[e] + i) * 128
                    w_hi, w_lo = k.w_hi[:, at_:at_ + 128], k.w_lo[:, at_:at_ + 128]
                    nc.tensor.matmul(out[:, i * CH:(i + 1) * CH], w_hi, lo, start=True, stop=False)
                    nc.tensor.matmul(out[:, i * CH:(i + 1) * CH], w_lo, hi, start=False, stop=False)
                    last = nc.tensor.matmul(out[:, i * CH:(i + 1) * CH], w_hi, hi, start=False, stop=True)
                last.then_inc(s.up, 1)

            def down(cc, e):
                m = cc * n + e
                wait(pe, s.h, m + 1)
                if slots <= e:
                    wait(pe, s.added, cc * sum(parts) + before[e - slots + 1])
                elif not isinstance(cc, int) or cc > 0:
                    wait(pe, s.added, (cc - 1) * sum(parts) + (before + [sum(parts)])[e - slots + 1 + n])
                wide = len(steps[e].shares) * D
                for i in range(TPC):
                    for j, rhs in enumerate(steps[e].downs):
                        last = nc.tensor.matmul(bank[:, ybase + e % slots, i * wide:(i + 1) * wide],
                                                hs[e % slots][:, j * CH + i * T:j * CH + (i + 1) * T], rhs,
                                                start=j == 0, stop=j == len(steps[e].downs) - 1)
                last.then_inc(s.y, 1)
                if b2 is not None and e == n // 2:
                    if isinstance(cc, int) and cc == 0:
                        pe.wait_ge(s.gate_step, GATE_STEPS)
                        nc.tensor.transpose(bank[:, 7, 0:T], k.gate_t[:, 0:B * n_gate], k.c["ident"]).then_inc(s.wT, 1)
                        pe.wait_ge(s.wT_out, 1)
                        pe.wait_ge(s.b2_rows, 1)
                    wait(pe, s.b2_added, cc)
                    rows = b2x[:, cc * CH:cc * CH + CH] if isinstance(cc, int) else b2x[:, bass.ds(cc * CH, CH)]
                    nc.tensor.matmul(bank[:, 6, 0:CH], wT, rows, start=True, stop=True).then_inc(s.b2, 1)

            two_deep(pe, up, down, n)

        @block.scalar
        def _(act):
            nc.scalar.activation(k.x_hi[:, first], xT[:, first], ACT.Copy).then_inc(s.x_hi, 1)
            act.wait_ge(loaded[0], loaded[1])
            for e in range(n):
                at_ = starts[e] * 128
                for ap in steps[e].sources:
                    last = nc.scalar.activation(k.w_hi[:, at_:at_ + ap.shape[1]], ap, ACT.Copy)
                    at_ += ap.shape[1]
                last.then_inc(s.w_hi, 1)
            choose_experts(nc, s, k, n_gate, gate, None, act)
            nc.scalar.activation(k.x_hi[:, rest], xT[:, rest], ACT.Copy).then_inc(s.x_hi, 1)

            def nonlinear(cc, e):
                m = cc * n + e
                wait(act, s.up, m + 1)
                src = hidden(e % slots)
                if steps[e].gated:
                    wait(act, s.h, m + 1 - slots)
                    nc.scalar.activation(gs[e % slots], src[:, 0:blocks * CH], func).then_inc(s.act, 1)
                else:
                    wait(act, s.y, m + 1 - slots)
                    for i, bias in enumerate(steps[e].biases):
                        last = nc.scalar.activation(hs[e % slots][:, i * CH:(i + 1) * CH], src[:, i * CH:(i + 1) * CH],
                                                    func, bias=bias)
                    last.then_inc(s.h, 1)
                if b2 is not None and e == n // 2 + 1 and isinstance(cc, int) and cc == 0:
                    act.wait_ge(s.wT, 1)
                    nc.scalar.activation(wT, bank[:, 7, 0:T], ACT.Copy).then_inc(s.wT_out, 1)

            def nothing(cc, e):
                pass
            two_deep(act, nothing, nonlinear, n)

        @block.vector
        def _(dve):
            choose_experts(nc, s, k, n_gate, gate, dve, None)

            def product(cc, e):
                if not steps[e].gated:
                    return
                m = cc * n + e
                wait(dve, s.act, m + 1)
                wait(dve, s.y, m + 1 - slots)
                nc.vector.tensor_tensor(hs[e % slots], gs[e % slots], hidden(e % slots)[:, blocks * CH:2 * blocks * CH],
                                        ALU.mult).then_inc(s.h, 1)

            def add(cc, e):
                m = cc * n + e
                wait(dve, s.y, m + 1)
                q = 0
                for j, share in enumerate(steps[e].shares):
                    for i in range(TPC):
                        b = cc * TPC + i
                        wide = len(steps[e].shares) * D
                        wait(dve, s.added, cc * sum(parts) + (before[e] + q + 1 - TPC))
                        nc.vector.scalar_tensor_tensor(at(k.x, b), bank[:, ybase + e % slots, i * wide + j * D:i * wide + j * D + D],
                                                       share(b), at(k.x, b), ALU.mult, ALU.add).then_inc(s.added, 1)
                        q += 1
                if b2 is not None and e == n - 1:
                    wait(dve, s.b2, cc + 1)
                    wait(dve, s.added, cc * sum(parts) + sum(parts))
                    xs = (k.x[:, TPC * cc:TPC * cc + TPC, :] if isinstance(cc, int)
                          else k.x[:, bass.ds(cc * TPC, TPC), :]).rearrange("p b d -> p (b d)")
                    nc.vector.tensor_tensor(xs, bank[:, 6, 0:CH], xs, ALU.add).then_inc(s.b2_added, 1)

            two_deep(dve, product, add, n)

        @block.gpsimd
        def _(pool):
            def low_part(e):
                pool.wait_ge(s.w_hi, e + 1)
                at_ = starts[e] * 128
                for ap in steps[e].sources:
                    part = slice(at_, at_ + ap.shape[1])
                    last = nc.gpsimd.tensor_tensor(k.w_lo[:, part], ap, k.w_hi[:, part], ALU.subtract)
                    at_ += ap.shape[1]
                last.then_inc(s.w_lo, 1)

            pool.wait_ge(s.x_hi, 1)
            nc.gpsimd.tensor_tensor(k.x_lo[:, first], xT[:, first], k.x_hi[:, first], ALU.subtract).then_inc(s.x_lo, 1)
            for e in range(n):
                low_part(e)
            pool.wait_ge(s.x_hi, 2)
            nc.gpsimd.tensor_tensor(k.x_lo[:, rest], xT[:, rest], k.x_hi[:, rest], ALU.subtract).then_inc(s.x_lo, 1)
            if b2 is not None:
                nc.gpsimd.tensor_tensor(split(b2x, D), over(b2, B, 1), over(k.c["owner"], D, 2),
                                        ALU.mult).then_inc(s.b2_rows, 1)


def receptance_layer(nc, sems, k):
    s = Semaphores()
    (s.xh, s.xs, s.xT, s.xr, s.xk, s.kr, s.rk, s.ka, s.tt, s.kv, s.cleared, s.pk, s.sg, s.pr, s.added) = sems.new("f2", """
        xh xs xT xr xk kr rk ka tt kv cleared pk sg pr added""")
    c, cols, bank, w = k.c, k.cols, k.bank, k.work
    xh = split(w[:, 0:256], D)
    xs = w[:, 256:256 + 2 * 130].rearrange("p (s t) -> p s t", s=2)
    pr, pk, xr, xk, sg, kr, ka, tt = (split(w[:, 1024 + 256 * n:1280 + 256 * n], T) for n in range(8))
    sn = norm_names(sems, "f2_in")
    stats, dev, norm = layer_norm_steps(nc, k, sn, *norm_scratch(k.small, 0))
    tg = k.tg[:, 6:7]

    with nc.Block() as block:
        @block.sync
        def _(sp):
            sems.clear_last(sp)

        @block.tensor
        def _(pe):
            def in_T(b, sl):
                wait(pe, s.xh, b + 1)
                wait(pe, s.xs, b - 1)
                nc.tensor.transpose(bank[:, sl, 0:T], xh[:, sl, :], c["ident"]).then_inc(s.xT, 1)

            def project(b, sl):
                wait(pe, s.xr, b + 1)
                wait(pe, s.xk, b + 1)
                wait(pe, s.kr, b - 1)
                nc.tensor.matmul(bank[:, 2 + sl, 0:D], xr[:, sl, :], k.w["wr"], start=True, stop=True)
                nc.tensor.matmul(bank[:, 2 + sl, D:2 * D], k.w["wk"], xk[:, sl, :], start=True, stop=True).then_inc(s.rk, 1)

            def value(b, sl):
                wait(pe, s.ka, b + 1)
                wait(pe, s.tt, b - 1)
                nc.tensor.matmul(bank[:, 4 + sl, 0:D], ka[:, sl, :], k.w["wv"], start=True, stop=True).then_inc(s.kv, 1)

            walk(pe, [(value, 4), (in_T, 0), (project, 2)])

        @block.scalar
        def _(act):
            act.wait_ge(s.cleared, 1)

            def in_T(b, sl):
                wait(act, s.xT, b + 1)
                wait(act, s.xr, b - 1)
                wait(act, s.xk, b - 1)
                wait(act, s.pk, b - 1)
                nc.scalar.activation(xs[:, sl, 1:T + 1], bank[:, sl, 0:T], ACT.Copy).then_inc(s.xs, 1)

            def gates(b, sl):
                wait(act, s.rk, b + 1)
                wait(act, s.tt, b - 1)
                wait(act, s.ka, b - 1)
                nc.scalar.activation(sg[:, sl, :], bank[:, 2 + sl, 0:D], ACT.Sigmoid).then_inc(s.sg, 1)
                nc.scalar.activation(kr[:, sl, :], bank[:, 2 + sl, D:2 * D], ACT.Relu).then_inc(s.kr, 1)

            walk(act, [(gates, 3), (in_T, 0)])

        @block.gpsimd
        def _(pool):
            nc.gpsimd.memset(xs, 0.0).then_inc(s.cleared, 1)
            pool.wait_ge(s.cleared, 1)

            def dev_in(b, sl):
                dev(pool, sl, b + 1)

            def square(b, sl):
                wait(pool, s.kr, b + 1)
                wait(pool, s.kv, b - 1)
                nc.gpsimd.tensor_tensor(ka[:, sl, :], kr[:, sl, :], kr[:, sl, :], ALU.mult).then_inc(s.ka, 1)

            walk(pool, [(dev_in, 0), (square, 4)])

        @block.vector
        def _(dve):
            def stats_in(b, sl):
                stats(dve, at(k.x, b), sl, b + 1, s.xh)

            def norm_in(b, sl):
                wait(dve, s.xT, b - 1)
                norm(dve, xh[:, sl, :], at(k.x, b), sl, b + 1).then_inc(s.xh, 1)

            def previous(b, sl):
                wait(dve, s.xs, b + 1)
                wait(dve, s.xk, b - 1)
                nc.vector.tensor_scalar(pr[:, sl, :], xs[:, sl, 0:T], k.omu[:, 0:1], None, ALU.mult).then_inc(s.pr, 1)
                nc.vector.tensor_scalar(pk[:, sl, :], xs[:, sl, 0:T], k.omu[:, 1:2], None, ALU.mult).then_inc(s.pk, 1)

            def mix(b, sl):
                wait(dve, s.rk, b - 1)
                wait(dve, s.pr, b + 1)
                nc.vector.scalar_tensor_tensor(xr[:, sl, :], xs[:, sl, 1:T + 1], cols["mu_r"], pr[:, sl, :], ALU.mult,
                                               ALU.add).then_inc(s.xr, 1)
                wait(dve, s.pk, b + 1)
                nc.vector.scalar_tensor_tensor(xk[:, sl, :], xs[:, sl, 1:T + 1], cols["mu_k"], pk[:, sl, :], ALU.mult,
                                               ALU.add).then_inc(s.xk, 1)

            def gated(b, sl):
                wait(dve, s.kv, b + 1)
                wait(dve, s.sg, b + 1)
                wait(dve, s.added, b - 1)
                nc.vector.tensor_tensor(tt[:, sl, :], bank[:, 4 + sl, 0:D], sg[:, sl, :], ALU.mult).then_inc(s.tt, 1)

            def add(b, sl):
                wait(dve, s.tt, b + 1)
                wait(dve, s.xh, b + 1)
                nc.vector.scalar_tensor_tensor(at(k.x, b), tt[:, sl, :], tg, at(k.x, b), ALU.mult,
                                               ALU.add).then_inc(s.added, 1)

            walk(dve, [(stats_in, 0), (norm_in, 1), (mix, 3), (previous, 2), (add, 6), (gated, 5)])


def correlation_block(nc, sems, k, scratch_g, scratch_c):
    s = Semaphores()
    (s.xh, s.xhT, s.xT, s.ctxs, s.qk_out, s.v, s.qkv, s.g2, s.g, s.skew, s.mean, s.m, s.all_mean, s.eq,
     s.eqT, s.eqT_out, s.rank, s.cw, s.cwT, s.cwT_out, s.cr, s.pen, s.ex, s.biased, s.sent0, s.sent1,
     s.cr2, s.sent_c, s.circ, s.step) = sems.new("c3", """
        xh xhT xT ctxs qk_out v qkv g2 g skew mean m all_mean eq eqT eqT_out rank cw cwT cwT_out cr pen
        ex biased sent0 sent1 cr2 sent_c circ step""")
    c, cols, bank, w = k.c, k.cols, k.bank, k.work
    xh, xhT, qT, kT, ctxs = (split(w[:, 256 * n:256 * (n + 1)], 128) for n in range(5))
    g2 = w[:, 1280:1792].rearrange("p (s r t) -> p s r t", s=2, r=2)
    vtok = w[:, 2048:4096].rearrange("p (b d) -> p b d", b=B)
    skew = k.e[:, 0, :].rearrange("p (b t) -> p b t", b=B)
    circ = k.pT[:, :].rearrange("p (b t) -> p b t", b=B)
    r = w[0:B, 4096:8192]
    m, gm, gt, eq, sel, pen, ex, cw, tmp = (r[:, 128 * n:128 * (n + 1)] for n in range(9))
    cr2 = split(r[:, 1280:1536], T)
    top8, ngt, mxv, rs, ri = (r[:, 1536 + 8 * n:1544 + 8 * n] for n in range(5))
    eqT, cwT = w[:, 6144:6144 + B], w[:, 6160:6160 + B]
    sn = norm_names(sems, "c3_in")
    stats, dev, norm = layer_norm_steps(nc, k, sn, *norm_scratch(k.small, 0))

    with nc.Block() as block:
        @block.tensor
        def _(pe):
            def in_T(b, sl):
                wait(pe, s.xh, b + 1)
                wait(pe, s.xhT, b - 1)
                nc.tensor.transpose(bank[:, sl, 0:T], xh[:, sl, :], c["ident"]).then_inc(s.xT, 1)

            def project(b, sl):
                wait(pe, s.xhT, b + 1)
                wait(pe, s.ctxs, b + 1)
                wait(pe, s.qk_out, b - 1)
                wait(pe, s.v, b - 1)
                nc.tensor.matmul(bank[:, 2 + sl, 0:T], k.w["wq3"], xhT[:, sl, :], start=True, stop=True)
                nc.tensor.matmul(bank[:, 2 + sl, T:2 * T], k.w["wk3"], ctxs[:, sl, :], start=True, stop=True)
                nc.tensor.matmul(bank[:, 2 + sl, 256:384], ctxs[:, sl, :], k.w["wv3"], start=True, stop=True).then_inc(s.qkv, 1)

            def products(b, sl):
                wait(pe, s.qk_out, b + 1)
                wait(pe, s.g2, b - 1)
                nc.tensor.matmul(bank[:, 4 + sl, 0:T], kT[:, sl, :], qT[:, sl, :], start=True, stop=True).then_inc(s.g, 1)

            walk(pe, [(in_T, 0), (products, 3), (project, 1)])
            pe.wait_ge(s.skew, 16)
            for b in range(B):
                last = nc.tensor.matmul(bank[0:B, 6, 0:T], c["column"][:, B - 1 - b:2 * B - 1 - b], skew[:, b, :],
                                        start=b == 0, stop=b == B - 1)
            last.then_inc(s.mean, 1)
            pe.wait_ge(s.m, 1)
            nc.tensor.matmul(bank[0:B, 7, 0:T], c["mean"][0:B, :], m, start=True, stop=True).then_inc(s.all_mean, 1)
            pe.wait_ge(s.eq, 1)
            nc.tensor.transpose(bank[:, 7, 128:128 + B], eq, c["ident"][0:B, 0:B]).then_inc(s.eqT, 1)
            pe.wait_ge(s.eqT_out, 1)
            nc.tensor.matmul(bank[0:B, 7, 256:256 + T], eqT, c["earlier"], start=True, stop=True).then_inc(s.rank, 1)
            pe.wait_ge(s.cw, 1)
            nc.tensor.transpose(bank[:, 6, 128:128 + B], cw, c["ident"][0:B, 0:B]).then_inc(s.cwT, 1)
            pe.wait_ge(s.cwT_out, 1)
            nc.tensor.matmul(bank[0:B, 6, 256:256 + T], cwT, c["mirror"], start=True, stop=True).then_inc(s.cr, 1)

        @block.scalar
        def _(act):
            def in_T(b, sl):
                wait(act, s.xT, b + 1)
                wait(act, s.qkv, b - 1)
                nc.scalar.activation(xhT[:, sl, :], bank[:, sl, 0:T], ACT.Copy).then_inc(s.xhT, 1)

            def qk(b, sl):
                wait(act, s.qkv, b + 1)
                wait(act, s.g, b - 1)
                nc.scalar.activation(qT[:, sl, :], bank[:, 2 + sl, 0:T], ACT.Identity, bias=cols["b3q"])
                nc.scalar.activation(kT[:, sl, :], bank[:, 2 + sl, T:2 * T], ACT.Identity, bias=cols["b3k"]).then_inc(s.qk_out, 1)

            walk(act, [(qk, 2), (in_T, 0)])
            act.wait_ge(s.pen, 2)
            nc.scalar.activation(ex, tmp, ACT.Exp, accum_out=rs[:, 0:1]).then_inc(s.ex, 1)

        @block.gpsimd
        def _(pool):
            def dev_in(b, sl):
                dev(pool, sl, b + 1)

            walk(pool, [(dev_in, 0)])
            pool.wait_ge(s.xh, B)
            nc.gpsimd.tensor_tensor(k.x[:, :, :], k.x[:, :, :], over(k.tgb[:, 2, :], B, 1), ALU.add).then_inc(s.biased, 1)

        @block.sync
        def _(sp):
            sems.clear_last(sp)

            def send(b, sl):
                wait(sp, s.g2, b + 1)
                dst = scratch_g[b] if isinstance(b, int) else scratch_g[bass.ds(b, 1)].rearrange("o t n -> (o t) n")
                sp.dma_start(dst, g2[:, sl, :, :].rearrange("p r t -> p (r t)")).then_inc((s.sent0, s.sent1)[sl], 16)

            walk(sp, [(send, 0)])
            sp.wait_ge((s.sent0, s.sent1)[0], 16 * B // 2)
            sp.wait_ge((s.sent0, s.sent1)[1], 16 * B // 2)
            row = 2 * T
            sp.dma_start(skew, bass.AP(scratch_g.tensor, 0, [[row + 1, T], [T * row, B], [1, T]])).then_inc(s.skew, 16)
            sp.wait_ge(s.cr2, 1)
            sp.dma_start(scratch_c, cr2.rearrange("p r t -> p (r t)")).then_inc(s.sent_c, 16)
            sp.wait_ge(s.sent_c, 16)
            sp.dma_start(circ, bass.AP(scratch_c.tensor, 0, [[1, T], [row, B], [1, T]])).then_inc(s.circ, 16)
            sp.wait_ge(s.circ, 16)

        @block.vector
        def _(dve):
            def stats_in(b, sl):
                stats(dve, at(k.x, b), sl, b + 1, s.xh)

            def norm_in(b, sl):
                wait(dve, s.xT, b - 1)
                norm(dve, xh[:, sl, :], at(k.x, b), sl, b + 1).then_inc(s.xh, 1)

            def context(b, sl):
                wait(dve, s.qkv, b - 1)
                nc.vector.tensor_copy(ctxs[:, sl, :], at(k.ctxT, b)).then_inc(s.ctxs, 1)

            def values(b, sl):
                wait(dve, s.qkv, b + 1)
                wait(dve, s.qk_out, b + 1)
                nc.vector.tensor_tensor(at(vtok, b), bank[:, 2 + sl, 256:384], k.rows["b3v"], ALU.add).then_inc(s.v, 1)

            def twice(b, sl):
                wait(dve, s.g, b + 1)
                wait(dve, (s.sent0, s.sent1)[sl], 8 * (b - sl))
                nc.vector.tensor_copy(g2[:, sl, :, :], over(bank[:, 4 + sl, 0:T], 2, 1)).then_inc(s.g2, 1)

            walk(dve, [(stats_in, 0), (norm_in, 1), (values, 5), (twice, 6), (context, 2)])
            v = nc.vector
            done = [0]

            def step(instruction):
                done[0] += 1
                instruction.then_inc(s.step, 1)
                dve.wait_ge(s.step, done[0])

            dve.wait_ge(s.mean, 1)
            v.tensor_copy(m, bank[0:B, 6, 0:T]).then_inc(s.m, 1)
            dve.wait_ge(s.all_mean, 1)
            step(v.tensor_copy(gm, bank[0:B, 7, 0:T]))
            step(v.max(top8, gm))
            fifth = top8[:, TOP_SHIFTS - 1:TOP_SHIFTS]
            v.tensor_scalar(eq, gm, fifth, None, ALU.is_equal).then_inc(s.eq, 1)
            step(v.tensor_scalar(gt, gm, fifth, None, ALU.is_gt))
            step(v.tensor_reduce(ngt[:, 0:1], gt, AX.X, ALU.add))
            dve.wait_ge(s.eqT, 1)
            v.tensor_copy(eqT, bank[:, 7, 128:128 + B]).then_inc(s.eqT_out, 1)
            dve.wait_ge(s.rank, 1)
            step(v.tensor_scalar(sel, bank[0:B, 7, 256:256 + T], ngt[:, 0:1], float(TOP_SHIFTS), ALU.add, ALU.is_lt))
            step(v.tensor_tensor(sel, sel, eq, ALU.mult))
            step(v.tensor_tensor(sel, sel, gt, ALU.add))
            step(v.tensor_scalar(pen, sel, -MASKED, MASKED, ALU.mult, ALU.add))
            dve.wait_ge(s.m, 1)
            step(v.tensor_tensor(tmp, m, pen, ALU.add))
            v.tensor_reduce(mxv[:, 0:1], tmp, AX.X, ALU.max).then_inc(s.pen, 1)
            dve.wait_ge(s.pen, 1)
            v.tensor_scalar(tmp, tmp, mxv[:, 0:1], None, ALU.subtract).then_inc(s.pen, 1)
            dve.wait_ge(s.ex, 1)
            step(v.reciprocal(ri[:, 0:1], rs[:, 0:1]))
            v.tensor_scalar(cw, ex, ri[:, 0:1], None, ALU.mult).then_inc(s.cw, 1)
            dve.wait_ge(s.cwT, 1)
            v.tensor_copy(cwT, bank[:, 6, 128:128 + B]).then_inc(s.cwT_out, 1)
            dve.wait_ge(s.cr, 1)
            v.tensor_copy(cr2, over(bank[0:B, 6, 256:256 + T], 2, 1)).then_inc(s.cr2, 1)


def roll_block(nc, sems, k):
    s = Semaphores()
    (s.xs2, s.vs, s.vm, s.agg_out, s.agg, s.added, s.out, s.xh2, s.xT2, s.logits_out, s.logits) = sems.new("r3", """
        xs2 vs vm agg_out agg added out xh2 xT2 logits_out logits""")
    c, bank, w = k.c, k.bank, k.work
    vtok = w[:, 2048:4096].rearrange("p (b d) -> p b d", b=B)
    circ = k.pT[:, :].rearrange("p (b t) -> p b t", b=B)
    vs, agg, xh2, xs2 = (split(w[:, 256 * n:256 * (n + 1)], 128) for n in range(4))
    so = norm_names(sems, "r3_out")
    stats, dev, norm = layer_norm_steps(nc, k, so, *norm_scratch(k.small, 0))
    tg = k.tg[:, 3:4]

    with nc.Block() as block:
        @block.sync
        def _(sp):
            sems.clear_last(sp)

        @block.gpsimd
        def _(pool):
            def dev_out(b, sl):
                dev(pool, sl, b + 1)

            walk(pool, [(dev_out, 0)])

        @block.tensor
        def _(pe):
            def mirror(b, sl):
                wait(pe, s.vs, b)
                nc.tensor.matmul(bank[:, 7, 0:D], c["mirror"], at(vtok, b), start=True, stop=True).then_inc(s.vm, 1)

            def aggregate(b, sl):
                wait(pe, s.vs, b + 1)
                wait(pe, s.agg_out, b - 1)
                nc.tensor.matmul(bank[:, sl, 0:T], vs[:, sl, :], at(circ, b), start=True, stop=True).then_inc(s.agg, 1)

            def out(b, sl):
                wait(pe, s.agg_out, b + 1)
                wait(pe, s.added, b - 1)
                nc.tensor.matmul(bank[:, 2 + sl, 0:D], agg[:, sl, :], k.w["wo3"], start=True, stop=True).then_inc(s.out, 1)

            def next_T(b, sl):
                wait(pe, s.xh2, b + 1)
                wait(pe, s.xs2, b - 1)
                nc.tensor.transpose(bank[:, 4 + sl, 0:T], xh2[:, sl, :], c["ident"]).then_inc(s.xT2, 1)

            def logits(b, sl):
                wait(pe, s.xs2, b + 1)
                wait(pe, s.logits_out, b)
                nc.tensor.matmul(bank[:, 6, 0:E3], xs2[:, sl, :], k.w["wg3"], start=True, stop=True).then_inc(s.logits, 1)

            walk(pe, [(mirror, 0), (next_T, 5), (logits, 6), (out, 1), (aggregate, 0)])

        @block.scalar
        def _(act):
            def mirrored(b, sl):
                wait(act, s.vm, b + 1)
                wait(act, s.agg, b - 1)
                nc.scalar.activation(vs[:, sl, :], bank[:, 7, 0:D], ACT.Copy).then_inc(s.vs, 1)

            def aggregated(b, sl):
                wait(act, s.agg, b + 1)
                wait(act, s.out, b - 1)
                nc.scalar.activation(agg[:, sl, :], bank[:, sl, 0:T], ACT.Copy).then_inc(s.agg_out, 1)

            def next_T(b, sl):
                wait(act, s.xT2, b + 1)
                wait(act, s.logits, b - 1)
                nc.scalar.activation(xs2[:, sl, :], bank[:, 4 + sl, 0:T], ACT.Copy)
                nc.scalar.activation(at(k.xT, b), bank[:, 4 + sl, 0:T], ACT.Copy).then_inc(s.xs2, 1)

            def logits(b, sl):
                wait_apart(act, k, s.logits, b + 1)
                nc.scalar.activation(at(k.logits, b)[:, 0:E3], bank[:, 6, 0:E3], ACT.Copy).then_inc(s.logits_out, 1)

            walk(act, [(mirrored, 0), (next_T, 5), (logits, 6), (aggregated, 0)])

        @block.vector
        def _(dve):
            def add(b, sl):
                wait(dve, s.out, b + 1)
                nc.vector.scalar_tensor_tensor(at(k.x, b), bank[:, 2 + sl, 0:D], tg, at(k.x, b), ALU.mult,
                                               ALU.add).then_inc(s.added, 1)

            def stats_out(b, sl):
                wait(dve, s.added, b + 1)
                stats(dve, at(k.x, b), sl, b + 1, s.xh2)

            def norm_out(b, sl):
                wait(dve, s.xT2, b - 1)
                norm(dve, xh2[:, sl, :], at(k.x, b), sl, b + 1).then_inc(s.xh2, 1)

            walk(dve, [(norm_out, 3), (add, 0), (stats_out, 1)])


def flamingo_layers(nc, a, out, until=8):
    ctx = ExitStack()
    with ctx:
        k = Core()
        k.used = []
        set_up(nc, ctx, k, a)
        scratch_g = nc.dram_tensor("shifted_rows", [B, T, 2 * T], FP32, kind="Internal").ap()
        scratch_c = nc.dram_tensor("circulant_rows", [B, 2 * T], FP32, kind="Internal").ap()
        ld = Semaphores()
        ld.consts, ld.ctx, ld.x, ld.rows, ld.out = (ctx.enter_context(nc.semaphore(f"dma_{name}"))
                                                    for name in ("consts", "ctx", "x", "rows", "out"))
        k.passed = ctx.enter_context(nc.semaphore("passed"))
        ld.weights = [ctx.enter_context(nc.semaphore(f"dma_{name}")) for name, _ in a.weight_parts]
        weight = lambda e, n: lambda b: k.gate_w(n)[:, b, e:e + 1] if isinstance(b, int) else \
            k.gate_w(n)[:, bass.ds(b, 1), e:e + 1].rearrange("p o n -> p (o n)")
        w = k.w
        col = lambda name, n, m=128: w[name][:, n * m:(n + 1) * m]
        with attention_scratch(nc, k, "a0"):
            with Sublayer(nc, k) as sems:
                load_block(nc, sems, k, a, ld)
            with Sublayer(nc, k) as sems:
                small_head_attention(nc, sems, k, "a0", None, True, False, w["w_proj"], k.tg[:, 0:1], k.tgb[:, 0, :],
                                     w["wg0"], E0, ld)
        if until >= 2:
            steps = [Step([col("w1", e, H0), col("w2", e, H0)], True, None, [col("w3", 2 * e), col("w3", 2 * e + 1)],
                          [weight(e, E0)]) for e in range(E0)]
            with expert_scratch(nc, k, "f0", 2 * CH * H0 // 128, 2 * CH * H0 // 128, 2 * E0 * H0, False), Sublayer(nc, k) as sems:
                expert_layer(nc, sems, k, "f0", steps, 2, ACT.Silu, E0, k.tg[:, 4:5], (ld.weights[1], 16))
        if until >= 3:
            with attention_scratch(nc, k, "a1"), Sublayer(nc, k) as sems:
                latent_attention(nc, sems, k, ld)
        if until >= 4:
            steps = [Step([col("gate1", p), col("up1", p)], True, None, [k.down1[:, p, :]],
                          [weight(2 * p, E1), weight(2 * p + 1, E1)]) for p in range(E1 // 2)]
            steps.append(Step([w["sh_gate"], w["sh_up"]], True, None, [w["sh_down"]], [lambda b: k.tg[:, 5:6]]))
            with expert_scratch(nc, k, "f1", 3 * CH, 3 * CH, 2 * (E1 * H1 + D), False), Sublayer(nc, k) as sems:
                expert_layer(nc, sems, k, "f1", steps, 3, ACT.Silu, E1, k.tg[:, 5:6], (ld.weights[3], 48))
        if until >= 5:
            with attention_scratch(nc, k, "a2"):
                with Sublayer(nc, k) as sems:
                    small_head_attention(nc, sems, k, "a2", None, False, True, w["wo2"], k.tg[:, 2:3], k.tgb[:, 1, :],
                                         None, 0, ld)
                if until >= 6:
                    with Sublayer(nc, k) as sems:
                        receptance_layer(nc, sems, k)
                if until >= 7:
                    with Sublayer(nc, k) as sems:
                        correlation_block(nc, sems, k, scratch_g, scratch_c)
                    with Sublayer(nc, k) as sems:
                        roll_block(nc, sems, k)
        if until >= 8:
            steps = [Step([col("w1_3", e, M3)], False, [k.cols["b1"][:, 4 * e + i:4 * e + i + 1] for i in range(M3 // 128)],
                          [col("w2_3", 4 * e + i) for i in range(4)], [weight(e, E3)]) for e in range(E3)]
            with expert_scratch(nc, k, "f3", 1, 2 * CH * M3 // 128, E3 * M3, True), Sublayer(nc, k) as sems:
                expert_layer(nc, sems, k, "f3", steps, 2, ACT.Gelu, E3, k.tg[:, 7:8], (ld.weights[5], 32), k.b2_3[:, :])
        with nc.Block() as block:
            @block.sync
            def _(sp):
                sp.dma_start(out.rearrange("b t d -> t b d"), k.x[:, :, :]).then_inc(ld.out, 16)
                for sem in k.used:
                    sp.sem_clear(sem)
                sp.wait_ge(ld.out, 16)
                for n, count in ((0, 16), (1, 16), (2, 16), (3, 48), (4, 16), (5, 32)):
                    sp.wait_ge(ld.weights[n], count)


WEIGHT_PARTS = [("weights_a0", WEIGHTS0), ("weights_f0", WEIGHTS_F0), ("weights_a1", WEIGHTS_A1), ("weights_f1", WEIGHTS_F1),
                ("weights_2", WEIGHTS_2), ("weights_f3", WEIGHTS_F3)]


def cat(parts, arrays):
    assert [a.shape[1] for a in arrays] == [n for _, n in parts], ([a.shape for a in arrays], parts)
    return np.ascontiguousarray(np.concatenate(arrays, axis=1))


def shape_constants():
    d = np.arange(L1D)
    theta = np.arange(T, dtype=np.float32)[:, None] * (
        1.0 / np.float32(10000.0) ** (np.arange(0, L1D, 2, dtype=np.float32) / L1D))[None, :]
    angles = np.concatenate([theta, theta], axis=1).astype(np.float32).T
    cos = np.tile(np.cos(angles), (2, 1))
    sin = np.tile(np.sin(angles) * np.where(d < L1D // 2, -1.0, 1.0)[:, None], (2, 1))
    p, t = np.arange(128)[:, None], np.arange(128)[None, :]
    column = np.zeros((128, 2 * B - 1))
    column[:, B - 1] = 1.0 / 128
    consts = [np.eye(128), cos, sin, (p % 32) // DH == np.arange(HG)[None, :], p < t, (p + t) % 128 == 0, column,
              np.full((128, B), 1.0 / B), np.where(np.abs(p - t) > WINDOW, MASKED, 0.0), np.tile(np.arange(E0, 0, -1.0), (128, 1)), np.tile(np.arange(E1, 0, -1.0), (128, 1)),
              p // E3 == np.arange(B)[None, :]]
    consts = cat(CONSTS, [np.asarray(x, np.float32) for x in consts])
    return consts


def kernel(**inputs):
    import concourse.bacc as _bacc
    from concourse.bass_utils import run_bass_kernel_spmd as _run

    i = {name: np.asarray(v) for name, v in inputs.items()}
    stack = lambda m: m.transpose(1, 0, 2).reshape(m.shape[1], -1)
    tall = lambda m: stack(m.reshape(-1, 128, m.shape[-1]))
    wkv = i["L1_xattn_Wkv"]
    wk, wv = wkv[:, :INNER], wkv[:, INNER:]
    rotated = (np.arange(INNER) // L1D) * L1D + (np.arange(INNER) + L1D // 2) % L1D
    w2_3 = i["L3_ffn_W2"].transpose(2, 0, 1).reshape(4, 128, E3, D).transpose(1, 2, 0, 3).reshape(128, -1)
    w3 = i["L0_ffn_W3"].reshape(E0, 2, 128, D).transpose(2, 0, 1, 3).reshape(128, -1)
    weights = [
        [i["L0_xattn_W_proj"].T, i["L0_ffn_Wg"]],
        [stack(i["L0_ffn_W1"]), stack(i["L0_ffn_W2"]), w3],
        [i["L1_xattn_Wq"], wk, wk[:, rotated], wv, tall(i["L1_xattn_Wo"]), i["L1_ffn_router_w"].T],
        [stack(i["L1_ffn_up_proj"]), stack(i["L1_ffn_gate_proj"]), i["L1_ffn_sh_gate"].T, i["L1_ffn_sh_up"].T,
         i["L1_ffn_sh_down"].T],
        [i["L2_xattn_W_q"].T, i["L2_xattn_W_k"].T, i["L2_xattn_W_v"].T, i["L2_xattn_W_out"].T, i["L2_ffn_W_r"].T,
         i["L2_ffn_W_k"].T, i["L2_ffn_W_v"].T, i["L3_xattn_Wq"], i["L3_xattn_Wk"], i["L3_xattn_Wv"], i["L3_xattn_Wo"],
         i["L3_ffn_Wr"].T],
        [i["L3_ffn_W1"].transpose(2, 0, 1).reshape(128, -1), w2_3],
    ]
    cols = [i[n].reshape(128, 1) for n in ("L1_xattn_gamma_x", "L1_xattn_beta_x", "L1_xattn_gamma_l", "L1_xattn_beta_l",
                                           "L2_xattn_b_q", "L2_xattn_b_k", "L2_ffn_mu_r", "L2_ffn_mu_k", "L3_xattn_bq",
                                           "L3_xattn_bk")]
    cols.append(i["L3_ffn_b1"].reshape(E3 * M3 // 128, 128).T)
    rows = [i["g_xattn"], i["g_ffn"], i["L1_ffn_router_bias"], i["L0_xattn_b_proj"], i["L2_xattn_b_v"], i["L2_xattn_b_out"],
            i["L3_xattn_bv"], i["L3_xattn_bo"]]
    consts = shape_constants()
    arrays = {"x": i["x"], "ctx": i["ctx_1024"], "rows": np.concatenate(rows), "cols": cat(COLS, cols), "consts": consts,
              "down": i["L1_ffn_down_proj"].reshape(E1 // 2, 2, H1, D).transpose(1, 0, 2, 3),
              "b2_3": np.tile(i["L3_ffn_b2"], (B, 1))}
    for (name, parts), ws in zip(WEIGHT_PARTS, weights):
        arrays[name] = cat(parts, ws)
    arrays = {f"in_{n}": np.ascontiguousarray(v) for n, v in arrays.items()}

    nc = _bacc.Bacc("TRN2", target_bir_lowering=False, num_devices=1)
    dram = {name[3:]: nc.dram_tensor(name, v.shape, mybir.dt.from_np(v.dtype), kind="ExternalInput").ap()
            for name, v in arrays.items()}
    a = Core()
    a.x, a.ctx, a.rows, a.cols, a.consts, a.down, a.b2_3 = (
        dram[name] for name in ("x", "ctx", "rows", "cols", "consts", "down", "b2_3"))
    a.weight_parts, a.weight_tiles, a.weights = WEIGHT_PARTS, [], [dram[name] for name, _ in WEIGHT_PARTS]
    out = nc.dram_tensor("out_0", (B, T, D), FP32, kind="ExternalOutput").ap()
    flamingo_layers(nc, a, out)
    r = _run(nc, [arrays], core_ids=[0])
    return r.results[0]["out_0"]
```
